# Optimizing a Trainium2 kernel written in Bass

```python
import numpy as np
import jax
import jax.numpy as jnp

def _softmax(x, axis=-1):
    return jax.nn.softmax(x, axis=axis)

def _gelu(x):
    return jax.nn.gelu(x, approximate=True)

def _silu(x):
    return jax.nn.silu(x)

def _sigmoid(x):
    return jax.nn.sigmoid(x)

def _layernorm(x, axis=-1, eps=1e-05):
    m = jnp.mean(x, axis=axis, keepdims=True)
    v = jnp.var(x, axis=axis, keepdims=True)
    return (x - m) / jnp.sqrt(v + eps)

def _scatter_add(tgt, idx, src, axis=0):
    return tgt.at[idx].add(src)

def _segment_sum(src, seg, n):
    return jax.ops.segment_sum(src, seg, n)
kernel_name = 'mk_gnn_preln_d4_gnn_r8_0c0bc3'

def setup_inputs(seed: int=0):
    np.random.seed(seed)
    _w = jnp.asarray

    def _rec_inputs():
        import jax
        import jax.numpy as jnp
        _gk = jax.random.key(seed)
        x = -0.0005121 + 1.001 * jax.random.normal(jax.random.fold_in(_gk, 1), (6250, 64), jnp.float32)
        src = jax.random.randint(jax.random.fold_in(_gk, 2), (200000,), 0, 6250, jnp.int32)
        dst = jax.random.randint(jax.random.fold_in(_gk, 3), (200000,), 0, 6250, jnp.int32)
        _o = jnp.argsort(dst, stable=True)
        src = src[_o]
        dst = dst[_o]
        edge_attr_32 = 0.000196303 + 1.00016 * jax.random.normal(jax.random.fold_in(_gk, 13), (200000, 32), jnp.float32)
        edge_weight = jax.random.uniform(jax.random.fold_in(_gk, 15), (200000,), jnp.float32, 0.0, 4)
        edge_weight1 = jax.random.uniform(jax.random.fold_in(_gk, 16), (200000, 1), jnp.float32, 0.0, 0.999999)
        return (x, src, dst, edge_attr_32, edge_weight, edge_weight1)
    x, src, dst, edge_attr_32, edge_weight, edge_weight1 = _rec_inputs()

    def _L0_gnn_setup():
        import jax, jax.numpy as jnp
        import numpy as np
        N = 6250
        E = 100000
        F = 64
        D = 64
        ALPHA = 0.5
        LCS_THR = 0.5
        key = jax.random.key(seed)
        ks = jax.random.split(key, 16)
        x = jax.random.normal(ks[0], (N, F), jnp.float32)
        src = jax.random.randint(ks[1], (E,), 0, N, jnp.int32)
        dst = jax.random.randint(ks[2], (E,), 0, N, jnp.int32)
        counts = jnp.floor(jax.random.uniform(ks[3], (E,), jnp.float32) * 4.0) + 1.0

        def lin(k, fan_in, shape):
            return jax.random.normal(k, shape, jnp.float32) / np.float32(np.sqrt(fan_in))
        return dict(x=x, counts=counts, W_s2d=lin(ks[4], F, (F, D)), b_s2d=jnp.zeros((D,), jnp.float32), W_d2s=lin(ks[5], F, (F, D)), b_d2s=jnp.zeros((D,), jnp.float32), W_l1=lin(ks[6], 2 * F, (2 * F, F)), b_l1=jnp.zeros((F,), jnp.float32), W_l2=lin(ks[7], F, (F, 1)), b_l2=jnp.zeros((1,), jnp.float32), W_g1=lin(ks[8], 2 * D, (2 * D, D)), b_g1=jnp.zeros((D,), jnp.float32), W_g2=lin(ks[9], D, (D, 1)), b_g2=jnp.zeros((1,), jnp.float32), src=src, dst=dst)
    _L0_gnn_all = _L0_gnn_setup()
    _L0_gnn_in = {k: v for k, v in _L0_gnn_all.items() if k in ('W_s2d', 'b_s2d', 'W_d2s', 'b_d2s', 'W_l1', 'b_l1', 'W_l2', 'b_l2', 'W_g1', 'b_g1', 'W_g2', 'b_g2')}
    del _L0_gnn_all

    def _L1_gnn_setup():
        import jax, jax.numpy as jnp
        import numpy as np
        N, E, G = (6250, 100000, 16)
        F_X, F_E, F_U = (64, 32, 64)
        H1, H2, H3 = (128, 64, 64)

        def _lin_init(key, fan_in, fan_out):
            kw, kb = jax.random.split(key)
            bound = 1.0 / np.sqrt(fan_in)
            W = jax.random.uniform(kw, (fan_in, fan_out), jnp.float32, -bound, bound)
            b = jax.random.uniform(kb, (fan_out,), jnp.float32, -bound, bound)
            return (W, b)
        key = jax.random.key(seed)
        ks = jax.random.split(key, 9)
        x = jax.random.normal(ks[0], (N, F_X), jnp.float32)
        edge_index = jax.random.randint(ks[1], (2, E), 0, N, jnp.int32)
        edge_attr = jax.random.normal(ks[2], (E, F_E), jnp.float32)
        u = jax.random.normal(ks[3], (G, F_U), jnp.float32)
        batch = jnp.sort(jax.random.randint(ks[4], (N,), 0, G, jnp.int32))
        W1, b1 = _lin_init(ks[5], F_X + F_E, H1)
        W2, b2 = _lin_init(ks[6], H1, H2)
        W3, b3 = _lin_init(ks[7], H2 + F_X + F_U, H2)
        W4, b4 = _lin_init(ks[8], H2, H3)
        return {'x': x, 'edge_index': edge_index, 'edge_attr': edge_attr, 'u': u, 'batch': batch, 'W1': W1, 'b1': b1, 'W2': W2, 'b2': b2, 'W3': W3, 'b3': b3, 'W4': W4, 'b4': b4}
    _L1_gnn_all = _L1_gnn_setup()
    _L1_gnn_in = {k: v for k, v in _L1_gnn_all.items() if k in ('u', 'W1', 'b1', 'W2', 'b2', 'W3', 'b3', 'W4', 'b4')}
    del _L1_gnn_all

    def _L2_gnn_setup():
        import jax, jax.numpy as jnp
        import numpy as np
        N_NODES = 6250
        N_EDGES = 100000
        IN_CH = 64
        HID = 128
        OUT_CH = 64
        BN_EPS = 1e-05
        key = jax.random.key(seed)
        k = jax.random.split(key, 6)
        x = jax.random.normal(k[0], (N_NODES, IN_CH), dtype=jnp.float32)
        edge_index = jax.random.randint(k[1], (2, N_EDGES), 0, N_NODES, dtype=jnp.int64)
        gamma = jnp.ones((IN_CH,), dtype=jnp.float32)
        beta = jnp.zeros((IN_CH,), dtype=jnp.float32)
        W1 = jax.random.normal(k[2], (2 * IN_CH, HID), dtype=jnp.float32) * 0.05
        b1 = jnp.zeros((HID,), dtype=jnp.float32)
        W2 = jax.random.normal(k[3], (HID, OUT_CH), dtype=jnp.float32) * 0.05
        b2 = jnp.zeros((OUT_CH,), dtype=jnp.float32)
        return {'x': x, 'edge_index': edge_index, 'gamma': gamma, 'beta': beta, 'W1': W1, 'b1': b1, 'W2': W2, 'b2': b2}
    _L2_gnn_all = _L2_gnn_setup()
    _L2_gnn_in = {k: v for k, v in _L2_gnn_all.items() if k in ('gamma', 'beta', 'W1', 'b1', 'W2', 'b2')}
    del _L2_gnn_all

    def _L3_gnn_setup():
        import jax, jax.numpy as jnp
        import numpy as np
        N_NODES = 12500
        N_EDGES = 200000
        HID = 64
        N_LAYERS = 3
        BN_EPS = 1e-05
        key = jax.random.key(seed)
        ks = jax.random.split(key, 10)
        x = jax.random.normal(ks[0], (N_NODES, HID), dtype=jnp.float32)
        edge_index = jax.random.randint(ks[1], (2, N_EDGES), 0, N_NODES, dtype=jnp.int64)
        edge_atten = jax.random.uniform(ks[2], (N_EDGES, 1), dtype=jnp.float32)
        s = 1.0 / np.sqrt(HID)
        W1 = jax.random.normal(ks[3], (N_LAYERS, HID, HID), dtype=jnp.float32) * s
        b1 = jax.random.normal(ks[4], (N_LAYERS, HID), dtype=jnp.float32) * s
        gamma = jnp.ones((N_LAYERS, HID), dtype=jnp.float32)
        beta = jnp.zeros((N_LAYERS, HID), dtype=jnp.float32)
        W2 = jax.random.normal(ks[5], (N_LAYERS, HID, HID), dtype=jnp.float32) * s
        b2 = jax.random.normal(ks[6], (N_LAYERS, HID), dtype=jnp.float32) * s
        return {'x': x, 'edge_index': edge_index, 'edge_atten': edge_atten, 'W1': W1, 'b1': b1, 'gamma': gamma, 'beta': beta, 'W2': W2, 'b2': b2}
    _L3_gnn_all = _L3_gnn_setup()
    _L3_gnn_in = {k: v for k, v in _L3_gnn_all.items() if k in ('W1', 'b1', 'gamma', 'beta', 'W2', 'b2')}
    del _L3_gnn_all
    return {'x': x, 'src': src, 'dst': dst, 'edge_attr_32': edge_attr_32, 'edge_weight': edge_weight, 'edge_weight1': edge_weight1, 'L0_gnn_W_s2d': _L0_gnn_in['W_s2d'], 'L0_gnn_b_s2d': _L0_gnn_in['b_s2d'], 'L0_gnn_W_d2s': _L0_gnn_in['W_d2s'], 'L0_gnn_b_d2s': _L0_gnn_in['b_d2s'], 'L0_gnn_W_l1': _L0_gnn_in['W_l1'], 'L0_gnn_b_l1': _L0_gnn_in['b_l1'], 'L0_gnn_W_l2': _L0_gnn_in['W_l2'], 'L0_gnn_b_l2': _L0_gnn_in['b_l2'], 'L0_gnn_W_g1': _L0_gnn_in['W_g1'], 'L0_gnn_b_g1': _L0_gnn_in['b_g1'], 'L0_gnn_W_g2': _L0_gnn_in['W_g2'], 'L0_gnn_b_g2': _L0_gnn_in['b_g2'], 'L1_gnn_u': _L1_gnn_in['u'], 'L1_gnn_W1': _L1_gnn_in['W1'], 'L1_gnn_b1': _L1_gnn_in['b1'], 'L1_gnn_W2': _L1_gnn_in['W2'], 'L1_gnn_b2': _L1_gnn_in['b2'], 'L1_gnn_W3': _L1_gnn_in['W3'], 'L1_gnn_b3': _L1_gnn_in['b3'], 'L1_gnn_W4': _L1_gnn_in['W4'], 'L1_gnn_b4': _L1_gnn_in['b4'], 'L2_gnn_gamma': _L2_gnn_in['gamma'], 'L2_gnn_beta': _L2_gnn_in['beta'], 'L2_gnn_W1': _L2_gnn_in['W1'], 'L2_gnn_b1': _L2_gnn_in['b1'], 'L2_gnn_W2': _L2_gnn_in['W2'], 'L2_gnn_b2': _L2_gnn_in['b2'], 'L3_gnn_W1': _L3_gnn_in['W1'], 'L3_gnn_b1': _L3_gnn_in['b1'], 'L3_gnn_gamma': _L3_gnn_in['gamma'], 'L3_gnn_beta': _L3_gnn_in['beta'], 'L3_gnn_W2': _L3_gnn_in['W2'], 'L3_gnn_b2': _L3_gnn_in['b2']}

def reference(x, src, dst, edge_attr_32, edge_weight, edge_weight1, L0_gnn_W_s2d, L0_gnn_b_s2d, L0_gnn_W_d2s, L0_gnn_b_d2s, L0_gnn_W_l1, L0_gnn_b_l1, L0_gnn_W_l2, L0_gnn_b_l2, L0_gnn_W_g1, L0_gnn_b_g1, L0_gnn_W_g2, L0_gnn_b_g2, L1_gnn_u, L1_gnn_W1, L1_gnn_b1, L1_gnn_W2, L1_gnn_b2, L1_gnn_W3, L1_gnn_b3, L1_gnn_W4, L1_gnn_b4, L2_gnn_gamma, L2_gnn_beta, L2_gnn_W1, L2_gnn_b1, L2_gnn_W2, L2_gnn_b2, L3_gnn_W1, L3_gnn_b1, L3_gnn_gamma, L3_gnn_beta, L3_gnn_W2, L3_gnn_b2):
    import jax
    import jax.numpy as jnp

    def _L0_gnn_ref(x, counts, W_s2d, b_s2d, W_d2s, b_d2s, W_l1, b_l1, W_l2, b_l2, W_g1, b_g1, W_g2, b_g2, src, dst):
        import jax, jax.numpy as jnp
        import numpy as np
        N = 6250
        E = 100000
        F = 64
        D = 64
        ALPHA = 0.5
        LCS_THR = 0.5
        in_deg = jnp.maximum(jax.ops.segment_sum(counts, dst, num_segments=N), 1.0)
        out_deg = jnp.maximum(jax.ops.segment_sum(counts, src, num_segments=N), 1.0)
        lcs_in = jnp.concatenate([x[src], x[dst]], axis=-1)
        lcs = jax.nn.sigmoid(jax.nn.relu(lcs_in @ W_l1 + b_l1) @ W_l2 + b_l2)[:, 0]
        lcs = jax.lax.stop_gradient(lcs)
        keep = (lcs >= LCS_THR).astype(x.dtype)
        w = counts * keep * jax.lax.rsqrt(out_deg[src] * in_deg[dst])
        h_s2d = x @ W_s2d + b_s2d
        h_d2s = x @ W_d2s + b_d2s
        m_in = jax.ops.segment_sum(w[:, None] * h_s2d[src], dst, num_segments=N)
        m_out = jax.ops.segment_sum(w[:, None] * h_d2s[dst], src, num_segments=N)
        gate = jax.nn.sigmoid(jax.nn.relu(jnp.concatenate([m_in, m_out], axis=-1) @ W_g1 + b_g1) @ W_g2 + b_g2)
        out = ALPHA * gate * m_in + (1.0 - ALPHA) * (1.0 - gate) * m_out + x
        return out

    def _L1_gnn_ref(x, edge_index, edge_attr, u, batch, W1, b1, W2, b2, W3, b3, W4, b4):
        import jax, jax.numpy as jnp
        import numpy as np
        N, E, G = (6250, 100000, 16)
        F_X, F_E, F_U = (64, 32, 64)
        H1, H2, H3 = (128, 64, 64)

        def _lin_init(key, fan_in, fan_out):
            kw, kb = jax.random.split(key)
            bound = 1.0 / np.sqrt(fan_in)
            W = jax.random.uniform(kw, (fan_in, fan_out), jnp.float32, -bound, bound)
            b = jax.random.uniform(kb, (fan_out,), jnp.float32, -bound, bound)
            return (W, b)
        row, col = (edge_index[0], edge_index[1])
        e = jnp.concatenate([x[row], edge_attr], axis=1)
        e = jax.nn.relu(e @ W1 + b1) @ W2 + b2
        s = jax.ops.segment_sum(e, col, num_segments=x.shape[0])
        cnt = jax.ops.segment_sum(jnp.ones((e.shape[0],), e.dtype), col, num_segments=x.shape[0])
        agg = s / jnp.maximum(cnt, 1.0)[:, None]
        h = jnp.concatenate([x, agg, u[batch]], axis=1)
        return jax.nn.relu(h @ W3 + b3) @ W4 + b4

    def _L2_gnn_ref(x, edge_index, gamma, beta, W1, b1, W2, b2):
        import jax, jax.numpy as jnp
        import numpy as np
        N_NODES = 6250
        N_EDGES = 100000
        IN_CH = 64
        HID = 128
        OUT_CH = 64
        BN_EPS = 1e-05
        mean = jnp.mean(x, axis=0)
        var = jnp.mean(jnp.square(x - mean), axis=0)
        xn = (x - mean) * jax.lax.rsqrt(var + BN_EPS) * gamma + beta
        src = edge_index[0]
        dst = edge_index[1]
        xi = xn[dst]
        xj = xn[src]
        feat = jnp.concatenate([xi, xj - xi], axis=-1)
        h = jax.nn.relu(feat @ W1 + b1)
        msg = h @ W2 + b2
        agg = jax.ops.segment_max(msg, dst, num_segments=N_NODES)
        agg = jnp.where(jnp.isfinite(agg), agg, 0.0)
        return jax.nn.relu(agg)

    def _L3_gnn_ref(x, edge_index, edge_atten, W1, b1, gamma, beta, W2, b2):
        import jax, jax.numpy as jnp
        import numpy as np
        N_NODES = 12500
        N_EDGES = 200000
        HID = 64
        N_LAYERS = 3
        BN_EPS = 1e-05
        src = edge_index[0]
        dst = edge_index[1]
        n = x.shape[0]
        for i in range(N_LAYERS):
            msg = x[src] * edge_atten
            agg = jax.ops.segment_sum(msg, dst, num_segments=n)
            h = agg + x
            h = h @ W1[i] + b1[i]
            mu = jnp.mean(h, axis=0)
            var = jnp.var(h, axis=0)
            h = (h - mu) * jax.lax.rsqrt(var + BN_EPS) * gamma[i] + beta[i]
            h = jax.nn.relu(h)
            h = h @ W2[i] + b2[i]
            x = jax.nn.relu(h)
        return x
    edge_index = jnp.stack([src, dst])
    batch0 = jnp.zeros((6250,), jnp.int32)
    h = jnp.maximum(_layernorm(x, axis=-1), 0.0)
    x = x + _L0_gnn_ref(h, edge_weight, L0_gnn_W_s2d, L0_gnn_b_s2d, L0_gnn_W_d2s, L0_gnn_b_d2s, L0_gnn_W_l1, L0_gnn_b_l1, L0_gnn_W_l2, L0_gnn_b_l2, L0_gnn_W_g1, L0_gnn_b_g1, L0_gnn_W_g2, L0_gnn_b_g2, src, dst)
    h = jnp.maximum(_layernorm(x, axis=-1), 0.0)
    x = x + _L1_gnn_ref(h, edge_index, edge_attr_32, L1_gnn_u, batch0, L1_gnn_W1, L1_gnn_b1, L1_gnn_W2, L1_gnn_b2, L1_gnn_W3, L1_gnn_b3, L1_gnn_W4, L1_gnn_b4)
    h = jnp.maximum(_layernorm(x, axis=-1), 0.0)
    x = x + _L2_gnn_ref(h, edge_index, L2_gnn_gamma, L2_gnn_beta, L2_gnn_W1, L2_gnn_b1, L2_gnn_W2, L2_gnn_b2)
    h = jnp.maximum(_layernorm(x, axis=-1), 0.0)
    x = x + _L3_gnn_ref(h, edge_index, edge_weight1, L3_gnn_W1, L3_gnn_b1, L3_gnn_gamma, L3_gnn_beta, L3_gnn_W2, L3_gnn_b2)
    return x

_drawn_inputs = setup_inputs


def setup_inputs(seed=0):
    import zlib

    import numpy as np

    out = dict(_drawn_inputs(seed))
    spreads = {'L0_gnn_b_s2d': (0.0, 0.8),
     'L0_gnn_b_d2s': (0.0, 0.573),
     'L0_gnn_b_l1': (0.0, 0.8),
     'L0_gnn_b_g1': (0.0, 2.0),
     'L2_gnn_gamma': (1.0, 0.542),
     'L2_gnn_beta': (0.0, 2.0),
     'L2_gnn_b1': (0.0, 0.406),
     'L2_gnn_b2': (0.0, 0.392),
     'L3_gnn_gamma': (1.0, 0.2),
     'L3_gnn_beta': (0.0, 0.375)}
    factors = {'edge_attr_32': 8.0,
     'edge_weight': 24.233,
     'L0_gnn_W_g1': 7.84,
     'L0_gnn_W_g2': 8.0,
     'L1_gnn_W1': 8.0,
     'L1_gnn_b1': 8.0,
     'L1_gnn_W2': 6.895,
     'L1_gnn_b2': 37.391,
     'L1_gnn_b3': 5.318,
     'L3_gnn_b1': 200.0,
     'L0_gnn_W_s2d': 7.269,
     'L1_gnn_b4': 2.786}
    for name, (base, spread) in spreads.items():
        noise = np.random.default_rng([zlib.crc32(name.encode()), seed]).standard_normal(out[name].shape)
        drawn = base * np.exp(spread * noise) if base else spread * noise
        out[name] = jnp.asarray(drawn.astype(out[name].dtype))
    for name, factor in factors.items():
        out[name] = (out[name] * factor).astype(out[name].dtype)
    return out
```

```python
from contextlib import ExitStack

import concourse.bass as bass
from concourse import mybir

F32 = mybir.dt.float32
I32 = mybir.dt.int32
BF16 = mybir.dt.bfloat16
ALU = mybir.AluOpType
ACT = mybir.ActivationFunctionType
AX = mybir.AxisListType.X

P = 128
NODES, EDGES, F = 6250, 200000, 64
NT = -(-NODES // P)
NP = NT * P
NB = 7
NBLK = NT // NB
BN = NB * P
GT = 4
GE = GT * P
SG = 4
ST = SG * GT
SE = ST * P
SUPERS = -(-EDGES // SE)
EP = SUPERS * SE
ITERS = SUPERS // 2
UN = 2 * SG
EC = EP // P
LEAD = 8
LN_EPS = 1e-5
BN_EPS = 1e-5
LAYERS = 3
PARTS = 3
ACCS = GT
assert NT % NB == 0 and SUPERS % 2 == 0


def bcast(ap, shape):
    return ap.to_broadcast(shape)


def node_rows(table, i):
    return table[bass.ds(i * BN, BN), :].rearrange("(t p) f -> p t f", p=P)


def super_flags(c, s):
    return c.flags.rearrange("(s g) e -> s (g e)", g=SG)[bass.ds(s, 1), :]


class Core:

    def __init__(self, nc, ctx):
        self.nc = nc

        def sb(name, shape, dt=F32):
            return ctx.enter_context(nc.sbuf_tensor(name, shape, dt))

        def dram(name, shape, dt=F32):
            return nc.dram_tensor(name, shape, dt, kind="Internal").ap()

        self.x = sb("x", [P, NT, F])
        self.h = sb("h", [P, NT, F])
        self.ends = sb("ends", [P, NT, F])
        self.ident = sb("ident", [P, P])
        self.before = sb("before", [P, P])
        self.after = sb("after", [P, P])
        self.src = sb("src", [P, EC + 2 * ST], I32)
        self.ew = sb("ew", [P, EC])
        self.trash = sb("trash", [P, 1])
        self.start_idx = sb("start_idx", [P, NT], I32)
        self.end_idx = sb("end_idx", [P, NT], I32)
        self.cnt_inv = sb("cnt_inv", [P, NT])
        self.has_in = sb("has_in", [P, NT])
        self.rs_in = sb("rs_in", [P, NT])
        self.rs_out = sb("rs_out", [P, NT])
        self.psP = ctx.enter_context(nc.psum_tensor("psP", [P, 4, 512], F32))
        self.psQ = ctx.enter_context(nc.psum_tensor("psQ", [P, 4, 512], F32))
        self.gathered = [ctx.enter_context(nc.semaphore(f"gathered{u}")) for u in range(UN)]
        self.added = [ctx.enter_context(nc.semaphore(f"added{t}")) for t in range(ACCS)]
        self.ends_in = ctx.enter_context(nc.semaphore("ends_in"))
        self.spread_in = ctx.enter_context(nc.semaphore("spread_in"))
        nums = [s.num for s in (*self.gathered, *self.added, self.ends_in, self.spread_in)]
        self.pool_sems = range(min(nums), max(nums) + 1)
        assert len(self.pool_sems) == len(nums)
        self.flags = dram("flags", [SUPERS * SG, GE], BF16)
        self.table = dram("node_table", [NP, 2 * F])
        self.table3 = dram("node_table3", [NP, F])
        self.spread = dram("spread", [EP + P, 2 * F])
        self.scans = dram("scans", [EP + P, F])
        self.acc = [dram(f"acc{k}", [NP + P, F]) for k in range(ACCS)]


def clear(c, sems):
    with c.nc.Block() as block:
        @block.sync
        def _(sp):
            for s in sems:
                sp.sem_clear(s)

        @block.gpsimd
        def _(g):
            g.dma_reset(c.pool_sems)
            g.sem_clear(c.pool_sems)


def stage(nc, tag):
    ctx = ExitStack()
    sems = []

    def sb(name, shape, dt=F32):
        return ctx.enter_context(nc.sbuf_tensor(f"{tag}_{name}", shape, dt))

    def sem(name):
        sems.append(ctx.enter_context(nc.semaphore(name)))
        return sems[-1]

    return ctx, sb, sem, sems


def prepare(c, x_in, src_cols, dst_cols, ew_cols, dst_seq, dst_prev):
    nc = c.nc
    ctx, sb, sem, sems = stage(nc, "prepare")
    with ctx:
        dst_i = sb("dst_i", [P, EC], I32)
        part_i = sb("part_i", [P, EC], I32)
        lo = [sb(f"lo{k}", [P, EC], BF16) for k in range(2)]
        hi = [sb(f"hi{k}", [P, EC], BF16) for k in range(2)]
        parts = sb("parts", [P, PARTS, EC], BF16)
        left = [sb(f"left{j}", [P, EC]) for j in range(PARTS - 1)]
        columns = sb("columns", [P, P, ST], BF16)
        seq = sb("seq", [P, EC], I32)
        prev = sb("prev", [P, EC], I32)
        flg = sb("flg", [P, EC], BF16)
        iota_i = sb("iota_i", [P, P], I32)
        trash_i = sb("trash_i", [P, 1], I32)
        zeros = sb("zeros", [P, 2048])
        ones = sb("ones", [P, P])
        oh = [[sb(f"oh{w}{k}", [P, P, ST], BF16) for k in range(2)] for w in range(2)]
        hot = [[sb(f"hot{w}{k}", [P, 1 + PARTS, NT, ST], BF16) for k in range(2)] for w in range(2)]
        cnt = sb("cnt", [P, NT])
        deg = sb("deg", [P, 2, NT])
        t0 = sb("t0", [P, NT])
        t1 = sb("t1", [P, NT])
        t2 = sb("t2", [P, NT])
        t3 = sb("t3", [P, NT])
        t4 = sb("t4", [P, NT])
        far = sb("far", [P, 1])

        loaded, seqs, made, split = sem("loaded"), sem("seqs"), sem("made"), sem("split")
        cut, added = sem("cut"), sem("added_up")
        cleared, flagged, flags_out = sem("cleared"), sem("flagged"), sem("flags_out")
        oh_made, binned, step, sums, rooted = (sem("oh_made"), sem("binned"), sem("step"),
                                               sem("sums"), sem("rooted"))
        zeroed = sem("zeroed")

        out_bins = c.psQ[:, 0, 0:PARTS * NT]
        in_bins = c.psQ[:, 1, 0:(1 + PARTS) * NT]
        within = c.psQ[:, 2, 0:NT]
        totals = c.psQ[:, 3, 0:NT]

        block = ctx.enter_context(nc.Block())

        @block.sync
        def _(sp):
            sp.dma_start(c.src[:, 0:EC], src_cols).then_inc(loaded, 16)
            sp.dma_start(dst_i[:, :], dst_cols).then_inc(loaded, 16)
            sp.dma_start(c.ew[:, :], ew_cols).then_inc(loaded, 16)
            sp.dma_start(c.x[:, :, :], x_in.rearrange("(t p) f -> p t f", p=P)).then_inc(loaded, 16)
            sp.dma_start(seq[:, :], dst_seq).then_inc(seqs, 16)
            sp.dma_start(prev[:, :], dst_prev).then_inc(seqs, 16)
            sp.wait_ge(flagged, 1)
            sp.dma_start(c.flags.rearrange("s e -> (s e)").rearrange("(p c) -> p c", p=P),
                         flg[:, :]).then_inc(flags_out, 16)
            sp.wait_ge(cleared, 1)
            sp.dma_start(c.scans[EP:EP + P, :], zeros[:, 0:F]).then_inc(zeroed, 16)
            for a in c.acc:
                sp.dma_start(a[0:NP, :].rearrange("(p t) f -> p (t f)", p=P)[:, 0:2048],
                             zeros[:, :]).then_inc(zeroed, 16)
                sp.dma_start(a[0:NP, :].rearrange("(p t) f -> p (t f)", p=P)[:, 2048:NT * F],
                             zeros[:, 0:NT * F - 2048]).then_inc(zeroed, 16)
                sp.dma_start(a[NP:NP + P, :], zeros[:, 0:F]).then_inc(zeroed, 16)
            with sp.Fori(0, SUPERS) as s:
                sp.dma_start(c.spread[bass.ds(s * SE, SE), :].rearrange("(p t) f -> p (t f)", p=P),
                             zeros[:, :]).then_inc(zeroed, 16)
            sp.wait_ge(flags_out, 16)
            sp.wait_ge(zeroed, 16 * (1 + 3 * ACCS + SUPERS))

        @block.gpsimd
        def _(g):
            g.memset(c.ident[:, :], 0.0).then_inc(made, 1)
            g.memset(c.before[:, :], 1.0).then_inc(made, 1)
            g.memset(c.after[:, :], 1.0).then_inc(made, 1)
            g.memset(ones[:, :], 1.0).then_inc(made, 1)
            g.iota(iota_i[:, :], pattern=[[1, P]], base=0, channel_multiplier=0).then_inc(made, 1)
            g.iota(trash_i[:, :], pattern=[[1, 1]], base=NP, channel_multiplier=1).then_inc(made, 1)
            g.wait_ge(made, 6)
            g.affine_select(out=c.ident[:, :], in_=c.ident[:, :], compare_op=ALU.not_equal, fill=1.0,
                            base=0, pattern=[[-1, P]], channel_multiplier=1).then_inc(made, 1)
            g.affine_select(out=c.before[:, :], in_=c.before[:, :], compare_op=ALU.is_gt, fill=0.0,
                            base=0, pattern=[[1, P]], channel_multiplier=-1).then_inc(made, 1)
            g.affine_select(out=c.after[:, :], in_=c.after[:, :], compare_op=ALU.is_gt, fill=0.0,
                            base=0, pattern=[[-1, P]], channel_multiplier=1).then_inc(made, 1)

        @block.scalar
        def _(a):
            a.wait_ge(step, 3)
            a.activation(deg[:, :, :], deg[:, :, :], ACT.Sqrt).then_inc(rooted, 1)

        @block.vector
        def _(v):
            v.memset(zeros[:, :], 0.0).then_inc(cleared, 1)
            v.memset(c.src[:, EC:EC + 2 * ST], 0)
            v.wait_ge(made, 9)
            v.tensor_copy(columns[:, :, :], bcast(iota_i[:, :].unsqueeze(2), [P, P, ST])).then_inc(split, 1)
            v.tensor_copy(c.trash[:, :], trash_i[:, :]).then_inc(split, 1)
            v.wait_ge(loaded, 64)
            for k, idx in enumerate((c.src[:, 0:EC], dst_i[:, :])):
                v.wait_ge(split, 2 + 4 * k)
                v.tensor_scalar(part_i[:, :], idx, P - 1, None, ALU.bitwise_and).then_inc(split, 1)
                v.wait_ge(split, 3 + 4 * k)
                v.tensor_copy(lo[k][:, :], part_i[:, :]).then_inc(split, 1)
                v.wait_ge(split, 4 + 4 * k)
                v.tensor_scalar(part_i[:, :], idx, 7, None, ALU.logical_shift_right).then_inc(split, 1)
                v.wait_ge(split, 5 + 4 * k)
                v.tensor_copy(hi[k][:, :], part_i[:, :]).then_inc(split, 1)
            v.wait_ge(seqs, 32)
            v.tensor_tensor(flg[:, :], seq[:, :], prev[:, :], ALU.is_equal).then_inc(flagged, 1)
            v.wait_ge(split, 10)
            v.tensor_scalar(far[:, :], c.trash[:, :], float(EP - NP), None, ALU.add).then_inc(split, 1)
            v.tensor_copy(parts[:, 0, :], c.ew[:, :]).then_inc(cut, 1)
            for j in range(PARTS - 1):
                rest = c.ew if j == 0 else left[j - 1]
                v.wait_ge(cut, 2 * j + 1)
                v.tensor_tensor(left[j][:, :], rest[:, :], parts[:, j, :], ALU.subtract).then_inc(cut, 1)
                v.wait_ge(cut, 2 * j + 2)
                v.tensor_copy(parts[:, j + 1, :], left[j][:, :]).then_inc(cut, 1)
            v.wait_ge(cut, 2 * PARTS - 1)
            v.wait_ge(split, 11)
            v.sem_inc(oh_made, LEAD)
            with v.Fori(0, ITERS) as i:
                for k in range(2):
                    cols = bass.ds((i * 2 + k) * ST, ST)
                    v.wait_ge(binned, i * 2 + k - 1 + LEAD)
                    for w in range(2):
                        v.tensor_tensor(hot[w][k][:, 0, :, :], columns[:, 0:NT, :],
                                        bcast(hi[w][:, cols].unsqueeze(1), [P, NT, ST]),
                                        ALU.is_equal).then_inc(oh_made, 1)
                    for w in range(2):
                        v.tensor_tensor(oh[w][k][:, :, :], columns[:, :, :],
                                        bcast(lo[w][:, cols].unsqueeze(1), [P, P, ST]),
                                        ALU.is_equal).then_inc(oh_made, 1)
                    for w in range(2):
                        v.wait_ge(oh_made, i * 12 + 6 * k + 1 + w + LEAD)
                        v.tensor_tensor(hot[w][k][:, 1:1 + PARTS, :, :],
                                        bcast(hot[w][k][:, 0:1, :, :], [P, PARTS, NT, ST]),
                                        bcast(parts[:, :, cols].unsqueeze(2), [P, PARTS, NT, ST]),
                                        ALU.mult).then_inc(oh_made, 1)
            v.wait_ge(binned, SUPERS + 1 + LEAD)
            v.tensor_copy(cnt[:, :], in_bins[:, 0:NT]).then_inc(step, 1)
            for w, (bins, at) in enumerate(((in_bins, 1), (out_bins, 0))):
                v.tensor_reduce(deg[:, w, :], bins[:, at * NT:(at + PARTS) * NT]
                                .rearrange("p (j n) -> p n j", j=PARTS), AX, ALU.add).then_inc(added, 1)
            v.wait_ge(added, 2)
            v.tensor_scalar(deg[:, :, :], deg[:, :, :], 1.0, None, ALU.max).then_inc(step, 2)
            v.wait_ge(step, 3)
            v.tensor_scalar(t0[:, :], cnt[:, :], 1.0, None, ALU.max).then_inc(step, 1)
            v.wait_ge(step, 4)
            v.reciprocal(c.cnt_inv[:, :], t0[:, :]).then_inc(step, 1)
            v.wait_ge(step, 5)
            v.tensor_tensor(c.has_in[:, :], cnt[:, :], c.cnt_inv[:, :], ALU.mult).then_inc(step, 1)
            v.tensor_scalar(t1[:, :], cnt[:, :], 0.0, None, ALU.is_equal).then_inc(step, 1)
            v.wait_ge(split, 11)
            v.wait_ge(sums, 2)
            v.wait_ge(step, 7)
            v.memset(t2[:, :], 0.0).then_inc(step, 1)
            v.wait_ge(step, 8)
            v.tensor_tensor_scan(t0[:, :], t2[:, :], totals, 0.0, ALU.add, ALU.add).then_inc(step, 1)
            v.wait_ge(step, 9)
            v.tensor_tensor(t0[:, :], t0[:, :], totals, ALU.subtract).then_inc(step, 1)
            v.wait_ge(step, 10)
            v.tensor_tensor(t4[:, :], t0[:, :], within, ALU.add).then_inc(step, 1)
            v.wait_ge(step, 11)
            v.tensor_scalar(t3[:, :], t4[:, :], -1.0, far[:, 0:1], ALU.mult, ALU.add).then_inc(step, 1)
            v.scalar_tensor_tensor(out=t2[:, :], in0=t4[:, :], scalar=-1.0, in1=cnt[:, :],
                                   op0=ALU.add, op1=ALU.add).then_inc(step, 1)
            v.wait_ge(step, 13)
            v.tensor_scalar(t0[:, :], t2[:, :], -1.0, float(EP), ALU.mult, ALU.add).then_inc(step, 1)
            v.wait_ge(step, 14)
            v.tensor_tensor(t0[:, :], t0[:, :], t1[:, :], ALU.mult).then_inc(step, 1)
            v.wait_ge(step, 15)
            v.tensor_tensor(c.end_idx[:, :], t0[:, :], t2[:, :], ALU.add).then_inc(step, 1)
            v.tensor_tensor(t3[:, :], t3[:, :], t1[:, :], ALU.mult).then_inc(step, 1)
            v.wait_ge(step, 17)
            v.tensor_tensor(c.start_idx[:, :], t3[:, :], t4[:, :], ALU.add).then_inc(step, 1)
            v.wait_ge(rooted, 1)
            v.reciprocal(c.rs_in[:, :], deg[:, 0, :]).then_inc(step, 1)
            v.reciprocal(c.rs_out[:, :], deg[:, 1, :]).then_inc(step, 1)

        @block.tensor
        def _(pe):
            pe.sem_inc(binned, LEAD)
            pe.wait_ge(cleared, 1)
            pe.matmul(out_bins, zeros[:, 0:P], zeros[:, 0:PARTS * NT], start=True, stop=False,
                      skip_group_check=True)
            pe.matmul(in_bins, zeros[:, 0:P], zeros[:, 0:(1 + PARTS) * NT], start=True, stop=False,
                      skip_group_check=True)
            with pe.Fori(0, ITERS) as i:
                for k in range(2):
                    pe.wait_ge(oh_made, i * 12 + 6 * k + 6 + LEAD)
                    for t in range(ST):
                        pe.matmul(out_bins, oh[0][k][:, :, t], hot[0][k][:, 1:1 + PARTS, :, t],
                                  start=False, stop=False, skip_group_check=True)
                        mm = pe.matmul(in_bins, oh[1][k][:, :, t], hot[1][k][:, :, :, t],
                                       start=False, stop=False, skip_group_check=True)
                    mm.then_inc(binned, 1)
            pe.matmul(out_bins, zeros[:, 0:P], zeros[:, 0:PARTS * NT], start=False, stop=True,
                      skip_group_check=True)
            pe.matmul(in_bins, zeros[:, 0:P], zeros[:, 0:(1 + PARTS) * NT], start=False, stop=True,
                      skip_group_check=True).then_inc(binned, 1)
            pe.wait_ge(made, 9)
            pe.wait_ge(step, 1)
            pe.matmul(within, c.before[:, :], cnt[:, :], start=True, stop=True).then_inc(sums, 1)
            pe.matmul(totals, ones[:, :], cnt[:, :], start=True, stop=True).then_inc(sums, 1)
    clear(c, sems)


def layernorm_relu(v, c, s, step, at, rooted):
    v.wait_ge(step, at)
    v.tensor_reduce(s["mean"][:, :], c.x[:, :, :], AX, ALU.add).then_inc(step, 1)
    v.wait_ge(step, at + 1)
    v.tensor_scalar(s["mean"][:, :], s["mean"][:, :], 1.0 / F, None, ALU.mult).then_inc(step, 1)
    v.wait_ge(step, at + 2)
    v.tensor_tensor(c.h[:, :, :], c.x[:, :, :], bcast(s["mean"][:, :].unsqueeze(2), [P, NT, F]),
                    ALU.subtract).then_inc(step, 1)
    v.wait_ge(step, at + 3)
    v.tensor_tensor(s["sq"][:, :, :], c.h[:, :, :], c.h[:, :, :], ALU.mult).then_inc(step, 1)
    v.wait_ge(step, at + 4)
    v.tensor_reduce(s["mean"][:, :], s["sq"][:, :, :], AX, ALU.add)\
        .then_inc(step, 1)
    v.wait_ge(step, at + 5)
    v.tensor_scalar(s["var"][:, :], s["mean"][:, :], 1.0 / F, LN_EPS, ALU.mult, ALU.add).then_inc(step, 1)
    v.wait_ge(rooted, 1)
    v.reciprocal(s["rstd"][:, :], s["root"][:, :]).then_inc(step, 1)
    v.wait_ge(step, at + 7)
    v.scalar_tensor_tensor(out=c.h[:, :, :], in0=c.h[:, :, :], scalar=0.0,
                           in1=bcast(s["rstd"][:, :].unsqueeze(2), [P, NT, F]),
                           op0=ALU.max, op1=ALU.mult).then_inc(step, 1)


LN_STEPS = 8


def layernorm_buffers(sb):
    s = {k: sb(f"ln_{k}", [P, NT]) for k in ("mean", "var", "root", "rstd")}
    s["sq"] = sb("ln_sq", [P, NT, F])
    return s


def turn_block(pe, c, rows, width=F):
    for t in range(NB):
        mm = pe.transpose(c.psQ[0:width, t // 4, (t % 4) * P:(t % 4 + 1) * P], rows[:, t, :], c.ident[:, :])
    return mm


def copy_turned(a, c, dst, width=F):
    a.copy(dst[0:width, 0:4 * P], c.psQ[0:width, 0, :])
    return a.copy(dst[0:width, 4 * P:BN], c.psQ[0:width, 1, 0:3 * P])


def nodes0(c, W_l1, b_l1, W_s2d, b_s2d, W_d2s, b_d2s):
    nc = c.nc
    ctx, sb, sem, sems = stage(nc, "nodes0")
    with ctx:
        s = layernorm_buffers(sb)
        w = sb("w", [F + 1, 4 * F])
        rows = sb("rows", [P, NB, F])
        turned_sb = sb("turned_sb", [F + 1, BN])
        out_rows = sb("out_rows", [P, NB, 2 * F])
        in_rows = sb("in_rows", [P, NB, 2 * F])
        idx = sb("idx", [P, NB], I32)
        weights, w_init, step, rooted = sem("weights"), sem("w_init"), sem("step"), sem("rooted")
        staged, turned, copied, proj, scaled = (sem("staged"), sem("turned"), sem("copied"),
                                                sem("proj"), sem("scaled"))
        stored, spread = sem("stored"), c.spread_in
        made = c.psP[:, :, :].rearrange("p b (j n) -> p (b j) n", j=2)
        block = ctx.enter_context(nc.Block())

        @block.sync
        def _(sp):
            sp.wait_ge(w_init, 2)
            for k, m in enumerate((W_l1[0:F, :], W_s2d, W_l1[F:2 * F, :], W_d2s)):
                sp.dma_start(w[0:F, k * F:(k + 1) * F], m).then_inc(weights, 16)
            for k, b in ((1, b_s2d), (2, b_l1), (3, b_d2s)):
                sp.dma_start(w[F:F + 1, k * F:(k + 1) * F], b.unsqueeze(0)).then_inc(weights, 16)
            with sp.Fori(0, NBLK) as i:
                sp.wait_ge(scaled, i * 5 + 5)
                sp.dma_start(node_rows(c.table, i), out_rows[:, :, :]).then_inc(stored, 16)
            sp.wait_ge(stored, 16 * NBLK)

        @block.gpsimd
        def _(g):
            g.memset(turned_sb[F:F + 1, :], 1.0).then_inc(w_init, 1)
            with g.Fori(0, NBLK) as i:
                rows_in = g.to_reg(i * 5 + 5)
                g.wait_ge(w_init, 2)
                g.wait_ge(scaled, rows_in)
                for t in range(NB):
                    g.indirect_dma_start(c.spread[:, :], bass.IndirectOffsetOnAxis(ap=idx[:, t:t + 1], axis=0),
                                         in_rows[:, t, :], None).then_inc(spread, 16)
            g.wait_ge(spread, 16 * NT)

        @block.vector
        def _(v):
            v.memset(w[F:F + 1, 0:F], 0.0).then_inc(w_init, 1)
            layernorm_relu(v, c, s, step, 0, rooted)
            v.wait_ge(step, LN_STEPS)
            v.tensor_tensor(c.x[:, :, :], c.x[:, :, :], c.h[:, :, :], ALU.add).then_inc(step, 1)
            with v.Fori(0, NBLK) as i:
                cols = bass.ds(i * NB, NB)
                v.wait_ge(proj, i + 1)
                v.wait_ge(stored, i * 16)
                v.wait_ge(spread, i * (16 * NB))
                v.tensor_copy(idx[:, :], c.start_idx[:, cols]).then_inc(scaled, 1)
                v.tensor_copy(out_rows[:, :, 0:F], made[:, 0:NB, 0:F]).then_inc(scaled, 1)
                v.tensor_copy(in_rows[:, :, 0:F], made[:, 0:NB, 2 * F:3 * F]).then_inc(scaled, 1)
                v.tensor_tensor(out_rows[:, :, F:2 * F], made[:, 0:NB, F:2 * F],
                                bcast(c.rs_out[:, cols].unsqueeze(2), [P, NB, F]),
                                ALU.mult).then_inc(scaled, 1)
                v.tensor_tensor(in_rows[:, :, F:2 * F], made[:, 0:NB, 3 * F:4 * F],
                                bcast(c.rs_in[:, cols].unsqueeze(2), [P, NB, F]),
                                ALU.mult).then_inc(scaled, 1)

        @block.scalar
        def _(a):
            a.wait_ge(step, 6)
            a.activation(s["root"][:, :], s["var"][:, :], ACT.Sqrt).then_inc(rooted, 1)
            a.wait_ge(step, LN_STEPS)
            with a.Fori(0, NBLK) as i:
                a.wait_ge(turned, i)
                a.copy(rows[:, :, :], c.h[:, bass.ds(i * NB, NB), :]).then_inc(staged, 1)
                a.wait_ge(turned, i + 1)
                a.wait_ge(proj, i)
                copy_turned(a, c, turned_sb).then_inc(copied, 1)

        @block.tensor
        def _(pe):
            pe.wait_ge(w_init, 2)
            pe.wait_ge(weights, 16 * 7)
            with pe.Fori(0, NBLK) as i:
                rows_in, ps_free = pe.to_reg(i + 1), pe.to_reg(i)
                pe.wait_ge(w_init, 2)
                pe.wait_ge(staged, rows_in)
                pe.wait_ge(copied, ps_free)
                turn_block(pe, c, rows).then_inc(turned, 1)
                pe.wait_ge(copied, i + 1)
                pe.wait_ge(scaled, i * 5)
                for t in range(NB):
                    mm = pe.matmul(made[:, t, :], turned_sb[:, t * P:(t + 1) * P], w[:, :],
                                   start=True, stop=True)
                mm.then_inc(proj, 1)
    clear(c, sems)


def pick(v, c, idx, super_, picked):
    v.tensor_copy(idx[:, :], c.src[:, super_]).then_inc(picked, 1)


def edges0(c, src_rows, W_l2, b_l2):
    nc = c.nc
    ctx, sb, sem, sems = stage(nc, "edges0")
    with ctx:
        R = 4
        idx = [sb(f"idx{k}", [P, ST], I32) for k in range(2)]
        srow = [sb(f"srow{u}", [P, GE], I32) for u in range(UN)]
        flg = [sb(f"flg{u}", [P, GE], BF16) for u in range(UN)]
        drow = [sb(f"drow{u}", [P, GT, 2 * F]) for u in range(UN)]
        rows = [sb(f"rows{u}", [P, GT, 2 * F]) for u in range(UN)]
        carried = [sb(f"carried{r}", [P, GE]) for r in range(2)]
        act_in = sb("act_in", [P, GT, F])
        act_w = sb("act_w", [P, GT, F])
        logit = sb("logit", [P, GT])
        kept = sb("kept", [P, GT])
        v_s = [sb(f"v_s{r}", [P, GT, F]) for r in range(2)]
        v_d = [sb(f"v_d{r}", [P, GT, F]) for r in range(2)]
        same = [sb(f"same{r}", [P, GT, P]) for r in range(2)]
        earlier = sb("earlier", [P, GT, P])
        rank = sb("rank", [P, GT])
        off = sb("off", [P, GT])
        away = sb("away", [P, GT])
        scn = [sb(f"scn{r}", [F, GE]) for r in range(2)]
        to_acc = [sb(f"to_acc{r}", [P, GT, F]) for r in range(R)]
        acc_idx = [sb(f"acc_idx{r}", [P, GT], I32) for r in range(R)]
        outr = [sb(f"outr{k}", [P, ST, F]) for k in range(2)]
        wl2 = sb("wl2", [P, F])
        bl2 = sb("bl2", [P, 1])
        neg_b = sb("neg_b", [P, 1])

        consts, ready = sem("consts"), sem("ready")
        loaded = [sem(f"loaded{u}") for u in range(UN)]
        picked = sem("picked")
        gathered = c.gathered
        stored = [sem(f"stored{k}") for k in range(2)]
        added = c.added
        d_turned, d_scanned, d_back = sem("d_turned"), sem("d_scanned"), sem("d_back")
        summed_in, act_done, dotted, kept_done = (sem("summed_in"), sem("act_done"), sem("dotted"),
                                                  sem("kept_done"))
        vs_done, vd_done, same_done, early_done, rank_done, off_done, away_done, idx_done = (
            sem("vs_done"), sem("vd_done"), sem("same_done"), sem("early_done"), sem("rank_done"),
            sem("off_done"), sem("away_done"), sem("idx_done"))
        merged, merged_out = sem("merged"), sem("merged_out")
        turned, scanned, back, copied = sem("turned"), sem("scanned"), sem("back"), sem("copied")

        ps_d = [c.psP[:, 0, :], c.psP[:, 1, :]]
        ps_e = c.psP[:, 2, :].rearrange("p (t f) -> p t f", t=GT)
        ps_m = c.psP[:, 3, 0:GT * F]
        ps_t = [c.psQ[0:F, 0, :], c.psQ[0:F, 1, :]]
        ps_b = [c.psQ[:, 2, 0:GT * F], c.psQ[:, 3, 0:GT * F]]
        block = ctx.enter_context(nc.Block())

        @block.sync
        def _(sp):
            sp.dma_start(wl2[:, :], bcast(W_l2.rearrange("f a -> a f"), [P, F])).then_inc(consts, 16)
            sp.dma_start(bl2[:, :], bcast(b_l2.unsqueeze(0), [P, 1])).then_inc(consts, 16)
            with sp.Fori(0, ITERS) as i:
                for u in range(UN):
                    sp.wait_ge(scanned, i * 8 + u + 1 - 8 + LEAD)
                    group = i * 8 + u
                    sp.dma_start(srow[u][:, :], bcast(src_rows[bass.ds(group, 1), :], [P, GE]))\
                        .then_inc(loaded[u], 16)
                    sp.dma_start(flg[u][:, :], bcast(c.flags[bass.ds(group, 1), :], [P, GE]))\
                        .then_inc(loaded[u], 16)
                    sp.dma_start(drow[u][:, :, :], c.spread[bass.ds(group * GE, GE), :]
                                 .rearrange("(t p) f -> p t f", p=P)).then_inc(loaded[u], 16)

        @block.gpsimd
        def _(g):
            for r in (2, 3):
                g.memset(to_acc[r][:, :, :], 0.0).then_inc(ready, 1)
                g.tensor_copy(acc_idx[r][:, :], bcast(c.trash[:, :], [P, GT])).then_inc(ready, 1)
            def scatter(r):
                for t in range(ACCS):
                    g.indirect_dma_start(c.acc[t][:, :],
                                         bass.IndirectOffsetOnAxis(ap=acc_idx[r][:, t:t + 1], axis=0),
                                         to_acc[r][:, t, :], None, compute_op=ALU.add)\
                        .then_inc(added[t], 16)

            with g.Fori(0, ITERS) as i:
                for u in range(UN):
                    k = u // SG
                    super_in, slot_free = g.to_reg(i * 2 + k + 1), g.to_reg(i * 8 + u + 1 - 8 + LEAD)
                    g.wait_ge(ready, 7)
                    g.wait_ge(picked, super_in)
                    g.wait_ge(vs_done, slot_free)
                    for t in range(GT):
                        col = (u % SG) * GT + t
                        g.indirect_dma_start(rows[u][:, t, :], None, c.table[:, :],
                                             bass.IndirectOffsetOnAxis(ap=idx[k][:, col:col + 1], axis=0))\
                            .then_inc(gathered[u], 16)
                    done2, acc_free = g.to_reg(i * 8 + u - 1 + LEAD), g.to_reg(i * 128 + 16 * u)
                    g.wait_ge(ready, 7)
                    g.wait_ge(merged_out, done2)
                    g.wait_ge(idx_done, done2)
                    for t in range(ACCS):
                        g.wait_ge(added[t], acc_free)
                    scatter((u - 2) % R)
            for n in range(2):
                g.wait_ge(merged_out, SUPERS * SG - 1 + n + LEAD)
                g.wait_ge(idx_done, SUPERS * SG - 1 + n + LEAD)
                for t in range(ACCS):
                    g.wait_ge(added[t], 16 * (SUPERS * SG + n))
                scatter((SUPERS * SG - 2 + n) % R)
            for t in range(ACCS):
                g.wait_ge(added[t], 16 * (SUPERS * SG + 2))

        @block.vector
        def _(v):
            for sm in (summed_in, act_done, dotted, kept_done, vs_done, vd_done, same_done, early_done,
                       rank_done, off_done, away_done, idx_done, d_scanned, scanned):
                v.sem_inc(sm, LEAD)
            v.memset(carried[1][:, :], 0.0).then_inc(ready, 1)
            v.memset(scn[1][:, :], 0.0).then_inc(ready, 1)
            v.wait_ge(consts, 32)
            v.tensor_scalar(neg_b[:, :], bl2[:, :], -1.0, None, ALU.mult).then_inc(ready, 1)
            v.wait_ge(ready, 7)
            for k in range(2):
                pick(v, c, idx[k], slice(k * ST, (k + 1) * ST), picked)
            with v.Fori(0, ITERS) as i:
                for u in range(UN):
                    k, r, q = u // SG, u % 2, u % R
                    n = i * 8 + u + 1 + LEAD
                    tiles = slice((u % SG) * GT, (u % SG + 1) * GT)
                    v.wait_ge(picked, i * 2 + k + 1)
                    v.wait_ge(loaded[u], i * 48 + 48)
                    v.wait_ge(d_turned, n)
                    v.wait_ge(d_back, n - 2)
                    v.wait_ge(d_scanned, n - 1)
                    v.tensor_tensor_scan(carried[r][:, :], flg[u][:, :], ps_d[r],
                                         carried[1 - r][:, GE - 1:GE], ALU.mult, ALU.add)\
                        .then_inc(d_scanned, 1)
                    v.wait_ge(merged, n - 2)
                    v.tensor_tensor(same[r][:, :, :],
                                    srow[u][:, :].rearrange("p (t e) -> p t e", t=GT),
                                    bcast(idx[k][:, tiles].unsqueeze(2), [P, GT, P]), ALU.is_equal)\
                        .then_inc(same_done, 1)
                    v.wait_ge(same_done, n)
                    v.wait_ge(rank_done, n - 1)
                    v.tensor_tensor(earlier[:, :, :], same[r][:, :, :],
                                    bcast(c.after[:, :].unsqueeze(1), [P, GT, P]), ALU.mult)\
                        .then_inc(early_done, 1)
                    v.wait_ge(gathered[u], i * 64 + 64)
                    v.wait_ge(d_back, n)
                    v.tensor_tensor(act_in[:, :, :], rows[u][:, :, 0:F], ps_e[:, :, 0:F], ALU.add)\
                        .then_inc(summed_in, 1)
                    v.wait_ge(early_done, n)
                    v.wait_ge(away_done, n - 1)
                    v.tensor_reduce(rank[:, :], earlier[:, :, :], AX, ALU.add).then_inc(rank_done, 1)
                    v.wait_ge(summed_in, n)
                    v.wait_ge(dotted, n - 1)
                    v.scalar_tensor_tensor(out=act_w[:, :, :], in0=act_in[:, :, :], scalar=0.0,
                                           in1=bcast(wl2[:, :].unsqueeze(1), [P, GT, F]), op0=ALU.max,
                                           op1=ALU.mult).then_inc(act_done, 1)
                    v.wait_ge(idx_done, n - 1)
                    v.tensor_scalar(off[:, :], idx[k][:, tiles], -1.0, c.trash[:, 0:1], ALU.mult, ALU.add)\
                        .then_inc(off_done, 1)
                    v.wait_ge(act_done, n)
                    v.tensor_reduce(logit[:, :], act_w[:, :, :], AX, ALU.add).then_inc(dotted, 1)
                    v.wait_ge(off_done, n)
                    v.wait_ge(rank_done, n)
                    v.scalar_tensor_tensor(out=away[:, :], in0=rank[:, :], scalar=0.0, in1=off[:, :],
                                           op0=ALU.is_gt, op1=ALU.mult).then_inc(away_done, 1)
                    v.wait_ge(dotted, n)
                    v.wait_ge(vd_done, n - 1)
                    v.scalar_tensor_tensor(out=kept[:, :], in0=logit[:, :], scalar=neg_b[:, 0:1],
                                           in1=c.ew[:, bass.ds((i * 8 + u) * GT, GT)], op0=ALU.is_ge, op1=ALU.mult)\
                        .then_inc(kept_done, 1)
                    v.wait_ge(kept_done, n)
                    v.wait_ge(away_done, n)
                    for t in range(ACCS):
                        v.wait_ge(added[t], i * 128 + 16 * u)
                    v.tensor_tensor(acc_idx[q][:, :], away[:, :], idx[k][:, tiles], ALU.add)\
                        .then_inc(idx_done, 1)
                    v.wait_ge(turned, n - 2)
                    v.tensor_tensor(v_s[r][:, :, :], rows[u][:, :, F:2 * F],
                                    bcast(kept[:, :].unsqueeze(2), [P, GT, F]), ALU.mult)\
                        .then_inc(vs_done, 1)
                    v.tensor_tensor(v_d[r][:, :, :], ps_e[:, :, F:2 * F],
                                    bcast(kept[:, :].unsqueeze(2), [P, GT, F]), ALU.mult)\
                        .then_inc(vd_done, 1)
                    v.wait_ge(turned, n)
                    v.wait_ge(back, n - 2)
                    v.wait_ge(scanned, n - 1)
                    v.tensor_tensor_scan(scn[r][:, :], flg[u][0:F, :], ps_t[r],
                                         scn[1 - r][:, GE - 1:GE], ALU.mult, ALU.add)\
                        .then_inc(scanned, 1)
                    if u % SG == SG - 1:
                        v.wait_ge(gathered[u], i * 64 + 64)
                        v.wait_ge(idx_done, n)
                        pick(v, c, idx[k], bass.ds((i * 2 + k + 2) * ST, ST), picked)

        @block.tensor
        def _(pe):
            for sm in (d_turned, d_back, merged, turned, back):
                pe.sem_inc(sm, LEAD)
            with pe.Fori(0, ITERS) as i:
                def turn_dst(u):
                    k, r, n = u // SG, u % 2, i * 8 + u + 1 + LEAD
                    pe.wait_ge(loaded[u], i * 48 + 48)
                    pe.wait_ge(d_scanned, n - 2)
                    for t in range(GT):
                        mm = pe.transpose(ps_d[r][:, t * P:(t + 1) * P], drow[u][:, t, :],
                                          c.ident[:, :])
                    mm.then_inc(d_turned, 1)

                turn_dst(0)
                for u in range(UN):
                    k, r, n = u // SG, u % 2, i * 8 + u + 1 + LEAD
                    pe.wait_ge(d_scanned, n)
                    pe.wait_ge(vd_done, n - 1)
                    for t in range(GT):
                        mm = pe.transpose(ps_e[:, t, :], carried[r][:, t * P:(t + 1) * P], c.ident[:, :])
                    mm.then_inc(d_back, 1)
                    if u + 1 < UN:
                        turn_dst(u + 1)
                    v_s_in, ps_free = pe.to_reg(n), pe.to_reg(n - 2)
                    pe.wait_ge(ready, 7)
                    pe.wait_ge(vs_done, v_s_in)
                    pe.wait_ge(scanned, ps_free)
                    for t in range(GT):
                        mm = pe.transpose(ps_t[r][:, t * P:(t + 1) * P], v_s[r][:, t, :], c.ident[:, :])
                    mm.then_inc(turned, 1)
                    pe.wait_ge(vd_done, n)
                    pe.wait_ge(same_done, n)
                    pe.wait_ge(merged_out, n - 1)
                    for t in range(GT):
                        mm = pe.matmul(ps_m[:, t * F:(t + 1) * F], same[r][:, t, :], v_d[r][:, t, :],
                                       start=True, stop=True)
                    mm.then_inc(merged, 1)
                    scan_in, ps_free = pe.to_reg(n), pe.to_reg(n - 2)
                    pe.wait_ge(ready, 7)
                    pe.wait_ge(scanned, scan_in)
                    pe.wait_ge(copied, ps_free)
                    for t in range(GT):
                        mm = pe.transpose(ps_b[r][:, t * F:(t + 1) * F], scn[r][:, t * P:(t + 1) * P],
                                          c.ident[0:F, 0:F])
                    mm.then_inc(back, 1)

        @block.scalar
        def _(a):
            for sm in (merged_out, copied):
                a.sem_inc(sm, LEAD)
            with a.Fori(0, ITERS) as i:
                for u in range(UN):
                    k, r, q, n = u // SG, u % 2, u % R, i * 8 + u + 1 + LEAD
                    a.wait_ge(merged, n)
                    for t in range(ACCS):
                        a.wait_ge(added[t], i * 128 + 16 * u)
                    a.copy(to_acc[q][:, :, :].rearrange("p t f -> p (t f)"), ps_m).then_inc(merged_out, 1)
                    if u % SG == 0:
                        a.wait_ge(stored[k], i * 16)
                    a.wait_ge(back, n)
                    a.copy(outr[k][:, (u % SG) * GT:(u % SG + 1) * GT, :].rearrange("p t f -> p (t f)"),
                           ps_b[r]).then_inc(copied, 1)
                    if u % SG == SG - 1:
                        a.wait_ge(copied, n)
                        a.dma_start(c.scans[bass.ds((i * 2 + k) * SE, SE), :]
                                    .rearrange("(t p) f -> p t f", p=P), outr[k][:, :, :])\
                            .then_inc(stored[k], 16)
            for k in range(2):
                a.wait_ge(stored[k], 16 * ITERS)
    clear(c, sems)


def gather_ends(g, c, ready, gathered):
    for t in range(NT):
        g.indirect_dma_start(c.ends[:, t, :], None, c.scans[:, :],
                             bass.IndirectOffsetOnAxis(ap=c.end_idx[:, t:t + 1], axis=0)).then_inc(gathered, 16)


def nodes1(c, W_g1, b_g1, W_g2, b_g2, W1, b1):
    nc = c.nc
    ctx, sb, sem, sems = stage(nc, "nodes1")
    with ctx:
        s = layernorm_buffers(sb)
        acc = [sb(f"acc_sb{k}", [P, NT, F]) for k in range(ACCS)]
        cat = sb("cat", [P, NT, 2 * F])
        wg1 = sb("wg1", [2 * F, F])
        bg1 = sb("bg1", [F, 1])
        wg2 = sb("wg2", [F, 1])
        bg2 = sb("bg2", [P, 1])
        gate = sb("gate", [P, NT])
        w = sb("w", [F + 1, 2 * F])
        rows = sb("rows", [P, NB, 2 * F])
        turned_sb = sb("turned_sb", [2 * F, BN])
        hidden = sb("hidden", [F, BN])
        h_rows = sb("h_rows", [P, NB, F])
        h_turned = sb("h_turned", [F + 1, BN])
        out_rows = sb("out_rows", [P, NB, 2 * F])
        weights, accs, ends, step, rooted, one = (sem("weights"), sem("accs"), c.ends_in, sem("step"),
                                                  sem("rooted"), sem("one"))
        staged, turned, copied, mixed, bent, dots, gated = (sem("staged"), sem("turned"), sem("copied"),
                                                            sem("mixed"), sem("bent"), sem("dots"),
                                                            sem("gated"))
        staged2, turned2, copied2, proj, out_made, stored = (sem("staged2"), sem("turned2"), sem("copied2"),
                                                             sem("proj"), sem("out_made"), sem("stored"))
        ps_mix = [c.psQ[0:F, 2, 0:BN // 2], c.psQ[0:F, 3, 0:BN // 2]]
        ps_dot = c.psP[:, 0, 0:NB]
        made = c.psP[:, 1:3, :].rearrange("p b (j n) -> p (b j) n", j=4)
        block = ctx.enter_context(nc.Block())

        @block.sync
        def _(sp):
            for k in range(ACCS):
                sp.dma_start(acc[k][:, :, :], c.acc[k][0:NP, :].rearrange("(t p) f -> p t f", p=P))\
                    .then_inc(accs, 16)
            sp.dma_start(wg1[:, :], W_g1).then_inc(weights, 16)
            sp.dma_start(bg1[:, :], b_g1.unsqueeze(1)).then_inc(weights, 16)
            sp.dma_start(wg2[:, :], W_g2).then_inc(weights, 16)
            sp.dma_start(bg2[:, :], bcast(b_g2.unsqueeze(0), [P, 1])).then_inc(weights, 16)
            sp.dma_start(w[0:F, :], W1[0:F, :]).then_inc(weights, 16)
            sp.dma_start(w[F:F + 1, :], b1.unsqueeze(0)).then_inc(weights, 16)
            with sp.Fori(0, NBLK) as i:
                sp.wait_ge(out_made, i + 1)
                sp.dma_start(node_rows(c.table, i), out_rows[:, :, :]).then_inc(stored, 16)
            sp.wait_ge(stored, 16 * NBLK)

        @block.gpsimd
        def _(g):
            g.memset(h_turned[F:F + 1, :], 1.0).then_inc(one, 1)
            gather_ends(g, c, one, ends)
            g.wait_ge(ends, 16 * NT)

        @block.vector
        def _(v):
            v.wait_ge(accs, 16 * ACCS)
            v.tensor_tensor(acc[0][:, :, :], acc[0][:, :, :], acc[1][:, :, :], ALU.add).then_inc(step, 1)
            v.tensor_tensor(acc[2][:, :, :], acc[2][:, :, :], acc[3][:, :, :], ALU.add).then_inc(step, 1)
            v.wait_ge(step, 2)
            v.tensor_tensor(acc[0][:, :, :], acc[0][:, :, :], acc[2][:, :, :], ALU.add).then_inc(step, 1)
            v.wait_ge(step, 3)
            v.tensor_tensor(cat[:, :, F:2 * F], acc[0][:, :, :],
                            bcast(c.rs_out[:, :].unsqueeze(2), [P, NT, F]), ALU.mult).then_inc(step, 1)
            v.wait_ge(ends, 16 * NT)
            v.tensor_tensor(cat[:, :, 0:F], c.ends[:, :, :],
                            bcast(c.rs_in[:, :].unsqueeze(2), [P, NT, F]), ALU.mult).then_inc(step, 1)
            v.wait_ge(step, 5)
            v.tensor_tensor(acc[1][:, :, :], cat[:, :, 0:F], cat[:, :, F:2 * F], ALU.subtract)\
                .then_inc(step, 1)
            v.wait_ge(gated, NBLK)
            v.wait_ge(step, 6)
            v.tensor_tensor(acc[1][:, :, :], acc[1][:, :, :], bcast(gate[:, :].unsqueeze(2), [P, NT, F]),
                            ALU.mult).then_inc(step, 1)
            v.wait_ge(step, 7)
            v.tensor_tensor(acc[1][:, :, :], acc[1][:, :, :], cat[:, :, F:2 * F], ALU.add)\
                .then_inc(step, 1)
            v.wait_ge(step, 8)
            v.scalar_tensor_tensor(out=c.x[:, :, :], in0=acc[1][:, :, :], scalar=0.5, in1=c.x[:, :, :],
                                   op0=ALU.mult, op1=ALU.add).then_inc(step, 1)
            layernorm_relu(v, c, s, step, 9, rooted)
            with v.Fori(0, NBLK) as i:
                v.wait_ge(proj, i + 1)
                v.wait_ge(stored, i * 16)
                v.tensor_copy(out_rows[:, :, :], made[:, 0:NB, :]).then_inc(out_made, 1)

        @block.scalar
        def _(a):
            a.wait_ge(step, 5)
            a.wait_ge(weights, 16 * 6)
            with a.Fori(0, NBLK) as i:
                a.wait_ge(turned, i)
                a.copy(rows[:, :, :], cat[:, bass.ds(i * NB, NB), :]).then_inc(staged, 1)
                a.wait_ge(turned, i + 1)
                a.wait_ge(mixed, i)
                copy_turned(a, c, turned_sb, 2 * F).then_inc(copied, 1)
                a.wait_ge(mixed, i + 1)
                a.wait_ge(dots, i)
                a.activation(hidden[:, 0:BN // 2], ps_mix[0], ACT.Relu, bias=bg1[:, 0:1])
                a.activation(hidden[:, BN // 2:BN], ps_mix[1], ACT.Relu, bias=bg1[:, 0:1]).then_inc(bent, 1)
                a.wait_ge(dots, i + 1)
                a.activation(gate[:, bass.ds(i * NB, NB)], ps_dot, ACT.Sigmoid, bias=bg2[:, 0:1])\
                    .then_inc(gated, 1)
            a.wait_ge(step, 9 + 6)
            a.activation(s["root"][:, :], s["var"][:, :], ACT.Sqrt).then_inc(rooted, 1)
            a.wait_ge(step, 9 + LN_STEPS)
            with a.Fori(0, NBLK) as i:
                a.wait_ge(turned2, i)
                a.copy(h_rows[:, :, :], c.h[:, bass.ds(i * NB, NB), :]).then_inc(staged2, 1)
                a.wait_ge(turned2, i + 1)
                a.wait_ge(proj, i)
                copy_turned(a, c, h_turned).then_inc(copied2, 1)

        @block.tensor
        def _(pe):
            pe.wait_ge(weights, 16 * 6)
            with pe.Fori(0, NBLK) as i:
                pe.wait_ge(staged, i + 1)
                pe.wait_ge(copied, i)
                turn_block(pe, c, rows, 2 * F).then_inc(turned, 1)
                turned_in, ps_free = pe.to_reg(i + 1), pe.to_reg(i)
                pe.wait_ge(weights, 16 * 6)
                pe.wait_ge(copied, turned_in)
                pe.wait_ge(bent, ps_free)
                for j in range(2):
                    mm = pe.matmul(ps_mix[j], wg1[:, :], turned_sb[:, j * BN // 2:(j + 1) * BN // 2],
                                   start=True, stop=True)
                mm.then_inc(mixed, 1)
                pe.wait_ge(weights, 16 * 6)
                pe.wait_ge(bent, turned_in)
                pe.wait_ge(gated, ps_free)
                for t in range(NB):
                    mm = pe.matmul(ps_dot[:, t:t + 1], hidden[:, t * P:(t + 1) * P], wg2[:, :],
                                   start=True, stop=True)
                mm.then_inc(dots, 1)
            pe.wait_ge(one, 1)
            with pe.Fori(0, NBLK) as i:
                rows_in, ps_free = pe.to_reg(i + 1), pe.to_reg(i)
                pe.wait_ge(one, 1)
                pe.wait_ge(staged2, rows_in)
                pe.wait_ge(copied2, ps_free)
                turn_block(pe, c, h_rows).then_inc(turned2, 1)
                pe.wait_ge(one, 1)
                pe.wait_ge(copied2, rows_in)
                pe.wait_ge(out_made, ps_free)
                for t in range(NB):
                    mm = pe.matmul(made[:, t, :], h_turned[:, t * P:(t + 1) * P], w[:, :],
                                   start=True, stop=True)
                mm.then_inc(proj, 1)
    clear(c, sems)


def edges1(c, attr_g, W1, W2):
    nc = c.nc
    FE = P // SG
    ctx, sb, sem, sems = stage(nc, "edges1")
    with ctx:
        idx = [sb(f"idx{k}", [P, ST], I32) for k in range(2)]
        flg = [sb(f"flg{k}", [F, SE], BF16) for k in range(2)]
        attr = [sb(f"attr{k}", [P, GE]) for k in range(2)]
        rows = [sb(f"rows{u}", [P, GT, 2 * F]) for u in range(UN)]
        act = [sb(f"act{r}", [P, GE]) for r in range(2)]
        scn = [sb(f"scn{r}", [F, GE]) for r in range(2)]
        outr = [sb(f"outr{k}", [P, ST, F]) for k in range(2)]
        w1 = sb("w1", [P, SG, 2 * F])
        w2 = sb("w2", [2 * F, F])
        weights, first = sem("weights"), sem("first")
        loaded = [sem(f"loaded{k}") for k in range(2)]
        picked = sem("picked")
        gathered = c.gathered
        stored = [sem(f"stored{k}") for k in range(2)]
        summed, bent, scanned, back, copied = (sem("summed"), sem("bent"), sem("scanned"), sem("back"),
                                               sem("copied"))
        mixed = sem("mixed")
        ps_z = [c.psP[:, 0, :], c.psP[:, 1, :]]
        ps_v = [c.psP[0:F, 2, :], c.psP[0:F, 3, :]]
        ps_b = [c.psQ[:, 0, 0:GT * F], c.psQ[:, 1, 0:GT * F]]
        block = ctx.enter_context(nc.Block())

        @block.sync
        def _(sp):
            sp.wait_ge(first, 2)
            for g in range(SG):
                sp.dma_start(w1[g * FE:(g + 1) * FE, g, :], W1[F:F + FE, :]).then_inc(weights, 16)
            sp.dma_start(w2[:, :], W2).then_inc(weights, 16)
            with sp.Fori(0, ITERS) as i:
                for k in range(2):
                    s = i * 2 + k
                    sp.wait_ge(scanned, i * 8 + 4 * k - 4 + LEAD)
                    sp.dma_start(attr[k][:, :], attr_g[bass.ds(s * P, P), :]).then_inc(loaded[k], 16)
                    sp.dma_start(flg[k][:, :], bcast(super_flags(c, s), [F, SE]))\
                        .then_inc(loaded[k], 16)

        @block.gpsimd
        def _(g):
            with g.Fori(0, ITERS) as i:
                for u in range(UN):
                    k = u // SG
                    super_in, slot_free = g.to_reg(i * 2 + k + 1), g.to_reg(i * 8 + u + 1 - 8 + LEAD)
                    g.wait_ge(weights, 16 * (SG + 1))
                    g.wait_ge(picked, super_in)
                    g.wait_ge(summed, slot_free)
                    for t in range(GT):
                        col = (u % SG) * GT + t
                        g.indirect_dma_start(rows[u][:, t, :], None, c.table[:, :],
                                             bass.IndirectOffsetOnAxis(ap=idx[k][:, col:col + 1], axis=0))\
                            .then_inc(gathered[u], 16)

        @block.vector
        def _(v):
            v.sem_inc(scanned, LEAD)
            v.memset(scn[1][:, :], 0.0).then_inc(first, 1)
            v.memset(w1[:, :, :], 0.0).then_inc(first, 1)
            v.wait_ge(first, 2)
            for k in range(2):
                pick(v, c, idx[k], slice(k * ST, (k + 1) * ST), picked)
            with v.Fori(0, ITERS) as i:
                for u in range(UN):
                    k, r, n = u // SG, u % 2, i * 8 + u + 1 + LEAD
                    v.wait_ge(loaded[k], i * 32 + 32)
                    v.wait_ge(mixed, n)
                    v.wait_ge(back, n - 2)
                    v.wait_ge(scanned, n - 1)
                    v.tensor_tensor_scan(scn[r][:, :], flg[k][:, (u % SG) * GE:(u % SG + 1) * GE],
                                         ps_v[r], scn[1 - r][:, GE - 1:GE], ALU.mult, ALU.add)\
                        .then_inc(scanned, 1)
                    if u % SG == SG - 1:
                        v.wait_ge(gathered[u], i * 64 + 64)
                        pick(v, c, idx[k], bass.ds((i * 2 + k + 2) * ST, ST), picked)

        @block.tensor
        def _(pe):
            for sm in (summed, mixed, back):
                pe.sem_inc(sm, LEAD)
            pe.wait_ge(weights, 16 * (SG + 1))
            with pe.Fori(0, ITERS) as i:
                def attr_part(u):
                    k, r, n = u // SG, u % 2, i * 8 + u + 1 + LEAD
                    pe.wait_ge(loaded[k], i * 32 + 32)
                    pe.wait_ge(bent, n - 2)
                    pe.matmul(ps_z[r], w1[:, u % SG, :], attr[k][:, :], start=True, stop=False,
                              skip_group_check=True)

                def rows_part(u):
                    r = u % 2
                    pe.wait_ge(gathered[u], i * 64 + 64)
                    for t in range(GT):
                        mm = pe.matmul(ps_z[r][:, t * P:(t + 1) * P], rows[u][:, t, :], c.ident[:, :],
                                       start=False, stop=(t == GT - 1), skip_group_check=True)
                    mm.then_inc(summed, 1)

                attr_part(0)
                rows_part(0)
                for u in range(UN):
                    r, n = u % 2, i * 8 + u + 1 + LEAD
                    if u + 1 < UN:
                        attr_part(u + 1)
                    pe.wait_ge(bent, n)
                    pe.wait_ge(scanned, n - 2)
                    pe.matmul(ps_v[r], w2[:, :], act[r][:, :], start=True, stop=True).then_inc(mixed, 1)
                    if u + 1 < UN:
                        rows_part(u + 1)
                    scan_in, out_free = pe.to_reg(n), pe.to_reg(n - 2)
                    pe.wait_ge(weights, 16 * (SG + 1))
                    pe.wait_ge(scanned, scan_in)
                    pe.wait_ge(copied, out_free)
                    for t in range(GT):
                        mm = pe.transpose(ps_b[r][:, t * F:(t + 1) * F], scn[r][:, t * P:(t + 1) * P],
                                          c.ident[0:F, 0:F])
                    mm.then_inc(back, 1)

        @block.scalar
        def _(a):
            for sm in (bent, copied):
                a.sem_inc(sm, LEAD)
            with a.Fori(0, ITERS) as i:
                for u in range(UN):
                    k, r, n = u // SG, u % 2, i * 8 + u + 1 + LEAD
                    a.wait_ge(summed, n)
                    a.wait_ge(mixed, n - 2)
                    a.activation(act[r][:, :], ps_z[r], ACT.Relu).then_inc(bent, 1)
                    if u % SG == 0:
                        a.wait_ge(stored[k], i * 16)
                    a.wait_ge(back, n)
                    a.copy(outr[k][:, (u % SG) * GT:(u % SG + 1) * GT, :].rearrange("p t f -> p (t f)"),
                           ps_b[r]).then_inc(copied, 1)
                    if u % SG == SG - 1:
                        a.wait_ge(copied, n)
                        a.dma_start(c.scans[bass.ds((i * 2 + k) * SE, SE), :]
                                    .rearrange("(t p) f -> p t f", p=P), outr[k][:, :, :])\
                            .then_inc(stored[k], 16)
            for k in range(2):
                a.wait_ge(stored[k], 16 * ITERS)
    clear(c, sems)


SC = BN // 2
NSC = -(-NODES // SC)


def batch_scale(v, b, turned_all, gamma, beta, step, at, rooted):
    for j in range(NSC):
        v.bn_stats(b["stats"][:, j, :], turned_all[:, j * SC:min((j + 1) * SC, NODES)]).then_inc(step, 1)
    v.wait_ge(step, at + NSC)
    v.bn_aggr(b["mv"][:, :], b["stats"][:, :, :].rearrange("p a b -> p (a b)")).then_inc(step, 1)
    v.wait_ge(step, at + NSC + 1)
    v.tensor_scalar(b["var"][:, :], b["mv"][:, 1:2], BN_EPS, None, ALU.add).then_inc(step, 1)
    v.wait_ge(rooted, 1)
    v.reciprocal(b["rstd"][:, :], b["root"][:, :]).then_inc(step, 1)
    v.wait_ge(step, at + NSC + 3)
    v.tensor_tensor(b["scale"][:, :], b["rstd"][:, :], gamma[:, :], ALU.mult).then_inc(step, 1)
    v.wait_ge(step, at + NSC + 4)
    v.tensor_tensor(b["rstd"][:, :], b["mv"][:, 0:1], b["scale"][:, :], ALU.mult).then_inc(step, 1)
    v.wait_ge(step, at + NSC + 5)
    v.tensor_tensor(b["shift"][:, :], beta[:, :], b["rstd"][:, :], ALU.subtract).then_inc(step, 1)


BATCH_STEPS = NSC + 6


def batch_buffers(sb):
    b = {k: sb(f"bn_{k}", [F, 1]) for k in ("var", "root", "rstd", "scale", "shift")}
    b["mv"] = sb("bn_mv", [F, 2])
    b["stats"] = sb("bn_stats", [F, NSC, 6])
    return b


def nodes2(c, u, b2, W3, b3, W4, b4, gamma, beta, W1, b1):
    nc = c.nc
    ctx, sb, sem, sems = stage(nc, "nodes2")
    with ctx:
        s = layernorm_buffers(sb)
        bn = batch_buffers(sb)
        cat = sb("cat", [P, NT, 2 * F])
        b2_row = sb("b2_row", [P, F])
        w3 = sb("w3", [2 * F, F])
        w3u = sb("w3u", [F, F])
        u0 = sb("u0", [F, 1])
        b3_col = sb("b3_col", [F, 1])
        bias3 = sb("bias3", [F, 1])
        w4 = sb("w4", [F + 1, F])
        gam = sb("gam", [F, 1])
        bet = sb("bet", [F, 1])
        w = sb("w", [F + 1, 4 * F])
        rows = sb("rows", [P, NB, 2 * F])
        turned_sb = sb("turned_sb", [2 * F, BN])
        hidden = sb("hidden", [F + 1, BN])
        h_rows = sb("h_rows", [P, NB, F])
        turned_all = sb("turned_all", [F, NP])
        xn = sb("xn", [F + 1, BN])
        out_rows = sb("out_rows", [P, NB, 2 * F])
        in_rows = sb("in_rows", [P, NB, 2 * F])
        idx = sb("idx", [P, NB], I32)
        weights, w_init, ends, step = sem("weights"), sem("w_init"), c.ends_in, sem("step")
        rooted, rooted_bn, biased, ubias = sem("rooted"), sem("rooted_bn"), sem("biased"), sem("ubias")
        staged, turned, copied, mixed, bent, outs, added = (sem("staged"), sem("turned"), sem("copied"),
                                                            sem("mixed"), sem("bent"), sem("outs"),
                                                            sem("x_added"))
        staged2, turned2, copied2 = sem("staged2"), sem("turned2"), sem("copied2")
        normed, proj, split, stored, spread = (sem("normed"), sem("proj"), sem("split_rows"), sem("stored"),
                                               c.spread_in)
        ps_mix = [c.psQ[0:F, 2, 0:BN // 2], c.psQ[0:F, 3, 0:BN // 2]]
        ps_out = c.psP[:, 0, 0:NB * F]
        made = c.psP[:, :, :].rearrange("p b (j n) -> p (b j) n", j=2)
        NW = 16 * 13
        block = ctx.enter_context(nc.Block())

        @block.sync
        def _(sp):
            sp.wait_ge(w_init, 3)
            for dst, m in ((b2_row[:, :], bcast(b2.unsqueeze(0), [P, F])), (w3[:, :], W3[0:2 * F, :]),
                           (w3u[:, :], W3[2 * F:3 * F, :]), (u0[:, :], u[0:1, :].rearrange("a f -> f a")),
                           (b3_col[:, :], b3.unsqueeze(1)), (w4[0:F, :], W4), (w4[F:F + 1, :], b4.unsqueeze(0)),
                           (gam[:, :], gamma.unsqueeze(1)), (bet[:, :], beta.unsqueeze(1)),
                           (w[0:F, 0:2 * F], W1[F:2 * F, :]), (w[0:F, 2 * F:4 * F], W1[0:F, :]),
                           (w[F:F + 1, 2 * F:4 * F], b1.unsqueeze(0))):
                sp.dma_start(dst, m).then_inc(weights, 16)
            with sp.Fori(0, NBLK) as i:
                sp.wait_ge(split, i * 3 + 3)
                sp.dma_start(node_rows(c.table, i), out_rows[:, :, :]).then_inc(stored, 16)
            sp.wait_ge(stored, 16 * NBLK)

        @block.gpsimd
        def _(g):
            g.memset(hidden[F:F + 1, :], 1.0).then_inc(w_init, 1)
            g.memset(xn[F:F + 1, :], 1.0).then_inc(w_init, 1)
            gather_ends(g, c, w_init, ends)
            with g.Fori(0, NBLK) as i:
                rows_in = g.to_reg(i * 3 + 3)
                g.wait_ge(w_init, 3)
                g.wait_ge(split, rows_in)
                for t in range(NB):
                    g.indirect_dma_start(c.spread[:, :], bass.IndirectOffsetOnAxis(ap=idx[:, t:t + 1], axis=0),
                                         in_rows[:, t, :], None).then_inc(spread, 16)
            g.wait_ge(spread, 16 * NT)

        @block.vector
        def _(v):
            v.memset(w[F:F + 1, 0:2 * F], 0.0).then_inc(w_init, 1)
            v.wait_ge(weights, 16 * 12)
            v.tensor_tensor(w[0:F, 2 * F:4 * F], w[0:F, 2 * F:4 * F], w[0:F, 0:2 * F], ALU.subtract)\
                .then_inc(step, 1)
            v.tensor_copy(cat[:, :, 0:F], c.h[:, :, :]).then_inc(step, 1)
            v.tensor_tensor(s["sq"][:, :, :], bcast(b2_row[:, :].unsqueeze(1), [P, NT, F]),
                            bcast(c.has_in[:, :].unsqueeze(2), [P, NT, F]), ALU.mult).then_inc(step, 1)
            v.wait_ge(ends, 16 * NT)
            v.tensor_tensor(cat[:, :, F:2 * F], c.ends[:, :, :],
                            bcast(c.cnt_inv[:, :].unsqueeze(2), [P, NT, F]), ALU.mult).then_inc(step, 1)
            v.wait_ge(step, 4)
            v.tensor_tensor(cat[:, :, F:2 * F], cat[:, :, F:2 * F], s["sq"][:, :, :], ALU.add)\
                .then_inc(step, 1)
            with v.Fori(0, NBLK) as i:
                cols = bass.ds(i * NB, NB)
                v.wait_ge(outs, i + 1)
                v.tensor_tensor(c.x[:, cols, :], c.x[:, cols, :],
                                ps_out.rearrange("p (t f) -> p t f", t=NB), ALU.add).then_inc(added, 1)
            v.wait_ge(added, NBLK)
            layernorm_relu(v, c, s, step, 5, rooted)
            v.wait_ge(copied2, NBLK)
            batch_scale(v, bn, turned_all, gam, bet, step, 5 + LN_STEPS, rooted_bn)
            with v.Fori(0, NBLK) as i:
                v.wait_ge(proj, i + 1)
                v.wait_ge(stored, i * 16)
                v.wait_ge(spread, i * (16 * NB))
                v.tensor_copy(idx[:, :], c.start_idx[:, bass.ds(i * NB, NB)]).then_inc(split, 1)
                v.tensor_copy(out_rows[:, :, :], made[:, 0:NB, 0:2 * F]).then_inc(split, 1)
                v.tensor_copy(in_rows[:, :, :], made[:, 0:NB, 2 * F:4 * F]).then_inc(split, 1)

        @block.scalar
        def _(a):
            a.wait_ge(ubias, 1)
            a.activation(bias3[:, :], c.psP[0:F, 3, 0:1], ACT.Identity, bias=b3_col[:, 0:1]).then_inc(biased, 1)
            a.wait_ge(biased, 1)
            a.wait_ge(step, 5)
            with a.Fori(0, NBLK) as i:
                a.wait_ge(turned, i)
                a.copy(rows[:, :, :], cat[:, bass.ds(i * NB, NB), :]).then_inc(staged, 1)
                a.wait_ge(turned, i + 1)
                a.wait_ge(mixed, i)
                copy_turned(a, c, turned_sb, 2 * F).then_inc(copied, 1)
                a.wait_ge(mixed, i + 1)
                a.wait_ge(outs, i)
                a.activation(hidden[0:F, 0:BN // 2], ps_mix[0], ACT.Relu, bias=bias3[:, 0:1])
                a.activation(hidden[0:F, BN // 2:BN], ps_mix[1], ACT.Relu, bias=bias3[:, 0:1])\
                    .then_inc(bent, 1)
            a.wait_ge(step, 5 + 6)
            a.activation(s["root"][:, :], s["var"][:, :], ACT.Sqrt).then_inc(rooted, 1)
            a.wait_ge(step, 5 + LN_STEPS)
            with a.Fori(0, NBLK) as i:
                a.wait_ge(turned2, i)
                a.copy(h_rows[:, :, :], c.h[:, bass.ds(i * NB, NB), :]).then_inc(staged2, 1)
                a.wait_ge(turned2, i + 1)
                a.copy(turned_all[:, bass.ds(i * BN, 4 * P)], c.psQ[0:F, 0, :])
                a.copy(turned_all[:, bass.ds(i * BN + 4 * P, 3 * P)], c.psQ[0:F, 1, 0:3 * P])\
                    .then_inc(copied2, 1)
            a.wait_ge(step, 5 + LN_STEPS + NSC + 2)
            a.activation(bn["root"][:, :], bn["var"][:, :], ACT.Sqrt).then_inc(rooted_bn, 1)
            a.wait_ge(step, 5 + LN_STEPS + BATCH_STEPS)
            a.wait_ge(copied2, NBLK)
            with a.Fori(0, NBLK) as i:
                a.wait_ge(proj, i)
                a.activation(xn[0:F, :], turned_all[:, bass.ds(i * BN, BN)], ACT.Identity,
                             bias=bn["shift"][:, 0:1], scale=bn["scale"][:, 0:1]).then_inc(normed, 1)

        @block.tensor
        def _(pe):
            pe.wait_ge(weights, 16 * 12)
            pe.matmul(c.psP[0:F, 3, 0:1], w3u[:, :], u0[:, :], start=True, stop=True).then_inc(ubias, 1)
            pe.wait_ge(w_init, 3)
            with pe.Fori(0, NBLK) as i:
                pe.wait_ge(staged, i + 1)
                pe.wait_ge(copied, i)
                turn_block(pe, c, rows, 2 * F).then_inc(turned, 1)
                turned_in, ps_free = pe.to_reg(i + 1), pe.to_reg(i)
                pe.wait_ge(w_init, 3)
                pe.wait_ge(copied, turned_in)
                pe.wait_ge(bent, ps_free)
                for j in range(2):
                    mm = pe.matmul(ps_mix[j], w3[:, :], turned_sb[:, j * BN // 2:(j + 1) * BN // 2],
                                   start=True, stop=True)
                mm.then_inc(mixed, 1)
                pe.wait_ge(w_init, 3)
                pe.wait_ge(bent, turned_in)
                pe.wait_ge(added, ps_free)
                for t in range(NB):
                    mm = pe.matmul(ps_out[:, t * F:(t + 1) * F], hidden[:, t * P:(t + 1) * P], w4[:, :],
                                   start=True, stop=True)
                mm.then_inc(outs, 1)
            with pe.Fori(0, NBLK) as i:
                rows_in, ps_free = pe.to_reg(i + 1), pe.to_reg(i)
                pe.wait_ge(w_init, 3)
                pe.wait_ge(staged2, rows_in)
                pe.wait_ge(copied2, ps_free)
                turn_block(pe, c, h_rows).then_inc(turned2, 1)
            pe.wait_ge(step, 1)
            with pe.Fori(0, NBLK) as i:
                xn_in, ps_free = pe.to_reg(i + 1), pe.to_reg(i * 3)
                pe.wait_ge(w_init, 3)
                pe.wait_ge(normed, xn_in)
                pe.wait_ge(split, ps_free)
                for t in range(NB):
                    mm = pe.matmul(made[:, t, :], xn[:, t * P:(t + 1) * P], w[:, :], start=True, stop=True)
                mm.then_inc(proj, 1)
    clear(c, sems)


def edges2(c, W2, b2):
    nc = c.nc
    ctx, sb, sem, sems = stage(nc, "edges2")
    with ctx:
        idx = [sb(f"idx{k}", [P, ST], I32) for k in range(2)]
        flg = [sb(f"flg{k}", [P, SE], BF16) for k in range(2)]
        drow = [sb(f"drow{k}", [P, ST, 2 * F]) for k in range(2)]
        rows = [sb(f"rows{u}", [P, GT, 2 * F]) for u in range(UN)]
        carried = [sb(f"carried{r}", [P, GE]) for r in range(2)]
        pre = [sb(f"pre{r}", [P, GE]) for r in range(2)]
        act = [sb(f"act{r}", [P, GE]) for r in range(2)]
        msg = [sb(f"msg{r}", [F, GE]) for r in range(2)]
        scn = [sb(f"scn{r}", [F, GE]) for r in range(2)]
        outr = [sb(f"outr{k}", [P, ST, F]) for k in range(2)]
        w2 = sb("w2", [2 * F, F])
        b2_col = sb("b2_col", [F, 1])
        weights, first = sem("weights"), sem("first")
        loaded = [sem(f"loaded{k}") for k in range(2)]
        picked = sem("picked")
        gathered = c.gathered
        stored = [sem(f"stored{k}") for k in range(2)]
        d_turned, d_scanned, s_turned, summed, bent = (sem("d_turned"), sem("d_scanned"), sem("s_turned"),
                                                       sem("summed"), sem("bent"))
        mixed, biased, scanned, back, copied = (sem("mixed"), sem("biased"), sem("scanned"), sem("back"),
                                                sem("copied"))
        ps_d = [c.psP[:, 0, :], c.psP[:, 1, :]]
        ps_s = [c.psP[:, 2, :], c.psP[:, 3, :]]
        ps_m = [c.psQ[0:F, 0, :], c.psQ[0:F, 1, :]]
        ps_b = [c.psQ[:, 2, 0:GT * F], c.psQ[:, 3, 0:GT * F]]
        block = ctx.enter_context(nc.Block())

        @block.sync
        def _(sp):
            sp.dma_start(w2[:, :], W2).then_inc(weights, 16)
            sp.dma_start(b2_col[:, :], b2.unsqueeze(1)).then_inc(weights, 16)
            with sp.Fori(0, ITERS) as i:
                for k in range(2):
                    s = i * 2 + k
                    sp.wait_ge(scanned, i * 8 + 4 * k - 4 + LEAD)
                    sp.dma_start(flg[k][:, :], bcast(super_flags(c, s), [P, SE]))\
                        .then_inc(loaded[k], 16)
                    for half in range(2):
                        sp.dma_start(drow[k][:, half * ST // 2:(half + 1) * ST // 2, :],
                                     c.spread[bass.ds(s * SE + half * SE // 2, SE // 2), :]
                                     .rearrange("(t p) f -> p t f", p=P)).then_inc(loaded[k], 16)

        @block.gpsimd
        def _(g):
            with g.Fori(0, ITERS) as i:
                for u in range(UN):
                    k = u // SG
                    super_in, slot_free = g.to_reg(i * 2 + k + 1), g.to_reg(i * 8 + u + 1 - 8 + LEAD)
                    g.wait_ge(weights, 32)
                    g.wait_ge(picked, super_in)
                    g.wait_ge(s_turned, slot_free)
                    for t in range(GT):
                        col = (u % SG) * GT + t
                        g.indirect_dma_start(rows[u][:, t, :], None, c.table[:, :],
                                             bass.IndirectOffsetOnAxis(ap=idx[k][:, col:col + 1], axis=0))\
                            .then_inc(gathered[u], 16)

        @block.vector
        def _(v):
            for sm in (d_scanned, summed, scanned):
                v.sem_inc(sm, LEAD)
            v.memset(carried[1][:, :], 0.0).then_inc(first, 1)
            v.memset(scn[1][:, :], 0.0).then_inc(first, 1)
            v.wait_ge(first, 2)
            for k in range(2):
                pick(v, c, idx[k], slice(k * ST, (k + 1) * ST), picked)
            with v.Fori(0, ITERS) as i:
                def before_relu(u):
                    k, r, n = u // SG, u % 2, i * 8 + u + 1 + LEAD
                    v.wait_ge(loaded[k], i * 48 + 48)
                    v.wait_ge(d_turned, n)
                    v.wait_ge(d_scanned, n - 1)
                    v.tensor_tensor_scan(carried[r][:, :], flg[k][:, (u % SG) * GE:(u % SG + 1) * GE],
                                         ps_d[r], carried[1 - r][:, GE - 1:GE], ALU.mult, ALU.add)\
                        .then_inc(d_scanned, 1)
                    v.wait_ge(s_turned, n)
                    v.wait_ge(d_scanned, n)
                    v.wait_ge(bent, n - 2)
                    v.tensor_tensor(pre[r][:, :], ps_s[r], carried[r][:, :], ALU.add).then_inc(summed, 1)

                def running_max(u):
                    k, r, n = u // SG, u % 2, i * 8 + u + 1 + LEAD
                    v.wait_ge(biased, n)
                    v.wait_ge(back, n - 2)
                    v.wait_ge(scanned, n - 1)
                    v.tensor_tensor_scan(scn[r][:, :], flg[k][0:F, (u % SG) * GE:(u % SG + 1) * GE],
                                         msg[r][:, :], scn[1 - r][:, GE - 1:GE], ALU.mult, ALU.max)\
                        .then_inc(scanned, 1)
                    if u % SG == SG - 1:
                        v.wait_ge(gathered[u], i * 64 + 64)
                        pick(v, c, idx[k], bass.ds((i * 2 + k + 2) * ST, ST), picked)

                before_relu(0)
                for u in range(UN):
                    if u + 1 < UN:
                        before_relu(u + 1)
                    running_max(u)

        @block.tensor
        def _(pe):
            for sm in (d_turned, s_turned, mixed, back):
                pe.sem_inc(sm, LEAD)
            pe.wait_ge(weights, 32)
            with pe.Fori(0, ITERS) as i:
                def turn_in(u):
                    k, r, n = u // SG, u % 2, i * 8 + u + 1 + LEAD
                    pe.wait_ge(loaded[k], i * 48 + 48)
                    pe.wait_ge(d_scanned, n - 2)
                    for t in range(GT):
                        mm = pe.transpose(ps_d[r][:, t * P:(t + 1) * P], drow[k][:, (u % SG) * GT + t, :],
                                          c.ident[:, :])
                    mm.then_inc(d_turned, 1)
                    pe.wait_ge(gathered[u], i * 64 + 64)
                    pe.wait_ge(summed, n - 2)
                    for t in range(GT):
                        mm = pe.transpose(ps_s[r][:, t * P:(t + 1) * P], rows[u][:, t, :], c.ident[:, :])
                    mm.then_inc(s_turned, 1)

                def turn_out(u):
                    r, n = u % 2, i * 8 + u + 1 + LEAD
                    scan_in, ps_free = pe.to_reg(n), pe.to_reg(n - 2)
                    pe.wait_ge(weights, 32)
                    pe.wait_ge(scanned, scan_in)
                    pe.wait_ge(copied, ps_free)
                    for t in range(GT):
                        mm = pe.transpose(ps_b[r][:, t * F:(t + 1) * F], scn[r][:, t * P:(t + 1) * P],
                                          c.ident[0:F, 0:F])
                    mm.then_inc(back, 1)

                turn_in(0)
                for u in range(UN):
                    r, n = u % 2, i * 8 + u + 1 + LEAD
                    if u + 1 < UN:
                        turn_in(u + 1)
                    pe.wait_ge(bent, n)
                    pe.wait_ge(biased, n - 2)
                    pe.matmul(ps_m[r], w2[:, :], act[r][:, :], start=True, stop=True).then_inc(mixed, 1)
                    if u > 0:
                        turn_out(u - 1)
                turn_out(UN - 1)

        @block.scalar
        def _(a):
            for sm in (bent, biased, copied):
                a.sem_inc(sm, LEAD)
            a.wait_ge(weights, 32)
            with a.Fori(0, ITERS) as i:
                def evacuate(u):
                    k, r, n = u // SG, u % 2, i * 8 + u + 1 + LEAD
                    if u % SG == 0:
                        a.wait_ge(stored[k], i * 16)
                    a.wait_ge(back, n)
                    a.copy(outr[k][:, (u % SG) * GT:(u % SG + 1) * GT, :].rearrange("p t f -> p (t f)"),
                           ps_b[r]).then_inc(copied, 1)
                    if u % SG == SG - 1:
                        a.wait_ge(copied, n)
                        a.dma_start(c.scans[bass.ds((i * 2 + k) * SE, SE), :]
                                    .rearrange("(t p) f -> p t f", p=P), outr[k][:, :, :])\
                            .then_inc(stored[k], 16)

                for u in range(UN):
                    r, n = u % 2, i * 8 + u + 1 + LEAD
                    a.wait_ge(summed, n)
                    a.wait_ge(mixed, n - 2)
                    a.activation(act[r][:, :], pre[r][:, :], ACT.Relu).then_inc(bent, 1)
                    a.wait_ge(mixed, n)
                    a.wait_ge(scanned, n - 2)
                    a.activation(msg[r][:, :], ps_m[r], ACT.Identity, bias=b2_col[:, 0:1])\
                        .then_inc(biased, 1)
                    if u > 0:
                        evacuate(u - 1)
                evacuate(UN - 1)
            for k in range(2):
                a.wait_ge(stored[k], 16 * ITERS)
    clear(c, sems)


def nodes3(c):
    nc = c.nc
    ctx, sb, sem, sems = stage(nc, "nodes3")
    with ctx:
        s = layernorm_buffers(sb)
        ends, step, rooted, stored, ready = (c.ends_in, sem("step"), sem("rooted"), sem("stored"),
                                             sem("ready"))
        block = ctx.enter_context(nc.Block())

        @block.gpsimd
        def _(g):
            gather_ends(g, c, ready, ends)
            g.wait_ge(ends, 16 * NT)

        @block.vector
        def _(v):
            v.wait_ge(ends, 16 * NT)
            v.tensor_tensor(c.x[:, :, :], c.x[:, :, :], c.ends[:, :, :], ALU.add).then_inc(step, 1)
            layernorm_relu(v, c, s, step, 1, rooted)

        @block.scalar
        def _(a):
            a.wait_ge(step, 1 + 6)
            a.activation(s["root"][:, :], s["var"][:, :], ACT.Sqrt).then_inc(rooted, 1)

        @block.sync
        def _(sp):
            sp.wait_ge(step, 1 + LN_STEPS)
            sp.dma_start(c.table3.rearrange("(t p) f -> p t f", p=P), c.h[:, :, :]).then_inc(stored, 16)
            sp.wait_ge(stored, 16)
    clear(c, sems)


def edges3(c, ew_cols):
    nc = c.nc
    ctx, sb, sem, sems = stage(nc, "edges3")
    with ctx:
        idx = [sb(f"idx{k}", [P, ST], I32) for k in range(2)]
        ew = [sb(f"ew{k}", [P, ST]) for k in range(2)]
        flg = [sb(f"flg{k}", [F, SE], BF16) for k in range(2)]
        rows = [sb(f"rows{u}", [P, GT, F]) for u in range(UN)]
        scaled_rows = [sb(f"scaled_rows{r}", [P, GT, F]) for r in range(2)]
        scn = [sb(f"scn{r}", [F, GE]) for r in range(2)]
        outr = [sb(f"outr{k}", [P, ST, F]) for k in range(2)]
        loaded = [sem(f"loaded{k}") for k in range(2)]
        picked = sem("picked")
        gathered = c.gathered
        stored = [sem(f"stored{k}") for k in range(2)]
        first, scaled, turned, scanned, back, copied = (sem("first"), sem("scaled"), sem("turned"),
                                                        sem("scanned"), sem("back"), sem("copied"))
        ps_t = [c.psP[0:F, 0, :], c.psP[0:F, 1, :]]
        ps_b = [c.psQ[:, 0, 0:GT * F], c.psQ[:, 1, 0:GT * F]]
        block = ctx.enter_context(nc.Block())

        @block.sync
        def _(sp):
            with sp.Fori(0, ITERS) as i:
                for k in range(2):
                    s = i * 2 + k
                    sp.wait_ge(scanned, i * 8 + 4 * k - 4 + LEAD)
                    sp.dma_start(ew[k][:, :], ew_cols[:, bass.ds(s * ST, ST)]).then_inc(loaded[k], 16)
                    sp.dma_start(flg[k][:, :], bcast(super_flags(c, s), [F, SE]))\
                        .then_inc(loaded[k], 16)

        @block.gpsimd
        def _(g):
            with g.Fori(0, ITERS) as i:
                for u in range(UN):
                    k = u // SG
                    super_in, slot_free = g.to_reg(i * 2 + k + 1), g.to_reg(i * 8 + u + 1 - 8 + LEAD)
                    g.wait_ge(first, 1)
                    g.wait_ge(picked, super_in)
                    g.wait_ge(scaled, slot_free)
                    for t in range(GT):
                        col = (u % SG) * GT + t
                        g.indirect_dma_start(rows[u][:, t, :], None, c.table3[:, :],
                                             bass.IndirectOffsetOnAxis(ap=idx[k][:, col:col + 1], axis=0))\
                            .then_inc(gathered[u], 16)

        @block.vector
        def _(v):
            v.sem_inc(scaled, LEAD)
            v.sem_inc(scanned, LEAD)
            v.memset(scn[1][:, :], 0.0).then_inc(first, 1)
            v.wait_ge(first, 1)
            for k in range(2):
                pick(v, c, idx[k], slice(k * ST, (k + 1) * ST), picked)
            with v.Fori(0, ITERS) as i:
                for u in range(UN):
                    k, r, n = u // SG, u % 2, i * 8 + u + 1 + LEAD
                    v.wait_ge(loaded[k], i * 32 + 32)
                    v.wait_ge(gathered[u], i * 64 + 64)
                    v.wait_ge(turned, n - 2)
                    v.tensor_tensor(scaled_rows[r][:, :, :], rows[u][:, :, :],
                                    bcast(ew[k][:, (u % SG) * GT:(u % SG + 1) * GT].unsqueeze(2),
                                          [P, GT, F]), ALU.mult).then_inc(scaled, 1)
                    v.wait_ge(turned, n)
                    v.wait_ge(back, n - 2)
                    v.wait_ge(scanned, n - 1)
                    v.tensor_tensor_scan(scn[r][:, :], flg[k][:, (u % SG) * GE:(u % SG + 1) * GE],
                                         ps_t[r], scn[1 - r][:, GE - 1:GE], ALU.mult, ALU.add)\
                        .then_inc(scanned, 1)
                    if u % SG == SG - 1:
                        v.wait_ge(gathered[u], i * 64 + 64)
                        pick(v, c, idx[k], bass.ds((i * 2 + k + 2) * ST, ST), picked)

        @block.tensor
        def _(pe):
            pe.sem_inc(turned, LEAD)
            pe.sem_inc(back, LEAD)
            with pe.Fori(0, ITERS) as i:
                for u in range(UN):
                    r, n = u % 2, i * 8 + u + 1 + LEAD
                    now, ps_free = pe.to_reg(n), pe.to_reg(n - 2)
                    pe.wait_ge(first, 1)
                    pe.wait_ge(scaled, now)
                    pe.wait_ge(scanned, ps_free)
                    for t in range(GT):
                        mm = pe.transpose(ps_t[r][:, t * P:(t + 1) * P], scaled_rows[r][:, t, :], c.ident[:, :])
                    mm.then_inc(turned, 1)
                    pe.wait_ge(first, 1)
                    pe.wait_ge(scanned, now)
                    pe.wait_ge(copied, ps_free)
                    for t in range(GT):
                        mm = pe.transpose(ps_b[r][:, t * F:(t + 1) * F], scn[r][:, t * P:(t + 1) * P],
                                          c.ident[0:F, 0:F])
                    mm.then_inc(back, 1)

        @block.scalar
        def _(a):
            a.sem_inc(copied, LEAD)
            with a.Fori(0, ITERS) as i:
                for u in range(UN):
                    k, r, n = u // SG, u % 2, i * 8 + u + 1 + LEAD
                    if u % SG == 0:
                        a.wait_ge(stored[k], i * 16)
                    a.wait_ge(back, n)
                    a.copy(outr[k][:, (u % SG) * GT:(u % SG + 1) * GT, :].rearrange("p t f -> p (t f)"),
                           ps_b[r]).then_inc(copied, 1)
                    if u % SG == SG - 1:
                        a.wait_ge(copied, n)
                        a.dma_start(c.scans[bass.ds((i * 2 + k) * SE, SE), :]
                                    .rearrange("(t p) f -> p t f", p=P), outr[k][:, :, :])\
                            .then_inc(stored[k], 16)
            for k in range(2):
                a.wait_ge(stored[k], 16 * ITERS)
    clear(c, sems)


def layer_nodes(c, layer, W1, b1, gamma, beta, W2, b2):
    nc = c.nc
    ctx, sb, sem, sems = stage(nc, "layer_nodes")
    with ctx:
        bn = batch_buffers(sb)
        w1 = sb("w1", [F, F])
        b1_col = sb("b1_col", [F, 1])
        w2 = sb("w2", [F + 1, F])
        gam = sb("gam", [F, 1])
        bet = sb("bet", [F, 1])
        rows = sb("rows", [P, NB, F])
        turned_sb = sb("turned_sb", [F, BN])
        mid = sb("mid", [F, NP])
        hidden = sb("hidden", [F + 1, BN])
        weights, one, ends, step, rooted = (sem("weights"), sem("one"), c.ends_in, sem("step"),
                                            sem("rooted"))
        staged, turned, copied, mixed, biased = (sem("staged"), sem("turned"), sem("copied"), sem("mixed"),
                                                 sem("biased"))
        bent, outs, h_new, stored = sem("bent"), sem("outs"), sem("h_new"), sem("stored")
        ps_mix = [c.psQ[0:F, 2, 0:BN // 2], c.psQ[0:F, 3, 0:BN // 2]]
        ps_out = c.psP[:, 0, 0:NB * F]
        block = ctx.enter_context(nc.Block())

        @block.sync
        def _(sp):
            for dst, m in ((w1[:, :], W1[bass.ds(layer, 1)].rearrange("a k n -> (a k) n")),
                           (b1_col[:, :], b1[bass.ds(layer, 1)].rearrange("a n -> n a")),
                           (w2[0:F, :], W2[bass.ds(layer, 1)].rearrange("a k n -> (a k) n")),
                           (w2[F:F + 1, :], b2[bass.ds(layer, 1)]),
                           (gam[:, :], gamma[bass.ds(layer, 1)].rearrange("a n -> n a")),
                           (bet[:, :], beta[bass.ds(layer, 1)].rearrange("a n -> n a"))):
                sp.dma_start(dst, m).then_inc(weights, 16)
            sp.wait_ge(h_new, NBLK)
            sp.dma_start(c.table3.rearrange("(t p) f -> p t f", p=P), c.h[:, :, :]).then_inc(stored, 16)
            sp.wait_ge(stored, 16)

        @block.gpsimd
        def _(g):
            g.memset(hidden[F:F + 1, :], 1.0).then_inc(one, 1)
            gather_ends(g, c, one, ends)
            g.wait_ge(ends, 16 * NT)

        @block.vector
        def _(v):
            v.wait_ge(ends, 16 * NT)
            v.tensor_tensor(c.h[:, :, :], c.h[:, :, :], c.ends[:, :, :], ALU.add).then_inc(step, 1)
            v.wait_ge(biased, NBLK)
            v.wait_ge(weights, 16 * 6)
            batch_scale(v, bn, mid, gam, bet, step, 1, rooted)
            with v.Fori(0, NBLK) as i:
                v.wait_ge(outs, i + 1)
                v.tensor_scalar(c.h[:, bass.ds(i * NB, NB), :], ps_out.rearrange("p (t f) -> p t f", t=NB),
                                0.0, None, ALU.max).then_inc(h_new, 1)

        @block.scalar
        def _(a):
            a.wait_ge(step, 1)
            a.wait_ge(weights, 16 * 6)
            with a.Fori(0, NBLK) as i:
                a.wait_ge(turned, i)
                a.copy(rows[:, :, :], c.h[:, bass.ds(i * NB, NB), :]).then_inc(staged, 1)
                a.wait_ge(turned, i + 1)
                a.wait_ge(mixed, i)
                copy_turned(a, c, turned_sb).then_inc(copied, 1)
                a.wait_ge(mixed, i + 1)
                for j in range(2):
                    act = a.activation(mid[:, bass.ds(i * BN + j * SC, SC)], ps_mix[j], ACT.Identity,
                                       bias=b1_col[:, 0:1])
                act.then_inc(biased, 1)
            a.wait_ge(step, 1 + NSC + 2)
            a.activation(bn["root"][:, :], bn["var"][:, :], ACT.Sqrt).then_inc(rooted, 1)
            a.wait_ge(step, 1 + BATCH_STEPS)
            a.wait_ge(biased, NBLK)
            with a.Fori(0, NBLK) as i:
                a.wait_ge(outs, i)
                a.activation(hidden[0:F, :], mid[:, bass.ds(i * BN, BN)], ACT.Relu,
                             bias=bn["shift"][:, 0:1], scale=bn["scale"][:, 0:1]).then_inc(bent, 1)

        @block.tensor
        def _(pe):
            pe.wait_ge(weights, 16 * 6)
            pe.wait_ge(one, 1)
            with pe.Fori(0, NBLK) as i:
                now, ps_free = pe.to_reg(i + 1), pe.to_reg(i)
                pe.wait_ge(one, 1)
                pe.wait_ge(staged, now)
                pe.wait_ge(copied, ps_free)
                turn_block(pe, c, rows).then_inc(turned, 1)
                pe.wait_ge(one, 1)
                pe.wait_ge(copied, now)
                pe.wait_ge(biased, ps_free)
                for j in range(2):
                    mm = pe.matmul(ps_mix[j], w1[:, :], turned_sb[:, j * SC:(j + 1) * SC],
                                   start=True, stop=True)
                mm.then_inc(mixed, 1)
            with pe.Fori(0, NBLK) as i:
                now, ps_free = pe.to_reg(i + 1), pe.to_reg(i)
                pe.wait_ge(one, 1)
                pe.wait_ge(bent, now)
                pe.wait_ge(h_new, ps_free)
                for t in range(NB):
                    mm = pe.matmul(ps_out[:, t * F:(t + 1) * F], hidden[:, t * P:(t + 1) * P], w2[:, :],
                                   start=True, stop=True)
                mm.then_inc(outs, 1)
    clear(c, sems)


def finish(c, out):
    nc = c.nc
    full = NODES // P
    rest = NODES - full * P
    with ExitStack() as ctx:
        summed = ctx.enter_context(nc.semaphore("summed_out"))
        stored = ctx.enter_context(nc.semaphore("stored_out"))
        block = ctx.enter_context(nc.Block())

        @block.vector
        def _(v):
            v.tensor_tensor(c.x[:, :, :], c.x[:, :, :], c.h[:, :, :], ALU.add).then_inc(summed, 1)

        @block.sync
        def _(sp):
            sp.wait_ge(summed, 1)
            sp.dma_start(out[0:full * P, :].rearrange("(t p) f -> p t f", p=P), c.x[:, 0:full, :])\
                .then_inc(stored, 16)
            sp.dma_start(out[full * P:NODES, :], c.x[0:rest, full, :]).then_inc(stored, 16)
            sp.wait_ge(stored, 32)


def build(nc, ins, out):
    with ExitStack() as ctx:
        c = Core(nc, ctx)
        w0, w1, w2, w3 = ({k[7:]: v for k, v in ins.items() if k.startswith(f"L{n}_gnn_")} for n in range(4))
        src_cols, ew_cols = ins["src_cols"], ins["ew_cols"]
        prepare(c, ins["x"], src_cols, ins["dst_cols"], ew_cols, ins["dst_seq"], ins["dst_prev"])
        nodes0(c, w0["W_l1"], w0["b_l1"], w0["W_s2d"], w0["b_s2d"], w0["W_d2s"], w0["b_d2s"])
        edges0(c, ins["src_rows"], w0["W_l2"], w0["b_l2"])
        nodes1(c, w0["W_g1"], w0["b_g1"], w0["W_g2"], w0["b_g2"], w1["W1"], w1["b1"])
        edges1(c, ins["attr_g"], w1["W1"], w1["W2"])
        nodes2(c, w1["u"], w1["b2"], w1["W3"], w1["b3"], w1["W4"], w1["b4"], w2["gamma"], w2["beta"],
               w2["W1"], w2["b1"])
        edges2(c, w2["W2"], w2["b2"])
        nodes3(c)
        with nc.Fori(0, LAYERS) as layer:
            edges3(c, ins["ew1_cols"])
            layer_nodes(c, layer, w3["W1"], w3["b1"], w3["gamma"], w3["beta"], w3["W2"], w3["b2"])
        finish(c, out)


def arrays(**inputs):
    import numpy as np

    a = {k: np.ascontiguousarray(v) for k, v in inputs.items()}

    def padded(v, fill):
        out = np.full((EP,) + v.shape[1:], fill, v.dtype)
        out[:EDGES] = v
        return out

    def cols(v):
        return np.ascontiguousarray(v.reshape(EC, P).T)

    src, dst = padded(a.pop("src"), 0), padded(a.pop("dst"), NODES)
    x = np.zeros((NP, F), a["x"].dtype)
    x[:NODES] = a.pop("x")
    prev = np.full(EP, -1, dst.dtype)
    prev[1:] = dst[:-1]
    return dict(
        x=x, src_cols=cols(src), dst_cols=cols(dst), src_rows=src.reshape(SUPERS * SG, GE),
        dst_seq=dst.reshape(P, EC), dst_prev=prev.reshape(P, EC),
        ew_cols=cols(padded(a.pop("edge_weight"), 0)),
        ew1_cols=cols(padded(a.pop("edge_weight1")[:, 0], 0)),
        attr_g=np.ascontiguousarray(padded(a.pop("edge_attr_32"), 0).reshape(SUPERS, SG, GE, P // SG)
                                    .transpose(0, 1, 3, 2)).reshape(SUPERS * P, GE), **a)


def kernel(**inputs):
    import concourse.bacc as _bacc
    from concourse.bass_utils import run_bass_kernel_spmd as _run

    nc = _bacc.Bacc("TRN2", target_bir_lowering=False, num_devices=1)
    laid_out = arrays(**inputs)
    ins = {k: nc.dram_tensor(f"in_{k}", v.shape, mybir.dt.from_np(v.dtype), kind="ExternalInput").ap()
           for k, v in laid_out.items()}
    out = nc.dram_tensor("out", (NODES, F), F32, kind="ExternalOutput").ap()
    build(nc, ins, out)
    r = _run(nc, [{f"in_{k}": v for k, v in laid_out.items()}], core_ids=[0])
    return r.results[0]["out"]
```

```python
from contextlib import ExitStack

import concourse.bass as bass
from concourse import mybir

F32 = mybir.dt.float32
I32 = mybir.dt.int32
BF16 = mybir.dt.bfloat16
ALU = mybir.AluOpType
ACT = mybir.ActivationFunctionType
AX = mybir.AxisListType.X

P = 128
NODES, EDGES, F = 6250, 200000, 64
NT = -(-NODES // P)
NP = NT * P
NB = 7
NBLK = NT // NB
BN = NB * P
GT = 4
GE = GT * P
SG = 4
ST = SG * GT
SE = ST * P
SUPERS = -(-EDGES // SE)
EP = SUPERS * SE
ITERS = SUPERS // 2
UN = 2 * SG
EC = EP // P
LEAD = 8
LN_EPS = 1e-5
BN_EPS = 1e-5
LAYERS = 3
PARTS = 3
FE = P // SG
ACCS = GT
assert NT % NB == 0 and SUPERS % 2 == 0


def bcast(ap, shape):
    return ap.to_broadcast(shape)


def node_rows(table, i):
    return table[bass.ds(i * BN, BN), :].rearrange("(t p) f -> p t f", p=P)


def super_flags(c, s):
    return c.flags.rearrange("(s g) e -> s (g e)", g=SG)[bass.ds(s, 1), :]


class Core:

    def __init__(self, nc, ctx):
        self.nc = nc

        def sb(name, shape, dt=F32):
            return ctx.enter_context(nc.sbuf_tensor(name, shape, dt))

        def dram(name, shape, dt=F32):
            return nc.dram_tensor(name, shape, dt, kind="Internal").ap()

        self.x = sb("x", [P, NT, F])
        self.h = sb("h", [P, NT, F])
        self.ends = sb("ends", [P, NT, F])
        self.ident = sb("ident", [P, P])
        self.before = sb("before", [P, P])
        self.after = sb("after", [P, P])
        self.src = sb("src", [P, EC + 2 * ST], I32)
        self.ew = sb("ew", [P, EC])
        self.ew1 = sb("ew1", [P, EC])
        self.first = sb("first", [P, NT])
        self.unsorted = sb("unsorted", [1, 1], I32)
        self.trash = sb("trash", [P, 1])
        self.start_idx = sb("start_idx", [P, NT], I32)
        self.end_idx = sb("end_idx", [P, NT], I32)
        self.cnt_inv = sb("cnt_inv", [P, NT])
        self.has_in = sb("has_in", [P, NT])
        self.rs_in = sb("rs_in", [P, NT])
        self.rs_out = sb("rs_out", [P, NT])
        self.psP = ctx.enter_context(nc.psum_tensor("psP", [P, 4, 512], F32))
        self.psQ = ctx.enter_context(nc.psum_tensor("psQ", [P, 4, 512], F32))
        self.gathered = [ctx.enter_context(nc.semaphore(f"gathered{u}")) for u in range(UN)]
        self.added = [ctx.enter_context(nc.semaphore(f"added{t}")) for t in range(ACCS)]
        self.spread_in = ctx.enter_context(nc.semaphore("spread_in"))
        nums = [s.num for s in (*self.gathered, *self.added, self.spread_in)]
        self.pool_sems = range(min(nums), max(nums) + 1)
        assert len(self.pool_sems) == len(nums)
        self.flags = dram("flags", [SUPERS * SG, GE], BF16)
        self.src_rows = dram("src_rows", [SUPERS * SG, GE], I32)
        self.attr_g = dram("attr_g", [SUPERS * P, GE])
        self.by_dst = dram("by_dst", [1 + EP, FE + 4])
        self.table = dram("node_table", [NP, 2 * F])
        self.table3 = dram("node_table3", [NP, F])
        self.spread = dram("spread", [EP + P, 2 * F])
        self.scans = dram("scans", [EP + P, F])
        self.acc = [dram(f"acc{k}", [NP + P, F]) for k in range(ACCS)]


def clear(c, sems):
    with c.nc.Block() as block:
        @block.sync
        def _(sp):
            for s in sems:
                sp.sem_clear(s)

        @block.gpsimd
        def _(g):
            g.dma_reset(c.pool_sems)
            g.sem_clear(c.pool_sems)


def stage(nc, tag):
    ctx = ExitStack()
    sems = []

    def sb(name, shape, dt=F32):
        return ctx.enter_context(nc.sbuf_tensor(f"{tag}_{name}", shape, dt))

    def sem(name):
        sems.append(ctx.enter_context(nc.semaphore(name)))
        return sems[-1]

    return ctx, sb, sem, sems


def prepare(c, x_in, src_cols, dst_cols, ew_cols, ew1_cols, dst_seq, dst_prev, src_rows, attr_g):
    nc = c.nc
    ctx, sb, sem, sems = stage(nc, "prepare")
    with ctx:
        dst_i = sb("dst_i", [P, EC], I32)
        part_i = sb("part_i", [P, EC], I32)
        lo = [sb(f"lo{k}", [P, EC], BF16) for k in range(2)]
        hi = [sb(f"hi{k}", [P, EC], BF16) for k in range(2)]
        parts = sb("parts", [P, PARTS, EC], BF16)
        left = [sb(f"left{j}", [P, EC]) for j in range(PARTS - 1)]
        columns = sb("columns", [P, P, ST], BF16)
        seq = sb("seq", [P, EC], I32)
        prev = sb("prev", [P, EC], I32)
        flg = sb("flg", [P, EC], BF16)
        fall = sb("fall", [P, EC], BF16)
        fall_sum = sb("fall_sum", [P, 1])
        iota_i = sb("iota_i", [P, P], I32)
        trash_i = sb("trash_i", [P, 1], I32)
        zeros = sb("zeros", [P, 2048])
        ones = sb("ones", [P, P])
        oh = [[sb(f"oh{w}{k}", [P, P, ST], BF16) for k in range(2)] for w in range(2)]
        hot = [[sb(f"hot{w}{k}", [P, 1 + PARTS, NT, ST], BF16) for k in range(2)] for w in range(2)]
        cnt = sb("cnt", [P, NT])
        deg = sb("deg", [P, 2, NT])
        t0 = sb("t0", [P, NT])
        t1 = sb("t1", [P, NT])
        t2 = sb("t2", [P, NT])
        t3 = sb("t3", [P, NT])
        far = sb("far", [P, 1])

        loaded, seqs, made, split = sem("loaded"), sem("seqs"), sem("made"), sem("split")
        cut, added, copied = sem("cut"), sem("added_up"), sem("copied")
        falls, judged = sem("falls"), sem("judged")
        cleared, flagged, flags_out = sem("cleared"), sem("flagged"), sem("flags_out")
        oh_made, binned, step, sums, rooted = (sem("oh_made"), sem("binned"), sem("step"),
                                               sem("sums"), sem("rooted"))
        zeroed = sem("zeroed")

        out_bins = c.psQ[:, 0, 0:PARTS * NT]
        in_bins = c.psQ[:, 1, 0:(1 + PARTS) * NT]
        within = c.psQ[:, 2, 0:NT]
        totals = c.psQ[:, 3, 0:NT]
        all_falls = c.psP[0:1, 0, 0:1]

        block = ctx.enter_context(nc.Block())

        @block.sync
        def _(sp):
            sp.dma_start(c.src[:, 0:EC], src_cols).then_inc(loaded, 16)
            sp.dma_start(dst_i[:, :], dst_cols).then_inc(loaded, 16)
            sp.dma_start(c.ew[:, :], ew_cols).then_inc(loaded, 16)
            sp.dma_start(c.x[:, :, :], x_in.rearrange("(t p) f -> p t f", p=P)).then_inc(loaded, 16)
            sp.dma_start(seq[:, :], dst_seq).then_inc(seqs, 16)
            sp.dma_start(prev[:, :], dst_prev).then_inc(seqs, 16)
            sp.wait_ge(flagged, 1)
            sp.dma_start(c.flags.rearrange("s e -> (s e)").rearrange("(p c) -> p c", p=P),
                         flg[:, :]).then_inc(flags_out, 16)
            sp.dma_start(c.ew1[:, :], ew1_cols).then_inc(copied, 16)
            sp.dma_start(c.src_rows, src_rows).then_inc(copied, 16)
            sp.wait_ge(cleared, 1)
            sp.dma_start(c.scans[EP:EP + P, :], zeros[:, 0:F]).then_inc(zeroed, 16)
            for a in c.acc:
                sp.dma_start(a[0:NP, :].rearrange("(p t) f -> p (t f)", p=P)[:, 0:2048],
                             zeros[:, :]).then_inc(zeroed, 16)
                sp.dma_start(a[0:NP, :].rearrange("(p t) f -> p (t f)", p=P)[:, 2048:NT * F],
                             zeros[:, 0:NT * F - 2048]).then_inc(zeroed, 16)
                sp.dma_start(a[NP:NP + P, :], zeros[:, 0:F]).then_inc(zeroed, 16)
            with sp.Fori(0, SUPERS) as s:
                sp.dma_start(c.attr_g[bass.ds(s * P, P), :], attr_g[bass.ds(s * P, P), :])\
                    .then_inc(copied, 16)
                sp.dma_start(c.spread[bass.ds(s * SE, SE), :].rearrange("(p t) f -> p (t f)", p=P),
                             zeros[:, :]).then_inc(zeroed, 16)
            sp.wait_ge(flags_out, 16)
            sp.wait_ge(zeroed, 16 * (1 + 3 * ACCS + SUPERS))
            sp.wait_ge(copied, 16 * (2 + SUPERS))

        @block.gpsimd
        def _(g):
            g.memset(c.ident[:, :], 0.0).then_inc(made, 1)
            g.memset(c.before[:, :], 1.0).then_inc(made, 1)
            g.memset(c.after[:, :], 1.0).then_inc(made, 1)
            g.memset(ones[:, :], 1.0).then_inc(made, 1)
            g.iota(iota_i[:, :], pattern=[[1, P]], base=0, channel_multiplier=0).then_inc(made, 1)
            g.iota(trash_i[:, :], pattern=[[1, 1]], base=NP, channel_multiplier=1).then_inc(made, 1)
            g.wait_ge(made, 6)
            g.affine_select(out=c.ident[:, :], in_=c.ident[:, :], compare_op=ALU.not_equal, fill=1.0,
                            base=0, pattern=[[-1, P]], channel_multiplier=1).then_inc(made, 1)
            g.affine_select(out=c.before[:, :], in_=c.before[:, :], compare_op=ALU.is_gt, fill=0.0,
                            base=0, pattern=[[1, P]], channel_multiplier=-1).then_inc(made, 1)
            g.affine_select(out=c.after[:, :], in_=c.after[:, :], compare_op=ALU.is_gt, fill=0.0,
                            base=0, pattern=[[-1, P]], channel_multiplier=1).then_inc(made, 1)

        @block.scalar
        def _(a):
            a.wait_ge(step, 3)
            a.activation(deg[:, :, :], deg[:, :, :], ACT.Sqrt).then_inc(rooted, 1)

        @block.vector
        def _(v):
            v.memset(zeros[:, :], 0.0).then_inc(cleared, 1)
            v.memset(c.src[:, EC:EC + 2 * ST], 0)
            v.wait_ge(made, 9)
            v.tensor_copy(columns[:, :, :], bcast(iota_i[:, :].unsqueeze(2), [P, P, ST])).then_inc(split, 1)
            v.tensor_copy(c.trash[:, :], trash_i[:, :]).then_inc(split, 1)
            v.wait_ge(loaded, 64)
            for k, idx in enumerate((c.src[:, 0:EC], dst_i[:, :])):
                v.wait_ge(split, 2 + 4 * k)
                v.tensor_scalar(part_i[:, :], idx, P - 1, None, ALU.bitwise_and).then_inc(split, 1)
                v.wait_ge(split, 3 + 4 * k)
                v.tensor_copy(lo[k][:, :], part_i[:, :]).then_inc(split, 1)
                v.wait_ge(split, 4 + 4 * k)
                v.tensor_scalar(part_i[:, :], idx, 7, None, ALU.logical_shift_right).then_inc(split, 1)
                v.wait_ge(split, 5 + 4 * k)
                v.tensor_copy(hi[k][:, :], part_i[:, :]).then_inc(split, 1)
            v.wait_ge(seqs, 32)
            v.tensor_tensor(flg[:, :], seq[:, :], prev[:, :], ALU.is_equal).then_inc(flagged, 1)
            v.tensor_tensor(fall[:, :], prev[:, :], seq[:, :], ALU.is_gt).then_inc(falls, 1)
            v.wait_ge(falls, 1)
            v.tensor_reduce(fall_sum[:, :], fall[:, :], AX, ALU.add).then_inc(falls, 1)
            v.wait_ge(split, 10)
            v.tensor_scalar(far[:, :], c.trash[:, :], float(EP - NP), None, ALU.add).then_inc(split, 1)
            v.tensor_copy(parts[:, 0, :], c.ew[:, :]).then_inc(cut, 1)
            for j in range(PARTS - 1):
                rest = c.ew if j == 0 else left[j - 1]
                v.wait_ge(cut, 2 * j + 1)
                v.tensor_tensor(left[j][:, :], rest[:, :], parts[:, j, :], ALU.subtract).then_inc(cut, 1)
                v.wait_ge(cut, 2 * j + 2)
                v.tensor_copy(parts[:, j + 1, :], left[j][:, :]).then_inc(cut, 1)
            v.wait_ge(cut, 2 * PARTS - 1)
            v.wait_ge(split, 11)
            v.sem_inc(oh_made, LEAD)
            with v.Fori(0, ITERS) as i:
                for k in range(2):
                    cols = bass.ds((i * 2 + k) * ST, ST)
                    v.wait_ge(binned, i * 2 + k - 1 + LEAD)
                    for w in range(2):
                        v.tensor_tensor(hot[w][k][:, 0, :, :], columns[:, 0:NT, :],
                                        bcast(hi[w][:, cols].unsqueeze(1), [P, NT, ST]),
                                        ALU.is_equal).then_inc(oh_made, 1)
                    for w in range(2):
                        v.tensor_tensor(oh[w][k][:, :, :], columns[:, :, :],
                                        bcast(lo[w][:, cols].unsqueeze(1), [P, P, ST]),
                                        ALU.is_equal).then_inc(oh_made, 1)
                    for w in range(2):
                        v.wait_ge(oh_made, i * 12 + 6 * k + 1 + w + LEAD)
                        v.tensor_tensor(hot[w][k][:, 1:1 + PARTS, :, :],
                                        bcast(hot[w][k][:, 0:1, :, :], [P, PARTS, NT, ST]),
                                        bcast(parts[:, :, cols].unsqueeze(2), [P, PARTS, NT, ST]),
                                        ALU.mult).then_inc(oh_made, 1)
            v.wait_ge(binned, SUPERS + 1 + LEAD)
            v.tensor_copy(cnt[:, :], in_bins[:, 0:NT]).then_inc(step, 1)
            for w, (bins, at) in enumerate(((in_bins, 1), (out_bins, 0))):
                v.tensor_reduce(deg[:, w, :], bins[:, at * NT:(at + PARTS) * NT]
                                .rearrange("p (j n) -> p n j", j=PARTS), AX, ALU.add).then_inc(added, 1)
            v.wait_ge(added, 2)
            v.tensor_scalar(deg[:, :, :], deg[:, :, :], 1.0, None, ALU.max).then_inc(step, 2)
            v.wait_ge(step, 3)
            v.tensor_scalar(t0[:, :], cnt[:, :], 1.0, None, ALU.max).then_inc(step, 1)
            v.wait_ge(step, 4)
            v.reciprocal(c.cnt_inv[:, :], t0[:, :]).then_inc(step, 1)
            v.wait_ge(step, 5)
            v.tensor_tensor(c.has_in[:, :], cnt[:, :], c.cnt_inv[:, :], ALU.mult).then_inc(step, 1)
            v.tensor_scalar(t1[:, :], cnt[:, :], 0.0, None, ALU.is_equal).then_inc(step, 1)
            v.wait_ge(split, 11)
            v.wait_ge(sums, 2)
            v.wait_ge(step, 7)
            v.memset(t2[:, :], 0.0).then_inc(step, 1)
            v.wait_ge(step, 8)
            v.tensor_tensor_scan(t0[:, :], t2[:, :], totals, 0.0, ALU.add, ALU.add).then_inc(step, 1)
            v.wait_ge(step, 9)
            v.tensor_tensor(t0[:, :], t0[:, :], totals, ALU.subtract).then_inc(step, 1)
            v.wait_ge(step, 10)
            v.tensor_tensor(c.first[:, :], t0[:, :], within, ALU.add).then_inc(step, 1)
            v.wait_ge(step, 11)
            v.wait_ge(judged, 1)
            v.tensor_copy(c.unsorted[:, :], all_falls).then_inc(judged, 1)
            v.tensor_scalar(t3[:, :], c.first[:, :], -1.0, far[:, 0:1], ALU.mult, ALU.add).then_inc(step, 1)
            v.scalar_tensor_tensor(out=t2[:, :], in0=c.first[:, :], scalar=-1.0, in1=cnt[:, :],
                                   op0=ALU.add, op1=ALU.add).then_inc(step, 1)
            v.wait_ge(step, 13)
            v.tensor_scalar(t0[:, :], t2[:, :], -1.0, float(EP), ALU.mult, ALU.add).then_inc(step, 1)
            v.wait_ge(step, 14)
            v.tensor_tensor(t0[:, :], t0[:, :], t1[:, :], ALU.mult).then_inc(step, 1)
            v.wait_ge(step, 15)
            v.tensor_tensor(c.end_idx[:, :], t0[:, :], t2[:, :], ALU.add).then_inc(step, 1)
            v.tensor_tensor(t3[:, :], t3[:, :], t1[:, :], ALU.mult).then_inc(step, 1)
            v.wait_ge(step, 17)
            v.tensor_tensor(c.start_idx[:, :], t3[:, :], c.first[:, :], ALU.add).then_inc(step, 1)
            v.wait_ge(rooted, 1)
            v.reciprocal(c.rs_in[:, :], deg[:, 0, :]).then_inc(step, 1)
            v.reciprocal(c.rs_out[:, :], deg[:, 1, :]).then_inc(step, 1)

        @block.tensor
        def _(pe):
            pe.sem_inc(binned, LEAD)
            pe.wait_ge(cleared, 1)
            pe.matmul(out_bins, zeros[:, 0:P], zeros[:, 0:PARTS * NT], start=True, stop=False,
                      skip_group_check=True)
            pe.matmul(in_bins, zeros[:, 0:P], zeros[:, 0:(1 + PARTS) * NT], start=True, stop=False,
                      skip_group_check=True)
            with pe.Fori(0, ITERS) as i:
                for k in range(2):
                    pe.wait_ge(oh_made, i * 12 + 6 * k + 6 + LEAD)
                    for t in range(ST):
                        pe.matmul(out_bins, oh[0][k][:, :, t], hot[0][k][:, 1:1 + PARTS, :, t],
                                  start=False, stop=False, skip_group_check=True)
                        mm = pe.matmul(in_bins, oh[1][k][:, :, t], hot[1][k][:, :, :, t],
                                       start=False, stop=False, skip_group_check=True)
                    mm.then_inc(binned, 1)
            pe.matmul(out_bins, zeros[:, 0:P], zeros[:, 0:PARTS * NT], start=False, stop=True,
                      skip_group_check=True)
            pe.matmul(in_bins, zeros[:, 0:P], zeros[:, 0:(1 + PARTS) * NT], start=False, stop=True,
                      skip_group_check=True).then_inc(binned, 1)
            pe.wait_ge(made, 9)
            pe.wait_ge(step, 1)
            pe.matmul(within, c.before[:, :], cnt[:, :], start=True, stop=True).then_inc(sums, 1)
            pe.matmul(totals, ones[:, :], cnt[:, :], start=True, stop=True).then_inc(sums, 1)
            pe.wait_ge(falls, 2)
            pe.matmul(all_falls, ones[:, 0:1], fall_sum[:, :], start=True, stop=True).then_inc(judged, 1)
    clear(c, sems)


def sort_edges(c, dst_cols, dst_seq, attr_rows):
    nc = c.nc
    ctx, sb, sem, sems = stage(nc, "sort")
    with ctx:
        dcol = sb("dcol", [P, EC], I32)
        part_i = sb("part_i", [P, EC], I32)
        lo = sb("lo", [P, EC])
        hi = sb("hi", [P, EC])
        iota_i = sb("iota_i", [P, P], I32)
        column = sb("column", [P, P])
        partition = sb("partition", [P, 1])
        before_all = sb("before_all", [1, FE + 4])
        drow = [sb(f"drow{u}", [P, P], I32) for u in range(UN)]
        edge = [sb(f"edge{u}", [P, FE + 4]) for u in range(UN)]
        place = [sb(f"place{u}", [P, 1], I32) for u in range(UN)]
        start = sb("start", [P, NT])
        row_i = sb("row_i", [P, P], I32)
        row_f = sb("row_f", [P, P])
        lo_turned = sb("lo_turned", [P, P])
        lo_hot = sb("lo_hot", [P, P])
        hi_hot = sb("hi_hot", [P, NT])
        same = sb("same", [P, P])
        earlier = sb("earlier", [P, P])
        rank = sb("rank", [P, 1])
        at_hi = sb("at_hi", [P, NT])
        base = sb("base", [P, 1])
        columns_in, made, split, step, multiplied, row0 = (sem("columns_in"), sem("made"), sem("split"),
                                                           sem("step"), sem("multiplied"), sem("row0"))
        loaded = [sem(f"loaded{u}") for u in range(UN)]
        scattered = c.gathered
        ps_start = c.psP[:, 0, 0:NT]
        ps_count = c.psP[:, 1, 0:NT]
        STEPS = 16
        rows = dst_seq.rearrange("p c -> (p c)").rearrange("(t e) -> t e", e=P)
        block = ctx.enter_context(nc.Block())

        @block.sync
        def _(sp):
            sp.dma_start(dcol[:, :], dst_cols).then_inc(columns_in, 16)
            sp.wait_ge(made, 4)
            sp.dma_start(c.by_dst[0:1, :], before_all[:, :]).then_inc(row0, 16)
            with sp.Fori(0, EC // UN) as i:
                for u in range(UN):
                    n = i * UN + u
                    sp.wait_ge(scattered[u], i * 16)
                    sp.dma_start(drow[u][:, :], bcast(rows[bass.ds(n, 1), :], [P, P])).then_inc(loaded[u], 16)
                    sp.dma_start(edge[u][:, 0:FE], attr_rows[bass.ds(n * P, P), :]).then_inc(loaded[u], 16)
            sp.wait_ge(row0, 16)

        @block.gpsimd
        def _(g):
            g.iota(iota_i[:, :], pattern=[[1, P]], base=0, channel_multiplier=0).then_inc(made, 1)
            with g.Fori(0, EC // UN) as i:
                for u in range(UN):
                    placed = g.to_reg((i * UN + u + 1) * STEPS)
                    g.wait_ge(made, 4)
                    g.wait_ge(step, placed)
                    g.indirect_dma_start(c.by_dst[:, :], bass.IndirectOffsetOnAxis(ap=place[u][:, 0:1], axis=0),
                                         edge[u][:, :], None).then_inc(scattered[u], 16)
            for u in range(UN):
                g.wait_ge(scattered[u], 16 * (EC // UN))

        @block.scalar
        def _(a):
            a.copy(start[:, :], c.first[:, :]).then_inc(made, 1)

        @block.vector
        def _(v):
            v.memset(before_all[:, :], -1.0).then_inc(made, 1)
            v.tensor_scalar(partition[:, :], c.trash[:, :], float(-NP), None, ALU.add).then_inc(made, 1)
            v.wait_ge(made, 4)
            v.wait_ge(columns_in, 16)
            v.tensor_copy(column[:, :], iota_i[:, :]).then_inc(split, 1)
            v.tensor_scalar(part_i[:, :], dcol[:, :], P - 1, None, ALU.bitwise_and).then_inc(split, 1)
            v.wait_ge(split, 2)
            v.tensor_copy(lo[:, :], part_i[:, :]).then_inc(split, 1)
            v.wait_ge(split, 3)
            v.tensor_scalar(part_i[:, :], dcol[:, :], 7, None, ALU.logical_shift_right).then_inc(split, 1)
            v.wait_ge(split, 4)
            v.tensor_copy(hi[:, :], part_i[:, :]).then_inc(split, 1)
            v.wait_ge(split, 5)
            with v.Fori(0, EC // UN) as i:
                for u in range(UN):
                    n = i * UN + u
                    col, at = bass.ds(n, 1), n * STEPS
                    v.wait_ge(loaded[u], i * 32 + 32)
                    v.wait_ge(step, at)
                    v.tensor_scalar(row_i[:, :], drow[u][:, :], P - 1, None, ALU.bitwise_and).then_inc(step, 1)
                    v.tensor_tensor(hi_hot[:, :], column[:, 0:NT], bcast(hi[:, col], [P, NT]),
                                    ALU.is_equal).then_inc(step, 1)
                    v.tensor_tensor(lo_hot[:, :], column[:, :], bcast(lo[:, col], [P, P]),
                                    ALU.is_equal).then_inc(step, 1)
                    v.tensor_tensor(same[:, :], drow[u][:, :], bcast(dcol[:, col], [P, P]),
                                    ALU.is_equal).then_inc(step, 1)
                    v.wait_ge(step, at + 1)
                    v.tensor_copy(row_f[:, :], row_i[:, :]).then_inc(step, 1)
                    v.wait_ge(step, at + 5)
                    v.tensor_tensor(lo_turned[:, :], row_f[:, :], bcast(partition[:, :], [P, P]),
                                    ALU.is_equal).then_inc(step, 1)
                    v.tensor_tensor(earlier[:, :], same[:, :], c.after[:, :], ALU.mult).then_inc(step, 1)
                    v.wait_ge(step, at + 7)
                    v.tensor_reduce(rank[:, :], earlier[:, :], AX, ALU.add).then_inc(step, 1)
                    v.wait_ge(scattered[u], i * 16)
                    for k, field in enumerate((c.src, dcol, c.ew, c.ew1)):
                        v.tensor_copy(edge[u][:, FE + k:FE + k + 1], field[:, col]).then_inc(step, 1)
                    v.wait_ge(multiplied, n + 1)
                    v.tensor_tensor(at_hi[:, :], ps_start, hi_hot[:, :], ALU.mult).then_inc(step, 1)
                    v.tensor_tensor(start[:, :], start[:, :], ps_count, ALU.add).then_inc(step, 1)
                    v.wait_ge(step, at + 13)
                    v.tensor_reduce(base[:, :], at_hi[:, :], AX, ALU.add).then_inc(step, 1)
                    v.wait_ge(step, at + 15)
                    v.scalar_tensor_tensor(out=place[u][:, :], in0=base[:, :], scalar=1.0, in1=rank[:, :],
                                           op0=ALU.add, op1=ALU.add).then_inc(step, 1)

        @block.tensor
        def _(pe):
            pe.wait_ge(made, 4)
            with pe.Fori(0, EC // UN) as i:
                for u in range(UN):
                    hot = pe.to_reg((i * UN + u) * STEPS + 6)
                    pe.wait_ge(made, 4)
                    pe.wait_ge(step, hot)
                    pe.matmul(ps_start, lo_turned[:, :], start[:, :], start=True, stop=True)
                    pe.matmul(ps_count, lo_hot[:, :], hi_hot[:, :], start=True, stop=True)\
                        .then_inc(multiplied, 1)
    clear(c, sems)


def lay_out_sorted(c):
    nc = c.nc
    ctx, sb, sem, sems = stage(nc, "relay")
    with ctx:
        edges = sb("edges", [P, ST, FE + 4])
        prev = sb("prev", [P, ST, 2])
        pair = sb("pair", [P, P])
        attr = sb("attr", [P, GT, SG, FE])
        attr_out = sb("attr_out", [P, GE])
        src_out = sb("src_out", [ST, P], I32)
        flg_out = sb("flg_out", [F + ST, P], BF16)
        loaded, first, split, turned, out_made, stored = (sem("loaded"), sem("first"), sem("split"),
                                                          sem("turned"), sem("out_made"), sem("stored"))
        ps_pair = c.psP[:, 0, 0:P]
        ps_attr = c.psP[:, 1, :]
        block = ctx.enter_context(nc.Block())

        @block.sync
        def _(sp):
            with sp.Fori(0, SUPERS) as s:
                sp.wait_ge(split, s * 6)
                sp.dma_start(edges[:, :, :], c.by_dst[bass.ds(s * SE + 1, SE), :]
                             .rearrange("(t p) f -> p t f", p=P)).then_inc(loaded, 16)
                sp.dma_start(prev[:, :, :], c.by_dst[bass.ds(s * SE, SE), FE:FE + 2]
                             .rearrange("(t p) f -> p t f", p=P)).then_inc(loaded, 16)
                sp.wait_ge(out_made, s * 3 + 3)
                sp.dma_start(c.src_rows.rearrange("g (t e) -> (g t) e", e=P)[bass.ds(s * ST, ST), :],
                             src_out[:, :]).then_inc(stored, 16)
                sp.dma_start(c.flags.rearrange("g (t e) -> (g t) e", e=P)[bass.ds(s * ST, ST), :],
                             flg_out[F:F + ST, :]).then_inc(stored, 16)
                sp.dma_start(c.attr_g[bass.ds(s * P, P), :], attr_out[:, :]).then_inc(stored, 16)
            sp.wait_ge(stored, SUPERS * 48)

        @block.gpsimd
        def _(g):
            g.memset(pair[:, :], 0.0).then_inc(first, 1)

        @block.vector
        def _(v):
            v.wait_ge(first, 1)
            with v.Fori(0, SUPERS) as s:
                cols = bass.ds(s * ST, ST)
                v.wait_ge(loaded, s * 32 + 32)
                v.wait_ge(turned, s)
                v.tensor_copy(c.src[:, cols], edges[:, :, FE]).then_inc(split, 1)
                v.tensor_copy(c.ew[:, cols], edges[:, :, FE + 2]).then_inc(split, 1)
                v.tensor_copy(c.ew1[:, cols], edges[:, :, FE + 3]).then_inc(split, 1)
                v.tensor_copy(pair[:, 0:ST], edges[:, :, FE]).then_inc(split, 1)
                v.tensor_tensor(pair[:, F:F + ST], edges[:, :, FE + 1], prev[:, :, 1], ALU.is_equal)\
                    .then_inc(split, 1)
                v.tensor_copy(attr[:, :, :, :], edges[:, :, 0:FE].rearrange("p (g t) f -> p t g f", g=SG))\
                    .then_inc(split, 1)
                v.wait_ge(turned, s + 1)
                v.wait_ge(stored, s * 48)
                v.tensor_copy(src_out[:, :], ps_pair[0:ST, :]).then_inc(out_made, 1)
                v.tensor_copy(flg_out[F:F + ST, :], ps_pair[F:F + ST, :]).then_inc(out_made, 1)

        @block.scalar
        def _(a):
            with a.Fori(0, SUPERS) as s:
                a.wait_ge(turned, s + 1)
                a.wait_ge(stored, s * 48)
                a.copy(attr_out[:, :], ps_attr).then_inc(out_made, 1)

        @block.tensor
        def _(pe):
            with pe.Fori(0, SUPERS) as s:
                pe.wait_ge(split, s * 6 + 6)
                pe.wait_ge(out_made, s * 3)
                pe.transpose(ps_pair, pair[:, :], c.ident[:, :])
                for t in range(GT):
                    mm = pe.transpose(ps_attr[:, t * P:(t + 1) * P],
                                      attr[:, t, :, :].rearrange("p g f -> p (g f)"), c.ident[:, :])
                mm.then_inc(turned, 1)
    clear(c, sems)


def layernorm_relu(v, c, s, step, at, rooted):
    v.wait_ge(step, at)
    v.tensor_reduce(s["mean"][:, :], c.x[:, :, :], AX, ALU.add).then_inc(step, 1)
    v.wait_ge(step, at + 1)
    v.tensor_scalar(s["mean"][:, :], s["mean"][:, :], 1.0 / F, None, ALU.mult).then_inc(step, 1)
    v.wait_ge(step, at + 2)
    v.tensor_tensor(c.h[:, :, :], c.x[:, :, :], bcast(s["mean"][:, :].unsqueeze(2), [P, NT, F]),
                    ALU.subtract).then_inc(step, 1)
    v.wait_ge(step, at + 3)
    v.tensor_tensor(s["sq"][:, :, :], c.h[:, :, :], c.h[:, :, :], ALU.mult).then_inc(step, 1)
    v.wait_ge(step, at + 4)
    v.tensor_reduce(s["mean"][:, :], s["sq"][:, :, :], AX, ALU.add)\
        .then_inc(step, 1)
    v.wait_ge(step, at + 5)
    v.tensor_scalar(s["var"][:, :], s["mean"][:, :], 1.0 / F, LN_EPS, ALU.mult, ALU.add).then_inc(step, 1)
    v.wait_ge(rooted, 1)
    v.reciprocal(s["rstd"][:, :], s["root"][:, :]).then_inc(step, 1)
    v.wait_ge(step, at + 7)
    v.scalar_tensor_tensor(out=c.h[:, :, :], in0=c.h[:, :, :], scalar=0.0,
                           in1=bcast(s["rstd"][:, :].unsqueeze(2), [P, NT, F]),
                           op0=ALU.max, op1=ALU.mult).then_inc(step, 1)


LN_STEPS = 8


def layernorm_buffers(sb):
    s = {k: sb(f"ln_{k}", [P, NT]) for k in ("mean", "var", "root", "rstd")}
    s["sq"] = sb("ln_sq", [P, NT, F])
    return s


def in_pairs(eng, body):
    with eng.Fori(0, NBLK // 2) as j:
        for k in range(2):
            body(j * 2 + k, k)
    body(NBLK - 1, 0)


def turn_block(pe, c, rows, width=F, ps=None):
    ps = c.psQ if ps is None else ps
    for t in range(NB):
        mm = pe.transpose(ps[0:width, t // 4, (t % 4) * P:(t % 4 + 1) * P], rows[:, t, :], c.ident[:, :])
    return mm


def copy_turned(a, c, dst, width=F, ps=None):
    ps = c.psQ if ps is None else ps
    a.copy(dst[0:width, 0:4 * P], ps[0:width, 0, :])
    return a.copy(dst[0:width, 4 * P:BN], ps[0:width, 1, 0:3 * P])


def nodes0(c, W_l1, b_l1, W_s2d, b_s2d, W_d2s, b_d2s):
    nc = c.nc
    ctx, sb, sem, sems = stage(nc, "nodes0")
    with ctx:
        s = layernorm_buffers(sb)
        w = sb("w", [F + 1, 4 * F])
        rows = sb("rows", [P, NB, F])
        turned_sb = sb("turned_sb", [F + 1, BN])
        out_rows = sb("out_rows", [P, NB, 2 * F])
        in_rows = sb("in_rows", [P, NB, 2 * F])
        idx = sb("idx", [P, NB], I32)
        weights, w_init, step, rooted = sem("weights"), sem("w_init"), sem("step"), sem("rooted")
        staged, turned, copied, proj, scaled = (sem("staged"), sem("turned"), sem("copied"),
                                                sem("proj"), sem("scaled"))
        stored, spread = sem("stored"), c.spread_in
        made = c.psP[:, :, :].rearrange("p b (j n) -> p (b j) n", j=2)
        block = ctx.enter_context(nc.Block())

        @block.sync
        def _(sp):
            sp.wait_ge(w_init, 2)
            for k, m in enumerate((W_l1[0:F, :], W_s2d, W_l1[F:2 * F, :], W_d2s)):
                sp.dma_start(w[0:F, k * F:(k + 1) * F], m).then_inc(weights, 16)
            for k, b in ((1, b_s2d), (2, b_l1), (3, b_d2s)):
                sp.dma_start(w[F:F + 1, k * F:(k + 1) * F], b.unsqueeze(0)).then_inc(weights, 16)
            with sp.Fori(0, NBLK) as i:
                sp.wait_ge(scaled, i * 5 + 5)
                sp.dma_start(node_rows(c.table, i), out_rows[:, :, :]).then_inc(stored, 16)
            sp.wait_ge(stored, 16 * NBLK)

        @block.gpsimd
        def _(g):
            g.memset(turned_sb[F:F + 1, :], 1.0).then_inc(w_init, 1)
            with g.Fori(0, NBLK) as i:
                rows_in = g.to_reg(i * 5 + 5)
                g.wait_ge(w_init, 2)
                g.wait_ge(scaled, rows_in)
                for t in range(NB):
                    g.indirect_dma_start(c.spread[:, :], bass.IndirectOffsetOnAxis(ap=idx[:, t:t + 1], axis=0),
                                         in_rows[:, t, :], None).then_inc(spread, 16)
            g.wait_ge(spread, 16 * NT)

        @block.vector
        def _(v):
            v.memset(w[F:F + 1, 0:F], 0.0).then_inc(w_init, 1)
            layernorm_relu(v, c, s, step, 0, rooted)
            v.wait_ge(step, LN_STEPS)
            v.tensor_tensor(c.x[:, :, :], c.x[:, :, :], c.h[:, :, :], ALU.add).then_inc(step, 1)
            with v.Fori(0, NBLK) as i:
                cols = bass.ds(i * NB, NB)
                v.wait_ge(proj, i + 1)
                v.wait_ge(stored, i * 16)
                v.wait_ge(spread, i * (16 * NB))
                v.tensor_copy(idx[:, :], c.start_idx[:, cols]).then_inc(scaled, 1)
                v.tensor_copy(out_rows[:, :, 0:F], made[:, 0:NB, 0:F]).then_inc(scaled, 1)
                v.tensor_copy(in_rows[:, :, 0:F], made[:, 0:NB, 2 * F:3 * F]).then_inc(scaled, 1)
                v.tensor_tensor(out_rows[:, :, F:2 * F], made[:, 0:NB, F:2 * F],
                                bcast(c.rs_out[:, cols].unsqueeze(2), [P, NB, F]),
                                ALU.mult).then_inc(scaled, 1)
                v.tensor_tensor(in_rows[:, :, F:2 * F], made[:, 0:NB, 3 * F:4 * F],
                                bcast(c.rs_in[:, cols].unsqueeze(2), [P, NB, F]),
                                ALU.mult).then_inc(scaled, 1)

        @block.scalar
        def _(a):
            a.wait_ge(step, 6)
            a.activation(s["root"][:, :], s["var"][:, :], ACT.Sqrt).then_inc(rooted, 1)
            a.wait_ge(step, LN_STEPS)
            with a.Fori(0, NBLK) as i:
                a.wait_ge(turned, i)
                a.copy(rows[:, :, :], c.h[:, bass.ds(i * NB, NB), :]).then_inc(staged, 1)
                a.wait_ge(turned, i + 1)
                a.wait_ge(proj, i)
                copy_turned(a, c, turned_sb).then_inc(copied, 1)

        @block.tensor
        def _(pe):
            pe.wait_ge(w_init, 2)
            pe.wait_ge(weights, 16 * 7)
            with pe.Fori(0, NBLK) as i:
                rows_in, ps_free = pe.to_reg(i + 1), pe.to_reg(i)
                pe.wait_ge(w_init, 2)
                pe.wait_ge(staged, rows_in)
                pe.wait_ge(copied, ps_free)
                turn_block(pe, c, rows).then_inc(turned, 1)
                pe.wait_ge(copied, i + 1)
                pe.wait_ge(scaled, i * 5)
                for t in range(NB):
                    mm = pe.matmul(made[:, t, :], turned_sb[:, t * P:(t + 1) * P], w[:, :],
                                   start=True, stop=True)
                mm.then_inc(proj, 1)
    clear(c, sems)


def pick(v, c, idx, super_, picked):
    v.tensor_copy(idx[:, :], c.src[:, super_]).then_inc(picked, 1)


def edges0(c, W_l2, b_l2):
    nc = c.nc
    ctx, sb, sem, sems = stage(nc, "edges0")
    with ctx:
        R = 4
        idx = [sb(f"idx{k}", [P, ST], I32) for k in range(2)]
        srow = [sb(f"srow{u}", [P, GE], I32) for u in range(UN)]
        flg = [sb(f"flg{u}", [P, GE], BF16) for u in range(UN)]
        drow = [sb(f"drow{u}", [P, GT, 2 * F]) for u in range(UN)]
        rows = [sb(f"rows{u}", [P, GT, 2 * F]) for u in range(UN)]
        carried = [sb(f"carried{r}", [P, GE]) for r in range(2)]
        act_in = sb("act_in", [P, GT, F])
        act_w = sb("act_w", [P, GT, F])
        logit = sb("logit", [P, GT])
        kept = sb("kept", [P, GT])
        v_s = [sb(f"v_s{r}", [P, GT, F]) for r in range(2)]
        v_d = [sb(f"v_d{r}", [P, GT, F]) for r in range(2)]
        same = [sb(f"same{r}", [P, GT, P]) for r in range(2)]
        earlier = sb("earlier", [P, GT, P])
        rank = sb("rank", [P, GT])
        off = sb("off", [P, GT])
        away = sb("away", [P, GT])
        scn = [sb(f"scn{r}", [F, GE]) for r in range(2)]
        to_acc = [sb(f"to_acc{r}", [P, GT, F]) for r in range(R)]
        acc_idx = [sb(f"acc_idx{r}", [P, GT], I32) for r in range(R)]
        outr = [sb(f"outr{k}", [P, ST, F]) for k in range(2)]
        wl2 = sb("wl2", [P, F])
        bl2 = sb("bl2", [P, 1])
        neg_b = sb("neg_b", [P, 1])

        consts, ready = sem("consts"), sem("ready")
        loaded = [sem(f"loaded{u}") for u in range(UN)]
        picked = sem("picked")
        gathered = c.gathered
        stored = [sem(f"stored{k}") for k in range(2)]
        added = c.added
        d_turned, d_scanned, d_back = sem("d_turned"), sem("d_scanned"), sem("d_back")
        summed_in, act_done, dotted, kept_done = (sem("summed_in"), sem("act_done"), sem("dotted"),
                                                  sem("kept_done"))
        vs_done, vd_done, same_done, early_done, rank_done, off_done, away_done, idx_done = (
            sem("vs_done"), sem("vd_done"), sem("same_done"), sem("early_done"), sem("rank_done"),
            sem("off_done"), sem("away_done"), sem("idx_done"))
        merged, merged_out = sem("merged"), sem("merged_out")
        turned, scanned, back, copied = sem("turned"), sem("scanned"), sem("back"), sem("copied")

        ps_d = [c.psP[:, 0, :], c.psP[:, 1, :]]
        ps_e = c.psP[:, 2, :].rearrange("p (t f) -> p t f", t=GT)
        ps_m = c.psP[:, 3, 0:GT * F]
        ps_t = [c.psQ[0:F, 0, :], c.psQ[0:F, 1, :]]
        ps_b = [c.psQ[:, 2, 0:GT * F], c.psQ[:, 3, 0:GT * F]]
        block = ctx.enter_context(nc.Block())

        @block.sync
        def _(sp):
            sp.dma_start(wl2[:, :], bcast(W_l2.rearrange("f a -> a f"), [P, F])).then_inc(consts, 16)
            sp.dma_start(bl2[:, :], bcast(b_l2.unsqueeze(0), [P, 1])).then_inc(consts, 16)
            with sp.Fori(0, ITERS) as i:
                for u in range(UN):
                    sp.wait_ge(scanned, i * 8 + u + 1 - 8 + LEAD)
                    group = i * 8 + u
                    sp.dma_start(srow[u][:, :], bcast(c.src_rows[bass.ds(group, 1), :], [P, GE]))\
                        .then_inc(loaded[u], 16)
                    sp.dma_start(flg[u][:, :], bcast(c.flags[bass.ds(group, 1), :], [P, GE]))\
                        .then_inc(loaded[u], 16)
                    sp.dma_start(drow[u][:, :, :], c.spread[bass.ds(group * GE, GE), :]
                                 .rearrange("(t p) f -> p t f", p=P)).then_inc(loaded[u], 16)

        @block.gpsimd
        def _(g):
            for r in (2, 3):
                g.memset(to_acc[r][:, :, :], 0.0).then_inc(ready, 1)
                g.tensor_copy(acc_idx[r][:, :], bcast(c.trash[:, :], [P, GT])).then_inc(ready, 1)
            def scatter(r):
                for t in range(ACCS):
                    g.indirect_dma_start(c.acc[t][:, :],
                                         bass.IndirectOffsetOnAxis(ap=acc_idx[r][:, t:t + 1], axis=0),
                                         to_acc[r][:, t, :], None, compute_op=ALU.add)\
                        .then_inc(added[t], 16)

            with g.Fori(0, ITERS) as i:
                for u in range(UN):
                    k = u // SG
                    super_in, slot_free = g.to_reg(i * 2 + k + 1), g.to_reg(i * 8 + u + 1 - 8 + LEAD)
                    g.wait_ge(ready, 7)
                    g.wait_ge(picked, super_in)
                    g.wait_ge(vs_done, slot_free)
                    for t in range(GT):
                        col = (u % SG) * GT + t
                        g.indirect_dma_start(rows[u][:, t, :], None, c.table[:, :],
                                             bass.IndirectOffsetOnAxis(ap=idx[k][:, col:col + 1], axis=0))\
                            .then_inc(gathered[u], 16)
                    done2, acc_free = g.to_reg(i * 8 + u - 1 + LEAD), g.to_reg(i * 128 + 16 * u)
                    g.wait_ge(ready, 7)
                    g.wait_ge(merged_out, done2)
                    g.wait_ge(idx_done, done2)
                    for t in range(ACCS):
                        g.wait_ge(added[t], acc_free)
                    scatter((u - 2) % R)
            for n in range(2):
                g.wait_ge(merged_out, SUPERS * SG - 1 + n + LEAD)
                g.wait_ge(idx_done, SUPERS * SG - 1 + n + LEAD)
                for t in range(ACCS):
                    g.wait_ge(added[t], 16 * (SUPERS * SG + n))
                scatter((SUPERS * SG - 2 + n) % R)
            for t in range(ACCS):
                g.wait_ge(added[t], 16 * (SUPERS * SG + 2))

        @block.vector
        def _(v):
            for sm in (summed_in, act_done, dotted, kept_done, vs_done, vd_done, same_done, early_done,
                       rank_done, off_done, away_done, idx_done, d_scanned, scanned):
                v.sem_inc(sm, LEAD)
            v.memset(carried[1][:, :], 0.0).then_inc(ready, 1)
            v.memset(scn[1][:, :], 0.0).then_inc(ready, 1)
            v.wait_ge(consts, 32)
            v.tensor_scalar(neg_b[:, :], bl2[:, :], -1.0, None, ALU.mult).then_inc(ready, 1)
            v.wait_ge(ready, 7)
            for k in range(2):
                pick(v, c, idx[k], slice(k * ST, (k + 1) * ST), picked)
            with v.Fori(0, ITERS) as i:
                for u in range(UN):
                    k, r, q = u // SG, u % 2, u % R
                    n = i * 8 + u + 1 + LEAD
                    tiles = slice((u % SG) * GT, (u % SG + 1) * GT)
                    v.wait_ge(picked, i * 2 + k + 1)
                    v.wait_ge(loaded[u], i * 48 + 48)
                    v.wait_ge(d_turned, n)
                    v.wait_ge(d_back, n - 2)
                    v.wait_ge(d_scanned, n - 1)
                    v.tensor_tensor_scan(carried[r][:, :], flg[u][:, :], ps_d[r],
                                         carried[1 - r][:, GE - 1:GE], ALU.mult, ALU.add)\
                        .then_inc(d_scanned, 1)
                    v.wait_ge(merged, n - 2)
                    v.tensor_tensor(same[r][:, :, :],
                                    srow[u][:, :].rearrange("p (t e) -> p t e", t=GT),
                                    bcast(idx[k][:, tiles].unsqueeze(2), [P, GT, P]), ALU.is_equal)\
                        .then_inc(same_done, 1)
                    v.wait_ge(same_done, n)
                    v.wait_ge(rank_done, n - 1)
                    v.tensor_tensor(earlier[:, :, :], same[r][:, :, :],
                                    bcast(c.after[:, :].unsqueeze(1), [P, GT, P]), ALU.mult)\
                        .then_inc(early_done, 1)
                    v.wait_ge(gathered[u], i * 64 + 64)
                    v.wait_ge(d_back, n)
                    v.tensor_tensor(act_in[:, :, :], rows[u][:, :, 0:F], ps_e[:, :, 0:F], ALU.add)\
                        .then_inc(summed_in, 1)
                    v.wait_ge(early_done, n)
                    v.wait_ge(away_done, n - 1)
                    v.tensor_reduce(rank[:, :], earlier[:, :, :], AX, ALU.add).then_inc(rank_done, 1)
                    v.wait_ge(summed_in, n)
                    v.wait_ge(dotted, n - 1)
                    v.scalar_tensor_tensor(out=act_w[:, :, :], in0=act_in[:, :, :], scalar=0.0,
                                           in1=bcast(wl2[:, :].unsqueeze(1), [P, GT, F]), op0=ALU.max,
                                           op1=ALU.mult).then_inc(act_done, 1)
                    v.wait_ge(idx_done, n - 1)
                    v.tensor_scalar(off[:, :], idx[k][:, tiles], -1.0, c.trash[:, 0:1], ALU.mult, ALU.add)\
                        .then_inc(off_done, 1)
                    v.wait_ge(act_done, n)
                    v.tensor_reduce(logit[:, :], act_w[:, :, :], AX, ALU.add).then_inc(dotted, 1)
                    v.wait_ge(off_done, n)
                    v.wait_ge(rank_done, n)
                    v.scalar_tensor_tensor(out=away[:, :], in0=rank[:, :], scalar=0.0, in1=off[:, :],
                                           op0=ALU.is_gt, op1=ALU.mult).then_inc(away_done, 1)
                    v.wait_ge(dotted, n)
                    v.wait_ge(vd_done, n - 1)
                    v.scalar_tensor_tensor(out=kept[:, :], in0=logit[:, :], scalar=neg_b[:, 0:1],
                                           in1=c.ew[:, bass.ds((i * 8 + u) * GT, GT)], op0=ALU.is_ge, op1=ALU.mult)\
                        .then_inc(kept_done, 1)
                    v.wait_ge(kept_done, n)
                    v.wait_ge(away_done, n)
                    for t in range(ACCS):
                        v.wait_ge(added[t], i * 128 + 16 * u)
                    v.tensor_tensor(acc_idx[q][:, :], away[:, :], idx[k][:, tiles], ALU.add)\
                        .then_inc(idx_done, 1)
                    v.wait_ge(turned, n - 2)
                    v.tensor_tensor(v_s[r][:, :, :], rows[u][:, :, F:2 * F],
                                    bcast(kept[:, :].unsqueeze(2), [P, GT, F]), ALU.mult)\
                        .then_inc(vs_done, 1)
                    v.tensor_tensor(v_d[r][:, :, :], ps_e[:, :, F:2 * F],
                                    bcast(kept[:, :].unsqueeze(2), [P, GT, F]), ALU.mult)\
                        .then_inc(vd_done, 1)
                    v.wait_ge(turned, n)
                    v.wait_ge(back, n - 2)
                    v.wait_ge(scanned, n - 1)
                    v.tensor_tensor_scan(scn[r][:, :], flg[u][0:F, :], ps_t[r],
                                         scn[1 - r][:, GE - 1:GE], ALU.mult, ALU.add)\
                        .then_inc(scanned, 1)
                    if u % SG == SG - 1:
                        v.wait_ge(gathered[u], i * 64 + 64)
                        v.wait_ge(idx_done, n)
                        pick(v, c, idx[k], bass.ds((i * 2 + k + 2) * ST, ST), picked)

        @block.tensor
        def _(pe):
            for sm in (d_turned, d_back, merged, turned, back):
                pe.sem_inc(sm, LEAD)
            with pe.Fori(0, ITERS) as i:
                def turn_dst(u):
                    k, r, n = u // SG, u % 2, i * 8 + u + 1 + LEAD
                    pe.wait_ge(loaded[u], i * 48 + 48)
                    pe.wait_ge(d_scanned, n - 2)
                    for t in range(GT):
                        mm = pe.transpose(ps_d[r][:, t * P:(t + 1) * P], drow[u][:, t, :],
                                          c.ident[:, :])
                    mm.then_inc(d_turned, 1)

                turn_dst(0)
                for u in range(UN):
                    k, r, n = u // SG, u % 2, i * 8 + u + 1 + LEAD
                    pe.wait_ge(d_scanned, n)
                    pe.wait_ge(vd_done, n - 1)
                    for t in range(GT):
                        mm = pe.transpose(ps_e[:, t, :], carried[r][:, t * P:(t + 1) * P], c.ident[:, :])
                    mm.then_inc(d_back, 1)
                    if u + 1 < UN:
                        turn_dst(u + 1)
                    v_s_in, ps_free = pe.to_reg(n), pe.to_reg(n - 2)
                    pe.wait_ge(ready, 7)
                    pe.wait_ge(vs_done, v_s_in)
                    pe.wait_ge(scanned, ps_free)
                    for t in range(GT):
                        mm = pe.transpose(ps_t[r][:, t * P:(t + 1) * P], v_s[r][:, t, :], c.ident[:, :])
                    mm.then_inc(turned, 1)
                    pe.wait_ge(vd_done, n)
                    pe.wait_ge(same_done, n)
                    pe.wait_ge(merged_out, n - 1)
                    for t in range(GT):
                        mm = pe.matmul(ps_m[:, t * F:(t + 1) * F], same[r][:, t, :], v_d[r][:, t, :],
                                       start=True, stop=True)
                    mm.then_inc(merged, 1)
                    scan_in, ps_free = pe.to_reg(n), pe.to_reg(n - 2)
                    pe.wait_ge(ready, 7)
                    pe.wait_ge(scanned, scan_in)
                    pe.wait_ge(copied, ps_free)
                    for t in range(GT):
                        mm = pe.transpose(ps_b[r][:, t * F:(t + 1) * F], scn[r][:, t * P:(t + 1) * P],
                                          c.ident[0:F, 0:F])
                    mm.then_inc(back, 1)

        @block.scalar
        def _(a):
            for sm in (merged_out, copied):
                a.sem_inc(sm, LEAD)
            with a.Fori(0, ITERS) as i:
                for u in range(UN):
                    k, r, q, n = u // SG, u % 2, u % R, i * 8 + u + 1 + LEAD
                    a.wait_ge(merged, n)
                    for t in range(ACCS):
                        a.wait_ge(added[t], i * 128 + 16 * u)
                    a.copy(to_acc[q][:, :, :].rearrange("p t f -> p (t f)"), ps_m).then_inc(merged_out, 1)
                    if u % SG == 0:
                        a.wait_ge(stored[k], i * 16)
                    a.wait_ge(back, n)
                    a.copy(outr[k][:, (u % SG) * GT:(u % SG + 1) * GT, :].rearrange("p t f -> p (t f)"),
                           ps_b[r]).then_inc(copied, 1)
                    if u % SG == SG - 1:
                        a.wait_ge(copied, n)
                        a.dma_start(c.scans[bass.ds((i * 2 + k) * SE, SE), :]
                                    .rearrange("(t p) f -> p t f", p=P), outr[k][:, :, :])\
                            .then_inc(stored[k], 16)
            for k in range(2):
                a.wait_ge(stored[k], 16 * ITERS)
    clear(c, sems)


def gather_ends(g, c):
    for t in range(NT):
        g.indirect_dma_start(c.ends[:, t, :], None, c.scans[:, :],
                             bass.IndirectOffsetOnAxis(ap=c.end_idx[:, t:t + 1], axis=0))\
            .then_inc(c.gathered[t // NB], 16)
    for b in range(NBLK):
        g.wait_ge(c.gathered[b], 16 * NB)


def nodes1(c, W_g1, b_g1, W_g2, b_g2, W1, b1):
    nc = c.nc
    ctx, sb, sem, sems = stage(nc, "nodes1")
    with ctx:
        s = layernorm_buffers(sb)
        acc = [sb(f"acc_sb{k}", [P, NT, F]) for k in range(ACCS)]
        m_out, diff = acc[1], acc[0]
        wg1 = sb("wg1", [2 * F, F])
        bg1 = sb("bg1", [F, 1])
        wg2 = sb("wg2", [F, 1])
        bg2 = sb("bg2", [P, 1])
        gate = sb("gate", [P, NT])
        w = sb("w", [F + 1, 2 * F])
        cat = [sb(f"cat{k}", [P, NB, 2 * F]) for k in range(2)]
        turned_sb = [sb(f"turned_sb{k}", [2 * F, BN]) for k in range(2)]
        hidden = [sb(f"hidden{k}", [F, BN]) for k in range(2)]
        h_rows = [sb(f"h_rows{k}", [P, NB, F]) for k in range(2)]
        h_turned = [sb(f"h_turned{k}", [F + 1, BN]) for k in range(2)]
        out_rows = [sb(f"out_rows{k}", [P, NB, 2 * F]) for k in range(2)]
        weights, accs, step, rooted, one = (sem("weights"), sem("accs"), sem("step"), sem("rooted"),
                                            sem("one"))
        cat_made, turned, copied, mixed, bent, dots, gated = (sem("cat_made"), sem("turned"), sem("copied"),
                                                              sem("mixed"), sem("bent"), sem("dots"),
                                                              sem("gated"))
        diffed, joined = sem("diffed"), sem("joined")
        staged2, turned2, copied2, proj, out_made = (sem("staged2"), sem("turned2"), sem("copied2"),
                                                     sem("proj"), sem("out_made"))
        stored = [sem(f"stored{k}") for k in range(2)]
        ps_turn = c.psQ[:, 0:2, :]
        ps_mix = [c.psQ[0:F, 2, 0:BN // 2], c.psQ[0:F, 3, 0:BN // 2]]
        ps_dot = [c.psP[:, 0, 0:NB], c.psP[:, 1, 0:NB]]
        ps_turn2 = [c.psP[:, 0:2, :], c.psP[:, 2:4, :]]
        made = c.psQ[:, :, :].rearrange("p b (j n) -> p (b j) n", j=4)
        block = ctx.enter_context(nc.Block())

        @block.sync
        def _(sp):
            for k in range(ACCS):
                sp.dma_start(acc[k][:, :, :], c.acc[k][0:NP, :].rearrange("(t p) f -> p t f", p=P))\
                    .then_inc(accs, 16)
            sp.dma_start(wg1[:, :], W_g1).then_inc(weights, 16)
            sp.dma_start(bg1[:, :], b_g1.unsqueeze(1)).then_inc(weights, 16)
            sp.dma_start(wg2[:, :], W_g2).then_inc(weights, 16)
            sp.dma_start(bg2[:, :], bcast(b_g2.unsqueeze(0), [P, 1])).then_inc(weights, 16)
            sp.dma_start(w[0:F, :], W1[0:F, :]).then_inc(weights, 16)
            sp.dma_start(w[F:F + 1, :], b1.unsqueeze(0)).then_inc(weights, 16)

            def store(i, k):
                sp.wait_ge(out_made, i + 1 + LEAD)
                sp.dma_start(node_rows(c.table, i), out_rows[k][:, :, :]).then_inc(stored[k], 16)

            in_pairs(sp, store)
            for k in range(2):
                sp.wait_ge(stored[k], 16 * ((NBLK + 1 - k) // 2))

        @block.gpsimd
        def _(g):
            for k in range(2):
                g.memset(h_turned[k][F:F + 1, :], 1.0).then_inc(one, 1)
            gather_ends(g, c)

        @block.vector
        def _(v):
            v.sem_inc(out_made, LEAD)
            v.sem_inc(cat_made, LEAD)
            v.wait_ge(accs, 16 * ACCS)
            v.tensor_tensor(acc[0][:, :, :], acc[0][:, :, :], acc[1][:, :, :], ALU.add).then_inc(step, 1)
            v.tensor_tensor(acc[2][:, :, :], acc[2][:, :, :], acc[3][:, :, :], ALU.add).then_inc(step, 1)
            v.wait_ge(step, 2)
            v.tensor_tensor(acc[0][:, :, :], acc[0][:, :, :], acc[2][:, :, :], ALU.add).then_inc(step, 1)
            v.wait_ge(step, 3)
            v.tensor_tensor(m_out[:, :, :], acc[0][:, :, :],
                            bcast(c.rs_out[:, :].unsqueeze(2), [P, NT, F]), ALU.mult).then_inc(step, 1)
            v.wait_ge(step, 4)
            for j in range(NBLK + 1):
                if j < NBLK:
                    tiles, k = slice(j * NB, (j + 1) * NB), j % 2
                    v.wait_ge(c.gathered[j], 16 * NB)
                    v.wait_ge(turned, LEAD + j - 1)
                    v.wait_ge(diffed, j)
                    v.tensor_tensor(cat[k][:, :, 0:F], c.ends[:, tiles, :],
                                    bcast(c.rs_in[:, tiles].unsqueeze(2), [P, NB, F]), ALU.mult)\
                        .then_inc(cat_made, 1)
                    v.tensor_copy(cat[k][:, :, F:2 * F], m_out[:, tiles, :]).then_inc(cat_made, 1)
                    v.wait_ge(cat_made, 2 * j + 1 + LEAD)
                    v.tensor_tensor(diff[:, tiles, :], cat[k][:, :, 0:F], m_out[:, tiles, :],
                                    ALU.subtract).then_inc(diffed, 1)
                if j > 0:
                    tiles = slice((j - 1) * NB, j * NB)
                    v.wait_ge(gated, LEAD + j)
                    v.wait_ge(diffed, j)
                    v.tensor_tensor(diff[:, tiles, :], diff[:, tiles, :],
                                    bcast(gate[:, tiles].unsqueeze(2), [P, NB, F]), ALU.mult)\
                        .then_inc(joined, 1)
                    v.wait_ge(joined, 3 * j - 2)
                    v.tensor_tensor(diff[:, tiles, :], diff[:, tiles, :], m_out[:, tiles, :], ALU.add)\
                        .then_inc(joined, 1)
                    v.wait_ge(joined, 3 * j - 1)
                    v.scalar_tensor_tensor(out=c.x[:, tiles, :], in0=diff[:, tiles, :], scalar=0.5,
                                           in1=c.x[:, tiles, :], op0=ALU.mult, op1=ALU.add)\
                        .then_inc(joined, 1)
            v.wait_ge(joined, 3 * NBLK)
            layernorm_relu(v, c, s, step, 4, rooted)

            def out(i, k):
                v.wait_ge(proj, i + 1 + LEAD)
                v.wait_ge(stored[k], (i - k) * 8)
                v.tensor_copy(out_rows[k][:, :, :], made[:, k * 8:k * 8 + NB, :]).then_inc(out_made, 1)

            in_pairs(v, out)

        @block.scalar
        def _(a):
            for sm in (copied, bent, gated, staged2, copied2):
                a.sem_inc(sm, LEAD)
            a.wait_ge(weights, 16 * 6)

            def to_gate(i, k):
                n = i + 1 + LEAD
                a.wait_ge(turned, n)
                a.wait_ge(mixed, n - 2)
                copy_turned(a, c, turned_sb[k], 2 * F, ps_turn).then_inc(copied, 1)
                a.wait_ge(mixed, n)
                a.wait_ge(dots, n - 2)
                a.activation(hidden[k][:, 0:BN // 2], ps_mix[0], ACT.Relu, bias=bg1[:, 0:1])
                a.activation(hidden[k][:, BN // 2:BN], ps_mix[1], ACT.Relu, bias=bg1[:, 0:1])\
                    .then_inc(bent, 1)
                a.wait_ge(dots, n)
                a.activation(gate[:, bass.ds(i * NB, NB)], ps_dot[k], ACT.Sigmoid, bias=bg2[:, 0:1])\
                    .then_inc(gated, 1)

            def turn_h(i, k):
                n = i + 1 + LEAD
                a.wait_ge(turned2, n - 2)
                a.copy(h_rows[k][:, :, :], c.h[:, bass.ds(i * NB, NB), :]).then_inc(staged2, 1)
                a.wait_ge(turned2, n)
                a.wait_ge(proj, n - 2)
                copy_turned(a, c, h_turned[k], ps=ps_turn2[k]).then_inc(copied2, 1)

            in_pairs(a, to_gate)
            a.wait_ge(step, 4 + 6)
            a.activation(s["root"][:, :], s["var"][:, :], ACT.Sqrt).then_inc(rooted, 1)
            a.wait_ge(step, 4 + LN_STEPS)
            in_pairs(a, turn_h)

        @block.tensor
        def _(pe):
            for sm in (turned, mixed, dots, turned2, proj):
                pe.sem_inc(sm, LEAD)
            pe.wait_ge(weights, 16 * 6)
            pe.wait_ge(one, 2)

            def gate_products(i, k):
                now, one_back, two_back = (pe.to_reg(i + 1 + LEAD), pe.to_reg(i + LEAD),
                                           pe.to_reg(i - 1 + LEAD))
                cat_in = pe.to_reg(i * 2 + 2 + LEAD)
                pe.wait_ge(one, 2)
                pe.wait_ge(cat_made, cat_in)
                pe.wait_ge(copied, one_back)
                turn_block(pe, c, cat[k], 2 * F, ps_turn).then_inc(turned, 1)
                pe.wait_ge(one, 2)
                pe.wait_ge(copied, now)
                pe.wait_ge(bent, one_back)
                for j in range(2):
                    mm = pe.matmul(ps_mix[j], wg1[:, :], turned_sb[k][:, j * BN // 2:(j + 1) * BN // 2],
                                   start=True, stop=True)
                mm.then_inc(mixed, 1)
                pe.wait_ge(one, 2)
                pe.wait_ge(bent, now)
                pe.wait_ge(gated, two_back)
                for t in range(NB):
                    mm = pe.matmul(ps_dot[k][:, t:t + 1], hidden[k][:, t * P:(t + 1) * P], wg2[:, :],
                                   start=True, stop=True)
                mm.then_inc(dots, 1)

            def project(i, k):
                now, two_back = pe.to_reg(i + 1 + LEAD), pe.to_reg(i - 1 + LEAD)
                pe.wait_ge(one, 2)
                pe.wait_ge(staged2, now)
                pe.wait_ge(copied2, two_back)
                turn_block(pe, c, h_rows[k], ps=ps_turn2[k]).then_inc(turned2, 1)
                pe.wait_ge(one, 2)
                pe.wait_ge(copied2, now)
                pe.wait_ge(out_made, two_back)
                for t in range(NB):
                    mm = pe.matmul(made[:, k * 8 + t, :], h_turned[k][:, t * P:(t + 1) * P], w[:, :],
                                   start=True, stop=True)
                mm.then_inc(proj, 1)

            in_pairs(pe, gate_products)
            in_pairs(pe, project)
    clear(c, sems)


def edges1(c, W1, W2):
    nc = c.nc
    ctx, sb, sem, sems = stage(nc, "edges1")
    with ctx:
        idx = [sb(f"idx{k}", [P, ST], I32) for k in range(2)]
        flg = [sb(f"flg{k}", [F, SE], BF16) for k in range(2)]
        attr = [sb(f"attr{k}", [P, GE]) for k in range(2)]
        rows = [sb(f"rows{u}", [P, GT, 2 * F]) for u in range(UN)]
        act = [sb(f"act{r}", [P, GE]) for r in range(2)]
        scn = [sb(f"scn{r}", [F, GE]) for r in range(2)]
        outr = [sb(f"outr{k}", [P, ST, F]) for k in range(2)]
        w1 = sb("w1", [P, SG, 2 * F])
        w2 = sb("w2", [2 * F, F])
        weights, first = sem("weights"), sem("first")
        loaded = [sem(f"loaded{k}") for k in range(2)]
        picked = sem("picked")
        gathered = c.gathered
        stored = [sem(f"stored{k}") for k in range(2)]
        summed, bent, scanned, back, copied = (sem("summed"), sem("bent"), sem("scanned"), sem("back"),
                                               sem("copied"))
        mixed = sem("mixed")
        ps_z = [c.psP[:, 0, :], c.psP[:, 1, :]]
        ps_v = [c.psP[0:F, 2, :], c.psP[0:F, 3, :]]
        ps_b = [c.psQ[:, 0, 0:GT * F], c.psQ[:, 1, 0:GT * F]]
        block = ctx.enter_context(nc.Block())

        @block.sync
        def _(sp):
            sp.wait_ge(first, 2)
            for g in range(SG):
                sp.dma_start(w1[g * FE:(g + 1) * FE, g, :], W1[F:F + FE, :]).then_inc(weights, 16)
            sp.dma_start(w2[:, :], W2).then_inc(weights, 16)
            with sp.Fori(0, ITERS) as i:
                for k in range(2):
                    s = i * 2 + k
                    sp.wait_ge(scanned, i * 8 + 4 * k - 4 + LEAD)
                    sp.dma_start(attr[k][:, :], c.attr_g[bass.ds(s * P, P), :]).then_inc(loaded[k], 16)
                    sp.dma_start(flg[k][:, :], bcast(super_flags(c, s), [F, SE]))\
                        .then_inc(loaded[k], 16)

        @block.gpsimd
        def _(g):
            with g.Fori(0, ITERS) as i:
                for u in range(UN):
                    k = u // SG
                    super_in, slot_free = g.to_reg(i * 2 + k + 1), g.to_reg(i * 8 + u + 1 - 8 + LEAD)
                    g.wait_ge(weights, 16 * (SG + 1))
                    g.wait_ge(picked, super_in)
                    g.wait_ge(summed, slot_free)
                    for t in range(GT):
                        col = (u % SG) * GT + t
                        g.indirect_dma_start(rows[u][:, t, :], None, c.table[:, :],
                                             bass.IndirectOffsetOnAxis(ap=idx[k][:, col:col + 1], axis=0))\
                            .then_inc(gathered[u], 16)

        @block.vector
        def _(v):
            v.sem_inc(scanned, LEAD)
            v.memset(scn[1][:, :], 0.0).then_inc(first, 1)
            v.memset(w1[:, :, :], 0.0).then_inc(first, 1)
            v.wait_ge(first, 2)
            for k in range(2):
                pick(v, c, idx[k], slice(k * ST, (k + 1) * ST), picked)
            with v.Fori(0, ITERS) as i:
                for u in range(UN):
                    k, r, n = u // SG, u % 2, i * 8 + u + 1 + LEAD
                    v.wait_ge(loaded[k], i * 32 + 32)
                    v.wait_ge(mixed, n)
                    v.wait_ge(back, n - 2)
                    v.wait_ge(scanned, n - 1)
                    v.tensor_tensor_scan(scn[r][:, :], flg[k][:, (u % SG) * GE:(u % SG + 1) * GE],
                                         ps_v[r], scn[1 - r][:, GE - 1:GE], ALU.mult, ALU.add)\
                        .then_inc(scanned, 1)
                    if u % SG == SG - 1:
                        v.wait_ge(gathered[u], i * 64 + 64)
                        pick(v, c, idx[k], bass.ds((i * 2 + k + 2) * ST, ST), picked)

        @block.tensor
        def _(pe):
            for sm in (summed, mixed, back):
                pe.sem_inc(sm, LEAD)
            pe.wait_ge(weights, 16 * (SG + 1))
            with pe.Fori(0, ITERS) as i:
                def attr_part(u):
                    k, r, n = u // SG, u % 2, i * 8 + u + 1 + LEAD
                    pe.wait_ge(loaded[k], i * 32 + 32)
                    pe.wait_ge(bent, n - 2)
                    pe.matmul(ps_z[r], w1[:, u % SG, :], attr[k][:, :], start=True, stop=False,
                              skip_group_check=True)

                def rows_part(u):
                    r = u % 2
                    pe.wait_ge(gathered[u], i * 64 + 64)
                    for t in range(GT):
                        mm = pe.matmul(ps_z[r][:, t * P:(t + 1) * P], rows[u][:, t, :], c.ident[:, :],
                                       start=False, stop=(t == GT - 1), skip_group_check=True)
                    mm.then_inc(summed, 1)

                attr_part(0)
                rows_part(0)
                for u in range(UN):
                    r, n = u % 2, i * 8 + u + 1 + LEAD
                    if u + 1 < UN:
                        attr_part(u + 1)
                    pe.wait_ge(bent, n)
                    pe.wait_ge(scanned, n - 2)
                    pe.matmul(ps_v[r], w2[:, :], act[r][:, :], start=True, stop=True).then_inc(mixed, 1)
                    if u + 1 < UN:
                        rows_part(u + 1)
                    scan_in, out_free = pe.to_reg(n), pe.to_reg(n - 2)
                    pe.wait_ge(weights, 16 * (SG + 1))
                    pe.wait_ge(scanned, scan_in)
                    pe.wait_ge(copied, out_free)
                    for t in range(GT):
                        mm = pe.transpose(ps_b[r][:, t * F:(t + 1) * F], scn[r][:, t * P:(t + 1) * P],
                                          c.ident[0:F, 0:F])
                    mm.then_inc(back, 1)

        @block.scalar
        def _(a):
            for sm in (bent, copied):
                a.sem_inc(sm, LEAD)
            with a.Fori(0, ITERS) as i:
                for u in range(UN):
                    k, r, n = u // SG, u % 2, i * 8 + u + 1 + LEAD
                    a.wait_ge(summed, n)
                    a.wait_ge(mixed, n - 2)
                    a.activation(act[r][:, :], ps_z[r], ACT.Relu).then_inc(bent, 1)
                    if u % SG == 0:
                        a.wait_ge(stored[k], i * 16)
                    a.wait_ge(back, n)
                    a.copy(outr[k][:, (u % SG) * GT:(u % SG + 1) * GT, :].rearrange("p t f -> p (t f)"),
                           ps_b[r]).then_inc(copied, 1)
                    if u % SG == SG - 1:
                        a.wait_ge(copied, n)
                        a.dma_start(c.scans[bass.ds((i * 2 + k) * SE, SE), :]
                                    .rearrange("(t p) f -> p t f", p=P), outr[k][:, :, :])\
                            .then_inc(stored[k], 16)
            for k in range(2):
                a.wait_ge(stored[k], 16 * ITERS)
    clear(c, sems)


SC = BN // 2
NSC = -(-NODES // SC)


def batch_stats(v, b, turned_all, j, step):
    v.bn_stats(b["stats"][:, j, :], turned_all[:, j * SC:min((j + 1) * SC, NODES)]).then_inc(step, 1)


def batch_scale(v, b, gamma, beta, step, at, rooted):
    v.wait_ge(step, at + NSC)
    v.bn_aggr(b["mv"][:, :], b["stats"][:, :, :].rearrange("p a b -> p (a b)")).then_inc(step, 1)
    v.wait_ge(step, at + NSC + 1)
    v.tensor_scalar(b["var"][:, :], b["mv"][:, 1:2], BN_EPS, None, ALU.add).then_inc(step, 1)
    v.wait_ge(rooted, 1)
    v.reciprocal(b["rstd"][:, :], b["root"][:, :]).then_inc(step, 1)
    v.wait_ge(step, at + NSC + 3)
    v.tensor_tensor(b["scale"][:, :], b["rstd"][:, :], gamma[:, :], ALU.mult).then_inc(step, 1)
    v.wait_ge(step, at + NSC + 4)
    v.tensor_tensor(b["rstd"][:, :], b["mv"][:, 0:1], b["scale"][:, :], ALU.mult).then_inc(step, 1)
    v.wait_ge(step, at + NSC + 5)
    v.tensor_tensor(b["shift"][:, :], beta[:, :], b["rstd"][:, :], ALU.subtract).then_inc(step, 1)


BATCH_STEPS = NSC + 6


def batch_buffers(sb):
    b = {k: sb(f"bn_{k}", [F, 1]) for k in ("var", "root", "rstd", "scale", "shift")}
    b["mv"] = sb("bn_mv", [F, 2])
    b["stats"] = sb("bn_stats", [F, NSC, 6])
    return b


def nodes2(c, u, b2, W3, b3, W4, b4, gamma, beta, W1, b1):
    nc = c.nc
    ctx, sb, sem, sems = stage(nc, "nodes2")
    with ctx:
        s = layernorm_buffers(sb)
        bn = batch_buffers(sb)
        cat = [sb(f"cat{k}", [P, NB, 2 * F]) for k in range(2)]
        b2_row = sb("b2_row", [P, F])
        w3 = sb("w3", [2 * F, F])
        w3u = sb("w3u", [F, F])
        u0 = sb("u0", [F, 1])
        b3_col = sb("b3_col", [F, 1])
        bias3 = sb("bias3", [F, 1])
        w4 = sb("w4", [F + 1, F])
        gam = sb("gam", [F, 1])
        bet = sb("bet", [F, 1])
        w = sb("w", [F + 1, 4 * F])
        turned_sb = [sb(f"turned_sb{k}", [2 * F, BN]) for k in range(2)]
        hidden = [sb(f"hidden{k}", [F + 1, BN]) for k in range(2)]
        h_rows = sb("h_rows", [P, NB, F])
        turned_all = sb("turned_all", [F, NP])
        xn = sb("xn", [F + 1, BN])
        out_rows = sb("out_rows", [P, NB, 2 * F])
        in_rows = sb("in_rows", [P, NB, 2 * F])
        idx = sb("idx", [P, NB], I32)
        weights, w_init, step = sem("weights"), sem("w_init"), sem("step")
        rooted, rooted_bn, biased, ubias = sem("rooted"), sem("rooted_bn"), sem("biased"), sem("ubias")
        cat_made, turned, copied, mixed, bent, outs, added = (sem("cat_made"), sem("turned"), sem("copied"),
                                                            sem("mixed"), sem("bent"), sem("outs"),
                                                            sem("x_added"))
        staged2, turned2, copied2 = sem("staged2"), sem("turned2"), sem("copied2")
        normed, proj, split, stored, spread = (sem("normed"), sem("proj"), sem("split_rows"), sem("stored"),
                                               c.spread_in)
        ps_mix = [c.psQ[0:F, 2, 0:BN // 2], c.psQ[0:F, 3, 0:BN // 2]]
        ps_out = [c.psP[:, k, 0:NB * F] for k in range(2)]
        made = c.psP[:, :, :].rearrange("p b (j n) -> p (b j) n", j=2)
        block = ctx.enter_context(nc.Block())

        @block.sync
        def _(sp):
            sp.wait_ge(w_init, 4)
            for dst, m in ((b2_row[:, :], bcast(b2.unsqueeze(0), [P, F])), (w3[:, :], W3[0:2 * F, :]),
                           (w3u[:, :], W3[2 * F:3 * F, :]), (u0[:, :], u[0:1, :].rearrange("a f -> f a")),
                           (b3_col[:, :], b3.unsqueeze(1)), (w4[0:F, :], W4), (w4[F:F + 1, :], b4.unsqueeze(0)),
                           (gam[:, :], gamma.unsqueeze(1)), (bet[:, :], beta.unsqueeze(1)),
                           (w[0:F, 0:2 * F], W1[F:2 * F, :]), (w[0:F, 2 * F:4 * F], W1[0:F, :]),
                           (w[F:F + 1, 2 * F:4 * F], b1.unsqueeze(0))):
                sp.dma_start(dst, m).then_inc(weights, 16)
            with sp.Fori(0, NBLK) as i:
                sp.wait_ge(split, i * 3 + 3)
                sp.dma_start(node_rows(c.table, i), out_rows[:, :, :]).then_inc(stored, 16)
            sp.wait_ge(stored, 16 * NBLK)

        @block.gpsimd
        def _(g):
            for k in range(2):
                g.memset(hidden[k][F:F + 1, :], 1.0).then_inc(w_init, 1)
            g.memset(xn[F:F + 1, :], 1.0).then_inc(w_init, 1)
            gather_ends(g, c)
            with g.Fori(0, NBLK) as i:
                rows_in = g.to_reg(i * 3 + 3)
                g.wait_ge(w_init, 4)
                g.wait_ge(split, rows_in)
                for t in range(NB):
                    g.indirect_dma_start(c.spread[:, :], bass.IndirectOffsetOnAxis(ap=idx[:, t:t + 1], axis=0),
                                         in_rows[:, t, :], None).then_inc(spread, 16)
            g.wait_ge(spread, 16 * NT)

        @block.vector
        def _(v):
            v.sem_inc(added, LEAD)
            v.memset(w[F:F + 1, 0:2 * F], 0.0).then_inc(w_init, 1)
            v.wait_ge(weights, 16 * 12)
            v.tensor_tensor(w[0:F, 2 * F:4 * F], w[0:F, 2 * F:4 * F], w[0:F, 0:2 * F], ALU.subtract)\
                .then_inc(step, 1)
            v.tensor_tensor(s["sq"][:, :, :], bcast(b2_row[:, :].unsqueeze(1), [P, NT, F]),
                            bcast(c.has_in[:, :].unsqueeze(2), [P, NT, F]), ALU.mult).then_inc(step, 1)
            v.wait_ge(step, 2)
            for j in range(NBLK + 1):
                if j < NBLK:
                    tiles, k = slice(j * NB, (j + 1) * NB), j % 2
                    v.wait_ge(c.gathered[j], 16 * NB)
                    v.wait_ge(turned, LEAD + j - 1)
                    v.tensor_copy(cat[k][:, :, 0:F], c.h[:, tiles, :]).then_inc(cat_made, 1)
                    v.tensor_tensor(cat[k][:, :, F:2 * F], c.ends[:, tiles, :],
                                    bcast(c.cnt_inv[:, tiles].unsqueeze(2), [P, NB, F]), ALU.mult)\
                        .then_inc(cat_made, 1)
                    v.wait_ge(cat_made, 3 * j + 2)
                    v.tensor_tensor(cat[k][:, :, F:2 * F], cat[k][:, :, F:2 * F], s["sq"][:, tiles, :],
                                    ALU.add).then_inc(cat_made, 1)
                if j > 0:
                    tiles = slice((j - 1) * NB, j * NB)
                    v.wait_ge(outs, LEAD + j)
                    v.tensor_tensor(c.x[:, tiles, :], c.x[:, tiles, :],
                                    ps_out[(j - 1) % 2].rearrange("p (t f) -> p t f", t=NB), ALU.add)\
                        .then_inc(added, 1)
            v.wait_ge(added, NBLK + LEAD)
            layernorm_relu(v, c, s, step, 2, rooted)
            v.wait_ge(copied2, NBLK)
            for j in range(NSC):
                batch_stats(v, bn, turned_all, j, step)
            batch_scale(v, bn, gam, bet, step, 2 + LN_STEPS, rooted_bn)
            with v.Fori(0, NBLK) as i:
                v.wait_ge(proj, i + 1)
                v.wait_ge(stored, i * 16)
                v.wait_ge(spread, i * (16 * NB))
                v.tensor_copy(idx[:, :], c.start_idx[:, bass.ds(i * NB, NB)]).then_inc(split, 1)
                v.tensor_copy(out_rows[:, :, :], made[:, 0:NB, 0:2 * F]).then_inc(split, 1)
                v.tensor_copy(in_rows[:, :, :], made[:, 0:NB, 2 * F:4 * F]).then_inc(split, 1)

        @block.scalar
        def _(a):
            for sm in (copied, bent):
                a.sem_inc(sm, LEAD)
            a.wait_ge(ubias, 1)
            a.activation(bias3[:, :], c.psP[0:F, 3, 0:1], ACT.Identity, bias=b3_col[:, 0:1]).then_inc(biased, 1)
            a.wait_ge(biased, 1)

            def to_hidden(i, k):
                n = i + 1 + LEAD
                a.wait_ge(turned, n)
                a.wait_ge(mixed, n - 2)
                copy_turned(a, c, turned_sb[k], 2 * F).then_inc(copied, 1)
                a.wait_ge(mixed, n)
                a.wait_ge(outs, n - 2)
                a.activation(hidden[k][0:F, 0:BN // 2], ps_mix[0], ACT.Relu, bias=bias3[:, 0:1])
                a.activation(hidden[k][0:F, BN // 2:BN], ps_mix[1], ACT.Relu, bias=bias3[:, 0:1])\
                    .then_inc(bent, 1)

            in_pairs(a, to_hidden)
            a.wait_ge(step, 2 + 6)
            a.activation(s["root"][:, :], s["var"][:, :], ACT.Sqrt).then_inc(rooted, 1)
            a.wait_ge(step, 2 + LN_STEPS)
            with a.Fori(0, NBLK) as i:
                a.wait_ge(turned2, i)
                a.copy(h_rows[:, :, :], c.h[:, bass.ds(i * NB, NB), :]).then_inc(staged2, 1)
                a.wait_ge(turned2, i + 1)
                a.copy(turned_all[:, bass.ds(i * BN, 4 * P)], c.psQ[0:F, 0, :])
                a.copy(turned_all[:, bass.ds(i * BN + 4 * P, 3 * P)], c.psQ[0:F, 1, 0:3 * P])\
                    .then_inc(copied2, 1)
            a.wait_ge(step, 2 + LN_STEPS + NSC + 2)
            a.activation(bn["root"][:, :], bn["var"][:, :], ACT.Sqrt).then_inc(rooted_bn, 1)
            a.wait_ge(step, 2 + LN_STEPS + BATCH_STEPS)
            a.wait_ge(copied2, NBLK)
            with a.Fori(0, NBLK) as i:
                a.wait_ge(proj, i)
                a.activation(xn[0:F, :], turned_all[:, bass.ds(i * BN, BN)], ACT.Identity,
                             bias=bn["shift"][:, 0:1], scale=bn["scale"][:, 0:1]).then_inc(normed, 1)

        @block.tensor
        def _(pe):
            pe.wait_ge(weights, 16 * 12)
            pe.matmul(c.psP[0:F, 3, 0:1], w3u[:, :], u0[:, :], start=True, stop=True).then_inc(ubias, 1)
            pe.wait_ge(w_init, 4)
            for sm in (turned, mixed, outs):
                pe.sem_inc(sm, LEAD)

            def mean_products(i, k):
                now, one_back, two_back = (pe.to_reg(i + 1 + LEAD), pe.to_reg(i + LEAD),
                                           pe.to_reg(i - 1 + LEAD))
                cat_in = pe.to_reg(i * 3 + 3)
                pe.wait_ge(w_init, 4)
                pe.wait_ge(cat_made, cat_in)
                pe.wait_ge(copied, one_back)
                turn_block(pe, c, cat[k], 2 * F).then_inc(turned, 1)
                pe.wait_ge(w_init, 4)
                pe.wait_ge(copied, now)
                pe.wait_ge(bent, one_back)
                for j in range(2):
                    mm = pe.matmul(ps_mix[j], w3[:, :], turned_sb[k][:, j * BN // 2:(j + 1) * BN // 2],
                                   start=True, stop=True)
                mm.then_inc(mixed, 1)
                pe.wait_ge(w_init, 4)
                pe.wait_ge(bent, now)
                pe.wait_ge(added, two_back)
                for t in range(NB):
                    mm = pe.matmul(ps_out[k][:, t * F:(t + 1) * F], hidden[k][:, t * P:(t + 1) * P], w4[:, :],
                                   start=True, stop=True)
                mm.then_inc(outs, 1)

            in_pairs(pe, mean_products)
            with pe.Fori(0, NBLK) as i:
                rows_in, ps_free = pe.to_reg(i + 1), pe.to_reg(i)
                pe.wait_ge(w_init, 4)
                pe.wait_ge(staged2, rows_in)
                pe.wait_ge(copied2, ps_free)
                turn_block(pe, c, h_rows).then_inc(turned2, 1)
            pe.wait_ge(step, 1)
            with pe.Fori(0, NBLK) as i:
                xn_in, ps_free = pe.to_reg(i + 1), pe.to_reg(i * 3)
                pe.wait_ge(w_init, 4)
                pe.wait_ge(normed, xn_in)
                pe.wait_ge(split, ps_free)
                for t in range(NB):
                    mm = pe.matmul(made[:, t, :], xn[:, t * P:(t + 1) * P], w[:, :], start=True, stop=True)
                mm.then_inc(proj, 1)
    clear(c, sems)


def edges2(c, W2, b2):
    nc = c.nc
    ctx, sb, sem, sems = stage(nc, "edges2")
    with ctx:
        idx = [sb(f"idx{k}", [P, ST], I32) for k in range(2)]
        flg = [sb(f"flg{u}", [P, GE], BF16) for u in range(UN)]
        drow = [sb(f"drow{u}", [P, GT, 2 * F]) for u in range(UN)]
        rows = [sb(f"rows{u}", [P, GT, 2 * F]) for u in range(UN)]
        carried = [sb(f"carried{r}", [P, GE]) for r in range(2)]
        pre = [sb(f"pre{r}", [P, GE]) for r in range(2)]
        act = [sb(f"act{r}", [P, GE]) for r in range(2)]
        msg = [sb(f"msg{r}", [F, GE]) for r in range(2)]
        scn = [sb(f"scn{r}", [F, GE]) for r in range(2)]
        outr = [sb(f"outr{k}", [P, ST, F]) for k in range(2)]
        w2 = sb("w2", [2 * F, F])
        b2_col = sb("b2_col", [F, 1])
        weights, first = sem("weights"), sem("first")
        loaded = [sem(f"loaded{u}") for u in range(UN)]
        picked = sem("picked")
        gathered = c.gathered
        stored = [sem(f"stored{k}") for k in range(2)]
        d_turned, d_scanned, s_turned, summed, bent = (sem("d_turned"), sem("d_scanned"), sem("s_turned"),
                                                       sem("summed"), sem("bent"))
        mixed, biased, scanned, back, copied = (sem("mixed"), sem("biased"), sem("scanned"), sem("back"),
                                                sem("copied"))
        ps_d = [c.psP[:, 0, :], c.psP[:, 1, :]]
        ps_s = [c.psP[:, 2, :], c.psP[:, 3, :]]
        ps_m = [c.psQ[0:F, 0, :], c.psQ[0:F, 1, :]]
        ps_b = [c.psQ[:, 2, 0:GT * F], c.psQ[:, 3, 0:GT * F]]
        block = ctx.enter_context(nc.Block())

        @block.sync
        def _(sp):
            sp.dma_start(w2[:, :], W2).then_inc(weights, 16)
            sp.dma_start(b2_col[:, :], b2.unsqueeze(1)).then_inc(weights, 16)
            with sp.Fori(0, ITERS) as i:
                for u in range(UN):
                    sp.wait_ge(scanned, i * 8 + u + 1 - 8 + LEAD)
                    group = i * 8 + u
                    sp.dma_start(flg[u][:, :], bcast(c.flags[bass.ds(group, 1), :], [P, GE]))\
                        .then_inc(loaded[u], 16)
                    sp.dma_start(drow[u][:, :, :], c.spread[bass.ds(group * GE, GE), :]
                                 .rearrange("(t p) f -> p t f", p=P)).then_inc(loaded[u], 16)

        @block.gpsimd
        def _(g):
            with g.Fori(0, ITERS) as i:
                for u in range(UN):
                    k = u // SG
                    super_in, slot_free = g.to_reg(i * 2 + k + 1), g.to_reg(i * 8 + u + 1 - 8 + LEAD)
                    g.wait_ge(weights, 32)
                    g.wait_ge(picked, super_in)
                    g.wait_ge(s_turned, slot_free)
                    for t in range(GT):
                        col = (u % SG) * GT + t
                        g.indirect_dma_start(rows[u][:, t, :], None, c.table[:, :],
                                             bass.IndirectOffsetOnAxis(ap=idx[k][:, col:col + 1], axis=0))\
                            .then_inc(gathered[u], 16)

        @block.vector
        def _(v):
            for sm in (d_scanned, summed, scanned):
                v.sem_inc(sm, LEAD)
            v.memset(carried[1][:, :], 0.0).then_inc(first, 1)
            v.memset(scn[1][:, :], 0.0).then_inc(first, 1)
            v.wait_ge(first, 2)
            for k in range(2):
                pick(v, c, idx[k], slice(k * ST, (k + 1) * ST), picked)
            with v.Fori(0, ITERS) as i:
                def before_relu(u):
                    k, r, n = u // SG, u % 2, i * 8 + u + 1 + LEAD
                    v.wait_ge(loaded[u], i * 32 + 32)
                    v.wait_ge(d_turned, n)
                    v.wait_ge(d_scanned, n - 1)
                    v.tensor_tensor_scan(carried[r][:, :], flg[u][:, :],
                                         ps_d[r], carried[1 - r][:, GE - 1:GE], ALU.mult, ALU.add)\
                        .then_inc(d_scanned, 1)
                    v.wait_ge(s_turned, n)
                    v.wait_ge(d_scanned, n)
                    v.wait_ge(bent, n - 2)
                    v.tensor_tensor(pre[r][:, :], ps_s[r], carried[r][:, :], ALU.add).then_inc(summed, 1)

                def running_max(u):
                    k, r, n = u // SG, u % 2, i * 8 + u + 1 + LEAD
                    v.wait_ge(biased, n)
                    v.wait_ge(back, n - 2)
                    v.wait_ge(scanned, n - 1)
                    v.tensor_tensor_scan(scn[r][:, :], flg[u][0:F, :],
                                         msg[r][:, :], scn[1 - r][:, GE - 1:GE], ALU.mult, ALU.max)\
                        .then_inc(scanned, 1)
                    if u % SG == SG - 1:
                        v.wait_ge(gathered[u], i * 64 + 64)
                        pick(v, c, idx[k], bass.ds((i * 2 + k + 2) * ST, ST), picked)

                before_relu(0)
                for u in range(UN):
                    if u + 1 < UN:
                        before_relu(u + 1)
                    running_max(u)

        @block.tensor
        def _(pe):
            for sm in (d_turned, s_turned, mixed, back):
                pe.sem_inc(sm, LEAD)
            pe.wait_ge(weights, 32)
            with pe.Fori(0, ITERS) as i:
                def turn_in(u):
                    k, r, n = u // SG, u % 2, i * 8 + u + 1 + LEAD
                    pe.wait_ge(loaded[u], i * 32 + 32)
                    pe.wait_ge(d_scanned, n - 2)
                    for t in range(GT):
                        mm = pe.transpose(ps_d[r][:, t * P:(t + 1) * P], drow[u][:, t, :],
                                          c.ident[:, :])
                    mm.then_inc(d_turned, 1)
                    pe.wait_ge(gathered[u], i * 64 + 64)
                    pe.wait_ge(summed, n - 2)
                    for t in range(GT):
                        mm = pe.transpose(ps_s[r][:, t * P:(t + 1) * P], rows[u][:, t, :], c.ident[:, :])
                    mm.then_inc(s_turned, 1)

                def turn_out(u):
                    r, n = u % 2, i * 8 + u + 1 + LEAD
                    scan_in, ps_free = pe.to_reg(n), pe.to_reg(n - 2)
                    pe.wait_ge(weights, 32)
                    pe.wait_ge(scanned, scan_in)
                    pe.wait_ge(copied, ps_free)
                    for t in range(GT):
                        mm = pe.transpose(ps_b[r][:, t * F:(t + 1) * F], scn[r][:, t * P:(t + 1) * P],
                                          c.ident[0:F, 0:F])
                    mm.then_inc(back, 1)

                turn_in(0)
                for u in range(UN):
                    r, n = u % 2, i * 8 + u + 1 + LEAD
                    if u + 1 < UN:
                        turn_in(u + 1)
                    pe.wait_ge(bent, n)
                    pe.wait_ge(biased, n - 2)
                    pe.matmul(ps_m[r], w2[:, :], act[r][:, :], start=True, stop=True).then_inc(mixed, 1)
                    if u > 0:
                        turn_out(u - 1)
                turn_out(UN - 1)

        @block.scalar
        def _(a):
            for sm in (bent, biased, copied):
                a.sem_inc(sm, LEAD)
            a.wait_ge(weights, 32)
            with a.Fori(0, ITERS) as i:
                def evacuate(u):
                    k, r, n = u // SG, u % 2, i * 8 + u + 1 + LEAD
                    if u % SG == 0:
                        a.wait_ge(stored[k], i * 16)
                    a.wait_ge(back, n)
                    a.copy(outr[k][:, (u % SG) * GT:(u % SG + 1) * GT, :].rearrange("p t f -> p (t f)"),
                           ps_b[r]).then_inc(copied, 1)
                    if u % SG == SG - 1:
                        a.wait_ge(copied, n)
                        a.dma_start(c.scans[bass.ds((i * 2 + k) * SE, SE), :]
                                    .rearrange("(t p) f -> p t f", p=P), outr[k][:, :, :])\
                            .then_inc(stored[k], 16)

                for u in range(UN):
                    r, n = u % 2, i * 8 + u + 1 + LEAD
                    a.wait_ge(summed, n)
                    a.wait_ge(mixed, n - 2)
                    a.activation(act[r][:, :], pre[r][:, :], ACT.Relu).then_inc(bent, 1)
                    a.wait_ge(mixed, n)
                    a.wait_ge(scanned, n - 2)
                    a.activation(msg[r][:, :], ps_m[r], ACT.Identity, bias=b2_col[:, 0:1])\
                        .then_inc(biased, 1)
                    if u > 0:
                        evacuate(u - 1)
                evacuate(UN - 1)
            for k in range(2):
                a.wait_ge(stored[k], 16 * ITERS)
    clear(c, sems)


def nodes3(c):
    nc = c.nc
    ctx, sb, sem, sems = stage(nc, "nodes3")
    with ctx:
        s = layernorm_buffers(sb)
        step, rooted, stored = sem("step"), sem("rooted"), sem("stored")
        block = ctx.enter_context(nc.Block())

        @block.gpsimd
        def _(g):
            gather_ends(g, c)

        @block.vector
        def _(v):
            for b in range(NBLK):
                v.wait_ge(c.gathered[b], 16 * NB)
            v.tensor_tensor(c.x[:, :, :], c.x[:, :, :], c.ends[:, :, :], ALU.add).then_inc(step, 1)
            layernorm_relu(v, c, s, step, 1, rooted)

        @block.scalar
        def _(a):
            a.wait_ge(step, 1 + 6)
            a.activation(s["root"][:, :], s["var"][:, :], ACT.Sqrt).then_inc(rooted, 1)

        @block.sync
        def _(sp):
            sp.wait_ge(step, 1 + LN_STEPS)
            sp.dma_start(c.table3.rearrange("(t p) f -> p t f", p=P), c.h[:, :, :]).then_inc(stored, 16)
            sp.wait_ge(stored, 16)
    clear(c, sems)


def edges3(c):
    nc = c.nc
    ctx, sb, sem, sems = stage(nc, "edges3")
    with ctx:
        idx = [sb(f"idx{k}", [P, ST], I32) for k in range(2)]
        flg = [sb(f"flg{k}", [F, SE], BF16) for k in range(2)]
        rows = [sb(f"rows{u}", [P, GT, F]) for u in range(UN)]
        scaled_rows = [sb(f"scaled_rows{r}", [P, GT, F]) for r in range(2)]
        scn = [sb(f"scn{r}", [F, GE]) for r in range(2)]
        outr = [sb(f"outr{k}", [P, ST, F]) for k in range(2)]
        loaded = [sem(f"loaded{k}") for k in range(2)]
        picked = sem("picked")
        gathered = c.gathered
        stored = [sem(f"stored{k}") for k in range(2)]
        first, scaled, turned, scanned, back, copied = (sem("first"), sem("scaled"), sem("turned"),
                                                        sem("scanned"), sem("back"), sem("copied"))
        ps_t = [c.psP[0:F, 0, :], c.psP[0:F, 1, :]]
        ps_b = [c.psQ[:, 0, 0:GT * F], c.psQ[:, 1, 0:GT * F]]
        block = ctx.enter_context(nc.Block())

        @block.sync
        def _(sp):
            with sp.Fori(0, ITERS) as i:
                for k in range(2):
                    s = i * 2 + k
                    sp.wait_ge(scanned, i * 8 + 4 * k - 4 + LEAD)
                    sp.dma_start(flg[k][:, :], bcast(super_flags(c, s), [F, SE]))\
                        .then_inc(loaded[k], 16)

        @block.gpsimd
        def _(g):
            with g.Fori(0, ITERS) as i:
                for u in range(UN):
                    k = u // SG
                    super_in, slot_free = g.to_reg(i * 2 + k + 1), g.to_reg(i * 8 + u + 1 - 8 + LEAD)
                    g.wait_ge(first, 1)
                    g.wait_ge(picked, super_in)
                    g.wait_ge(scaled, slot_free)
                    for t in range(GT):
                        col = (u % SG) * GT + t
                        g.indirect_dma_start(rows[u][:, t, :], None, c.table3[:, :],
                                             bass.IndirectOffsetOnAxis(ap=idx[k][:, col:col + 1], axis=0))\
                            .then_inc(gathered[u], 16)

        @block.vector
        def _(v):
            v.sem_inc(scaled, LEAD)
            v.sem_inc(scanned, LEAD)
            v.memset(scn[1][:, :], 0.0).then_inc(first, 1)
            v.wait_ge(first, 1)
            for k in range(2):
                pick(v, c, idx[k], slice(k * ST, (k + 1) * ST), picked)
            with v.Fori(0, ITERS) as i:
                for u in range(UN):
                    k, r, n = u // SG, u % 2, i * 8 + u + 1 + LEAD
                    v.wait_ge(loaded[k], i * 16 + 16)
                    v.wait_ge(gathered[u], i * 64 + 64)
                    v.wait_ge(turned, n - 2)
                    v.tensor_tensor(scaled_rows[r][:, :, :], rows[u][:, :, :],
                                    bcast(c.ew1[:, bass.ds((i * 8 + u) * GT, GT)].unsqueeze(2),
                                          [P, GT, F]), ALU.mult).then_inc(scaled, 1)
                    v.wait_ge(turned, n)
                    v.wait_ge(back, n - 2)
                    v.wait_ge(scanned, n - 1)
                    v.tensor_tensor_scan(scn[r][:, :], flg[k][:, (u % SG) * GE:(u % SG + 1) * GE],
                                         ps_t[r], scn[1 - r][:, GE - 1:GE], ALU.mult, ALU.add)\
                        .then_inc(scanned, 1)
                    if u % SG == SG - 1:
                        v.wait_ge(gathered[u], i * 64 + 64)
                        pick(v, c, idx[k], bass.ds((i * 2 + k + 2) * ST, ST), picked)

        @block.tensor
        def _(pe):
            pe.sem_inc(turned, LEAD)
            pe.sem_inc(back, LEAD)
            with pe.Fori(0, ITERS) as i:
                for u in range(UN):
                    r, n = u % 2, i * 8 + u + 1 + LEAD
                    now, ps_free = pe.to_reg(n), pe.to_reg(n - 2)
                    pe.wait_ge(first, 1)
                    pe.wait_ge(scaled, now)
                    pe.wait_ge(scanned, ps_free)
                    for t in range(GT):
                        mm = pe.transpose(ps_t[r][:, t * P:(t + 1) * P], scaled_rows[r][:, t, :], c.ident[:, :])
                    mm.then_inc(turned, 1)
                    pe.wait_ge(first, 1)
                    pe.wait_ge(scanned, now)
                    pe.wait_ge(copied, ps_free)
                    for t in range(GT):
                        mm = pe.transpose(ps_b[r][:, t * F:(t + 1) * F], scn[r][:, t * P:(t + 1) * P],
                                          c.ident[0:F, 0:F])
                    mm.then_inc(back, 1)

        @block.scalar
        def _(a):
            a.sem_inc(copied, LEAD)
            with a.Fori(0, ITERS) as i:
                for u in range(UN):
                    k, r, n = u // SG, u % 2, i * 8 + u + 1 + LEAD
                    if u % SG == 0:
                        a.wait_ge(stored[k], i * 16)
                    a.wait_ge(back, n)
                    a.copy(outr[k][:, (u % SG) * GT:(u % SG + 1) * GT, :].rearrange("p t f -> p (t f)"),
                           ps_b[r]).then_inc(copied, 1)
                    if u % SG == SG - 1:
                        a.wait_ge(copied, n)
                        a.dma_start(c.scans[bass.ds((i * 2 + k) * SE, SE), :]
                                    .rearrange("(t p) f -> p t f", p=P), outr[k][:, :, :])\
                            .then_inc(stored[k], 16)
            for k in range(2):
                a.wait_ge(stored[k], 16 * ITERS)
    clear(c, sems)


def layer_nodes(c, layer, W1, b1, gamma, beta, W2, b2):
    nc = c.nc
    ctx, sb, sem, sems = stage(nc, "layer_nodes")
    with ctx:
        bn = batch_buffers(sb)
        w1 = sb("w1", [F, F])
        b1_col = sb("b1_col", [F, 1])
        w2 = sb("w2", [F + 1, F])
        gam = sb("gam", [F, 1])
        bet = sb("bet", [F, 1])
        rows = [sb(f"rows{k}", [P, NB, F]) for k in range(2)]
        turned_sb = [sb(f"turned_sb{k}", [F, BN]) for k in range(2)]
        mid = sb("mid", [F, NP])
        hidden = [sb(f"hidden{k}", [F + 1, BN]) for k in range(2)]
        weights, one, step, rooted = sem("weights"), sem("one"), sem("step"), sem("rooted")
        added, turned, copied, mixed, biased = (sem("h_added"), sem("turned"), sem("copied"), sem("mixed"),
                                                sem("biased"))
        bent, outs, h_new, stored = sem("bent"), sem("outs"), sem("h_new"), sem("stored")
        ps_turn = [c.psQ[:, 0:2, :], c.psP[:, 0:2, :]]
        ps_mix = [[c.psQ[0:F, 2, 0:SC], c.psQ[0:F, 3, 0:SC]], [c.psP[0:F, 2, 0:SC], c.psP[0:F, 3, 0:SC]]]
        ps_out = [c.psQ[:, 0, 0:NB * F], c.psP[:, 0, 0:NB * F]]
        block = ctx.enter_context(nc.Block())

        @block.sync
        def _(sp):
            for dst, m in ((w1[:, :], W1[bass.ds(layer, 1)].rearrange("a k n -> (a k) n")),
                           (b1_col[:, :], b1[bass.ds(layer, 1)].rearrange("a n -> n a")),
                           (w2[0:F, :], W2[bass.ds(layer, 1)].rearrange("a k n -> (a k) n")),
                           (w2[F:F + 1, :], b2[bass.ds(layer, 1)]),
                           (gam[:, :], gamma[bass.ds(layer, 1)].rearrange("a n -> n a")),
                           (bet[:, :], beta[bass.ds(layer, 1)].rearrange("a n -> n a"))):
                sp.dma_start(dst, m).then_inc(weights, 16)
            for j in range(NBLK):
                sp.wait_ge(h_new, LEAD + j + 1)
                sp.dma_start(c.table3[j * BN:(j + 1) * BN, :].rearrange("(t p) f -> p t f", p=P),
                             c.h[:, j * NB:(j + 1) * NB, :]).then_inc(stored, 16)
            sp.wait_ge(stored, 16 * NBLK)

        @block.gpsimd
        def _(g):
            for k in range(2):
                g.memset(hidden[k][F:F + 1, :], 1.0).then_inc(one, 1)
            gather_ends(g, c)

        @block.vector
        def _(v):
            v.sem_inc(added, LEAD)
            v.sem_inc(h_new, LEAD)
            for j in range(NBLK + 1):
                if j < NBLK:
                    v.wait_ge(c.gathered[j], 16 * NB)
                    v.wait_ge(turned, LEAD + j - 1)
                    v.tensor_tensor(rows[j % 2][:, :, :], c.h[:, j * NB:(j + 1) * NB, :],
                                    c.ends[:, j * NB:(j + 1) * NB, :], ALU.add).then_inc(added, 1)
                if j > 0:
                    v.wait_ge(biased, LEAD + j)
                    for n in range(2 * j - 2, 2 * j):
                        batch_stats(v, bn, mid, n, step)
            v.wait_ge(weights, 16 * 6)
            batch_scale(v, bn, gam, bet, step, 0, rooted)

            def last_relu(i, k):
                v.wait_ge(outs, i + 1 + LEAD)
                v.tensor_scalar(c.h[:, bass.ds(i * NB, NB), :], ps_out[k].rearrange("p (t f) -> p t f", t=NB),
                                0.0, None, ALU.max).then_inc(h_new, 1)

            in_pairs(v, last_relu)

        @block.scalar
        def _(a):
            for sm in (copied, biased, bent):
                a.sem_inc(sm, LEAD)
            a.wait_ge(weights, 16 * 6)

            def after_products(i, k):
                n = i + 1 + LEAD
                a.wait_ge(turned, n)
                a.wait_ge(mixed, n - 2)
                copy_turned(a, c, turned_sb[k], ps=ps_turn[k]).then_inc(copied, 1)
                a.wait_ge(mixed, n)
                for j in range(2):
                    act = a.activation(mid[:, bass.ds(i * BN + j * SC, SC)], ps_mix[k][j], ACT.Identity,
                                       bias=b1_col[:, 0:1])
                act.then_inc(biased, 1)

            def normed_relu(i, k):
                a.wait_ge(outs, i - 1 + LEAD)
                a.activation(hidden[k][0:F, :], mid[:, bass.ds(i * BN, BN)], ACT.Relu,
                             bias=bn["shift"][:, 0:1], scale=bn["scale"][:, 0:1]).then_inc(bent, 1)

            in_pairs(a, after_products)
            a.wait_ge(step, NSC + 2)
            a.activation(bn["root"][:, :], bn["var"][:, :], ACT.Sqrt).then_inc(rooted, 1)
            a.wait_ge(step, BATCH_STEPS)
            a.wait_ge(biased, NBLK + LEAD)
            in_pairs(a, normed_relu)

        @block.tensor
        def _(pe):
            for sm in (turned, mixed, outs):
                pe.sem_inc(sm, LEAD)
            pe.wait_ge(weights, 16 * 6)
            pe.wait_ge(one, 2)

            def turn_and_mix(i, k):
                now, before = pe.to_reg(i + 1 + LEAD), pe.to_reg(i - 1 + LEAD)
                pe.wait_ge(one, 2)
                pe.wait_ge(added, now)
                pe.wait_ge(copied, before)
                turn_block(pe, c, rows[k], ps=ps_turn[k]).then_inc(turned, 1)
                pe.wait_ge(one, 2)
                pe.wait_ge(copied, now)
                pe.wait_ge(biased, before)
                for j in range(2):
                    mm = pe.matmul(ps_mix[k][j], w1[:, :], turned_sb[k][:, j * SC:(j + 1) * SC],
                                   start=True, stop=True)
                mm.then_inc(mixed, 1)

            def second(i, k):
                now, before = pe.to_reg(i + 1 + LEAD), pe.to_reg(i - 1 + LEAD)
                pe.wait_ge(one, 2)
                pe.wait_ge(bent, now)
                pe.wait_ge(h_new, before)
                for t in range(NB):
                    mm = pe.matmul(ps_out[k][:, t * F:(t + 1) * F], hidden[k][:, t * P:(t + 1) * P], w2[:, :],
                                   start=True, stop=True)
                mm.then_inc(outs, 1)

            in_pairs(pe, turn_and_mix)
            in_pairs(pe, second)
    clear(c, sems)


def finish(c, out):
    nc = c.nc
    full = NODES // P
    rest = NODES - full * P
    with ExitStack() as ctx:
        summed = ctx.enter_context(nc.semaphore("summed_out"))
        stored = ctx.enter_context(nc.semaphore("stored_out"))
        block = ctx.enter_context(nc.Block())

        @block.vector
        def _(v):
            v.tensor_tensor(c.x[:, :, :], c.x[:, :, :], c.h[:, :, :], ALU.add).then_inc(summed, 1)

        @block.sync
        def _(sp):
            sp.wait_ge(summed, 1)
            sp.dma_start(out[0:full * P, :].rearrange("(t p) f -> p t f", p=P), c.x[:, 0:full, :])\
                .then_inc(stored, 16)
            sp.dma_start(out[full * P:NODES, :], c.x[0:rest, full, :]).then_inc(stored, 16)
            sp.wait_ge(stored, 32)


def build(nc, ins, out):
    with ExitStack() as ctx:
        c = Core(nc, ctx)
        w0, w1, w2, w3 = ({k[7:]: v for k, v in ins.items() if k.startswith(f"L{n}_gnn_")} for n in range(4))
        prepare(c, ins["x"], ins["src_cols"], ins["dst_cols"], ins["ew_cols"], ins["ew1_cols"],
                ins["dst_seq"], ins["dst_prev"], ins["src_rows"], ins["attr_g"])
        falls = nc.values_load(c.unsorted[0:1, 0:1], min_val=0, max_val=EP,
                               skip_runtime_bounds_check_because="a count of edges")
        with nc.If(falls > 0):
            sort_edges(c, ins["dst_cols"], ins["dst_seq"], ins["attr_rows"])
            lay_out_sorted(c)
        nc.end_all_ifs()
        nodes0(c, w0["W_l1"], w0["b_l1"], w0["W_s2d"], w0["b_s2d"], w0["W_d2s"], w0["b_d2s"])
        edges0(c, w0["W_l2"], w0["b_l2"])
        nodes1(c, w0["W_g1"], w0["b_g1"], w0["W_g2"], w0["b_g2"], w1["W1"], w1["b1"])
        edges1(c, w1["W1"], w1["W2"])
        nodes2(c, w1["u"], w1["b2"], w1["W3"], w1["b3"], w1["W4"], w1["b4"], w2["gamma"], w2["beta"],
               w2["W1"], w2["b1"])
        edges2(c, w2["W2"], w2["b2"])
        nodes3(c)
        with nc.Fori(0, LAYERS) as layer:
            edges3(c)
            layer_nodes(c, layer, w3["W1"], w3["b1"], w3["gamma"], w3["beta"], w3["W2"], w3["b2"])
        finish(c, out)


def arrays(**inputs):
    import numpy as np

    a = {k: np.ascontiguousarray(v) for k, v in inputs.items()}

    def padded(v, fill):
        out = np.full((EP,) + v.shape[1:], fill, v.dtype)
        out[:EDGES] = v
        return out

    def cols(v):
        return np.ascontiguousarray(v.reshape(EC, P).T)

    src, dst = padded(a.pop("src"), 0), padded(a.pop("dst"), NODES)
    attr = padded(a.pop("edge_attr_32"), 0)
    x = np.zeros((NP, F), a["x"].dtype)
    x[:NODES] = a.pop("x")
    prev = np.full(EP, -1, dst.dtype)
    prev[1:] = dst[:-1]
    return dict(
        x=x, src_cols=cols(src), dst_cols=cols(dst), src_rows=src.reshape(SUPERS * SG, GE),
        dst_seq=dst.reshape(P, EC), dst_prev=prev.reshape(P, EC),
        ew_cols=cols(padded(a.pop("edge_weight"), 0)),
        ew1_cols=cols(padded(a.pop("edge_weight1")[:, 0], 0)),
        attr_rows=attr,
        attr_g=np.ascontiguousarray(attr.reshape(SUPERS, SG, GE, FE).transpose(0, 1, 3, 2))
        .reshape(SUPERS * P, GE), **a)


def kernel(**inputs):
    import concourse.bacc as _bacc
    from concourse.bass_utils import run_bass_kernel_spmd as _run

    nc = _bacc.Bacc("TRN2", target_bir_lowering=False, num_devices=1)
    laid_out = arrays(**inputs)
    ins = {k: nc.dram_tensor(f"in_{k}", v.shape, mybir.dt.from_np(v.dtype), kind="ExternalInput").ap()
           for k, v in laid_out.items()}
    out = nc.dram_tensor("out", (NODES, F), F32, kind="ExternalOutput").ap()
    build(nc, ins, out)
    r = _run(nc, [{f"in_{k}": v for k, v in laid_out.items()}], core_ids=[0])
    return r.results[0]["out"]
```
